# Optimizing a Trainium2 kernel written in Bass

```python
import numpy as np
import jax
import jax.numpy as jnp

def _softmax(x, axis=-1):
    return jax.nn.softmax(x, axis=axis)

def _gelu(x):
    return jax.nn.gelu(x, approximate=True)

def _silu(x):
    return jax.nn.silu(x)

def _sigmoid(x):
    return jax.nn.sigmoid(x)

def _layernorm(x, axis=-1, eps=1e-05):
    m = jnp.mean(x, axis=axis, keepdims=True)
    v = jnp.var(x, axis=axis, keepdims=True)
    return (x - m) / jnp.sqrt(v + eps)

def _scatter_add(tgt, idx, src, axis=0):
    return tgt.at[idx].add(src)

def _segment_sum(src, seg, n):
    return jax.ops.segment_sum(src, seg, n)
kernel_name = 'mk_cond_resid_d4_seqx_r8_f04993'

def setup_inputs(seed: int=0):
    np.random.seed(seed)
    _w = jnp.asarray

    def _rec_inputs():
        import jax
        import jax.numpy as jnp
        _rk = jax.random.key(seed)
        x = -0.0002928 + 1 * jax.random.normal(jax.random.fold_in(_rk, 1), (8, 256, 128), jnp.float32)
        _lenS = 256 - jax.random.randint(jax.random.fold_in(_rk, 7), (8,), 0, max(1, 256 // 4) + 1, jnp.int32)
        _lenS2 = 256 - jax.random.randint(jax.random.fold_in(_rk, 8), (8,), 0, max(1, 256 // 4) + 1, jnp.int32)
        cond_1024 = 0.0061147 + 1.02565 * jax.random.normal(jax.random.fold_in(_rk, 11), (8, 128), jnp.float32)
        _validS = jnp.arange(256)[None, :] < _lenS[:, None]
        _validS2 = jnp.arange(256)[None, :] < _lenS2[:, None]
        _causal = jnp.tril(jnp.ones((256, 256), dtype=bool))
        mask_Bx1x1xS_ff0 = jnp.where(jnp.ones((8, 1, 1, 256), dtype=bool), 0.0, -1000000000.0).astype(jnp.float32)
        return (x, cond_1024, mask_Bx1x1xS_ff0)
    x, cond_1024, mask_Bx1x1xS_ff0 = _rec_inputs()

    def _L0_cond_setup():
        import jax, jax.numpy as jnp
        import numpy as np
        D, HS, HE, E, K = (128, 256, 128, 8, 2)
        B, T = (4, 128)
        N_SHARED = 1
        key = jax.random.key(seed)
        ks = jax.random.split(key, 9)
        g = lambda k, shape, s: jax.random.normal(k, shape, jnp.float32) * s
        return {'x': g(ks[0], (B, T, D), 1.0), 't_emb': g(ks[1], (B, D), 1.0), 'router_W': g(ks[2], (2 * D, E), 0.01), 'router_bias': jnp.zeros((E,), jnp.float32), 'w1': g(ks[3], (D, HS), 0.02), 'w3': g(ks[4], (D, HS), 0.02), 'w2': g(ks[5], (HS, D), 0.02), 'W1e': g(ks[6], (E, D, HE), 0.02), 'W2e': g(ks[7], (E, HE, D), 0.02)}
    _L0_cond_all = _L0_cond_setup()
    _L0_cond_in = {k: v for k, v in _L0_cond_all.items() if k in ('router_W', 'router_bias', 'w1', 'w3', 'w2', 'W1e', 'W2e')}
    del _L0_cond_all

    def _L1_cond_setup():
        import jax, jax.numpy as jnp
        import numpy as np
        D_MODEL = 128
        D_FF = 512
        N_EXPERTS = 8
        TOP_K = 2
        N_SHARED = 2
        B, T = (4, 256)
        key = jax.random.key(seed)
        ks = jax.random.split(key, 9)
        Hs = D_FF // 2
        Hr = D_FF // 4
        inp = {'x': jax.random.normal(ks[0], (B, T, D_MODEL), dtype=jnp.float32), 't_emb': jax.random.normal(ks[1], (B, D_MODEL), dtype=jnp.float32), 'W_router': 0.01 * jax.random.normal(ks[2], (N_EXPERTS, 2 * D_MODEL), dtype=jnp.float32), 'router_bias': jnp.zeros((N_EXPERTS,), dtype=jnp.float32), 's_w1': 0.02 * jax.random.normal(ks[3], (N_SHARED, Hs, D_MODEL), dtype=jnp.float32), 's_w3': 0.02 * jax.random.normal(ks[4], (N_SHARED, Hs, D_MODEL), dtype=jnp.float32), 's_w2': 0.02 * jax.random.normal(ks[5], (N_SHARED, D_MODEL, Hs), dtype=jnp.float32), 'r_w1': 0.02 * jax.random.normal(ks[6], (N_EXPERTS, Hr, D_MODEL), dtype=jnp.float32), 'r_w2': 0.02 * jax.random.normal(ks[7], (N_EXPERTS, D_MODEL, Hr), dtype=jnp.float32)}
        return inp
    _L1_cond_all = _L1_cond_setup()
    _L1_cond_in = {k: v for k, v in _L1_cond_all.items() if k in ('W_router', 'router_bias', 's_w1', 's_w3', 's_w2', 'r_w1', 'r_w2')}
    del _L1_cond_all

    def _L2_cond_setup():
        import jax, jax.numpy as jnp
        import numpy as np
        LATENT = 128
        key = jax.random.key(seed)
        k1, k2, k3, k4 = jax.random.split(key, 4)
        B, T, D = (64, 64, LATENT)
        h_t = jax.random.normal(k1, (B, D), dtype=jnp.float32)
        z = jax.random.normal(k2, (B, T, D), dtype=jnp.float32)
        bound = 1.0 / np.sqrt(2 * D)
        W = jax.random.uniform(k3, (D, 2 * D), minval=-bound, maxval=bound, dtype=jnp.float32)
        b = jax.random.uniform(k4, (D,), minval=-bound, maxval=bound, dtype=jnp.float32)
        alpha = jnp.full((D,), 0.1, dtype=jnp.float32)
        return {'h_t': h_t, 'z': z, 'W': W, 'b': b, 'alpha': alpha}
    _L2_cond_all = _L2_cond_setup()
    _L2_cond_in = {k: v for k, v in _L2_cond_all.items() if k in ('W', 'b', 'alpha')}
    del _L2_cond_all

    def _L3_cond_setup():
        import jax, jax.numpy as jnp
        import numpy as np
        EMBED = 128
        HEADS = 16
        HDIM = EMBED // HEADS
        MASK_OUT = -10000.0

        def _split_heads(t):
            B, T, _ = t.shape
            return t.reshape(B, T, HEADS, HDIM).transpose(0, 2, 1, 3)
        key = jax.random.key(seed)
        ks = jax.random.split(key, 12)
        B, S = (4, 1023)
        scale = 0.02
        return {'word_hidden_states': jax.random.normal(ks[0], (B, S, EMBED), jnp.float32), 'image_hidden_states': jax.random.normal(ks[1], (B, EMBED), jnp.float32), 'attention_mask': jnp.zeros((B, 1, 1, S), jnp.float32), 'c_attn_w': jax.random.normal(ks[2], (EMBED, 3 * EMBED), jnp.float32) * scale, 'c_attn_b': jnp.zeros((3 * EMBED,), jnp.float32), 'c_proj_w': jax.random.normal(ks[3], (EMBED, EMBED), jnp.float32) * scale, 'c_proj_b': jnp.zeros((EMBED,), jnp.float32), 'uk_w': jax.random.normal(ks[4], (EMBED, EMBED), jnp.float32) * scale, 'uk_b': jnp.zeros((EMBED,), jnp.float32), 'uv_w': jax.random.normal(ks[5], (EMBED, EMBED), jnp.float32) * scale, 'uv_b': jnp.zeros((EMBED,), jnp.float32)}
    _L3_cond_all = _L3_cond_setup()
    _L3_cond_in = {k: v for k, v in _L3_cond_all.items() if k in ('c_attn_w', 'c_attn_b', 'c_proj_w', 'c_proj_b', 'uk_w', 'uk_b', 'uv_w', 'uv_b')}
    del _L3_cond_all
    return {'x': x, 'cond_1024': cond_1024, 'mask_Bx1x1xS_ff0': mask_Bx1x1xS_ff0, 'L0_cond_router_W': _L0_cond_in['router_W'], 'L0_cond_router_bias': _L0_cond_in['router_bias'], 'L0_cond_w1': _L0_cond_in['w1'], 'L0_cond_w3': _L0_cond_in['w3'], 'L0_cond_w2': _L0_cond_in['w2'], 'L0_cond_W1e': _L0_cond_in['W1e'], 'L0_cond_W2e': _L0_cond_in['W2e'], 'L1_cond_W_router': _L1_cond_in['W_router'], 'L1_cond_router_bias': _L1_cond_in['router_bias'], 'L1_cond_s_w1': _L1_cond_in['s_w1'], 'L1_cond_s_w3': _L1_cond_in['s_w3'], 'L1_cond_s_w2': _L1_cond_in['s_w2'], 'L1_cond_r_w1': _L1_cond_in['r_w1'], 'L1_cond_r_w2': _L1_cond_in['r_w2'], 'L2_cond_W': _L2_cond_in['W'], 'L2_cond_b': _L2_cond_in['b'], 'L2_cond_alpha': _L2_cond_in['alpha'], 'L3_cond_c_attn_w': _L3_cond_in['c_attn_w'], 'L3_cond_c_attn_b': _L3_cond_in['c_attn_b'], 'L3_cond_c_proj_w': _L3_cond_in['c_proj_w'], 'L3_cond_c_proj_b': _L3_cond_in['c_proj_b'], 'L3_cond_uk_w': _L3_cond_in['uk_w'], 'L3_cond_uk_b': _L3_cond_in['uk_b'], 'L3_cond_uv_w': _L3_cond_in['uv_w'], 'L3_cond_uv_b': _L3_cond_in['uv_b']}

def reference(x, cond_1024, mask_Bx1x1xS_ff0, L0_cond_router_W, L0_cond_router_bias, L0_cond_w1, L0_cond_w3, L0_cond_w2, L0_cond_W1e, L0_cond_W2e, L1_cond_W_router, L1_cond_router_bias, L1_cond_s_w1, L1_cond_s_w3, L1_cond_s_w2, L1_cond_r_w1, L1_cond_r_w2, L2_cond_W, L2_cond_b, L2_cond_alpha, L3_cond_c_attn_w, L3_cond_c_attn_b, L3_cond_c_proj_w, L3_cond_c_proj_b, L3_cond_uk_w, L3_cond_uk_b, L3_cond_uv_w, L3_cond_uv_b):
    import jax
    import jax.numpy as jnp

    def _L0_cond_ref(x, t_emb, router_W, router_bias, w1, w3, w2, W1e, W2e):
        import jax, jax.numpy as jnp
        import numpy as np
        D, HS, HE, E, K = (128, 256, 128, 8, 2)
        B, T = (4, 128)
        N_SHARED = 1
        Bb, Tt, C = x.shape
        xf = x.reshape(-1, C)
        tf = jnp.broadcast_to(t_emb[:, None, :], (Bb, Tt, C)).reshape(-1, C)
        N = xf.shape[0]
        shared = jax.nn.silu(xf @ w1) * (xf @ w3) @ w2
        s = jax.nn.sigmoid((jnp.concatenate([xf, tf], axis=-1) @ router_W).astype(jnp.float32))
        sel_scores = s + router_bias
        _, topk_idx = jax.lax.top_k(sel_scores, K)
        s_sel = jnp.take_along_axis(s, topk_idx, axis=1)
        denom = s_sel.sum(axis=1, keepdims=True)
        gates = jnp.where(denom > 1e-09, s_sel / (denom + 1e-09), 1.0 / K).astype(x.dtype)
        combine = jnp.zeros((N, E), x.dtype).at[jnp.arange(N)[:, None], topk_idx].add(gates)
        h = jax.nn.gelu(jnp.einsum('nc,ech->enh', xf, W1e), approximate=False)
        y = jnp.einsum('enh,ehc->enc', h, W2e)
        routed = jnp.einsum('ne,enc->nc', combine, y)
        return ((shared + routed) / (N_SHARED + K)).reshape(Bb, Tt, C)

    def _L1_cond_ref(x, t_emb, W_router, router_bias, s_w1, s_w3, s_w2, r_w1, r_w2):
        import jax, jax.numpy as jnp
        import numpy as np
        D_MODEL = 128
        D_FF = 512
        N_EXPERTS = 8
        TOP_K = 2
        N_SHARED = 2
        B, T = (4, 256)
        Bn, Tn, C = x.shape
        N = Bn * Tn
        x_flat = x.reshape(N, C)
        t_flat = jnp.broadcast_to(t_emb[:, None, :], (Bn, Tn, C)).reshape(N, C)
        shared_out = jnp.zeros_like(x_flat)
        for e in range(N_SHARED):
            h = jax.nn.silu(x_flat @ s_w1[e].T) * (x_flat @ s_w3[e].T)
            shared_out = shared_out + h @ s_w2[e].T
        shared_out = shared_out / N_SHARED
        router_in = jnp.concatenate([x_flat, t_flat], axis=-1)
        s = jax.nn.sigmoid((router_in @ W_router.T).astype(jnp.float32))
        sel_scores = s + router_bias
        _, topk_idx = jax.lax.top_k(sel_scores, TOP_K)
        s_sel = jnp.take_along_axis(s, topk_idx, axis=1)
        denom = jnp.sum(s_sel, axis=1, keepdims=True)
        gates = jnp.where(denom > 1e-09, s_sel / (denom + 1e-09), 1.0 / TOP_K).astype(x.dtype)
        gates_full = jnp.sum(jax.nn.one_hot(topk_idx, N_EXPERTS, dtype=x.dtype) * gates[..., None], axis=1)
        routed_out = jnp.zeros_like(x_flat)
        for e in range(N_EXPERTS):
            h = jax.nn.gelu(x_flat @ r_w1[e].T, approximate=False)
            routed_out = routed_out + h @ r_w2[e].T * gates_full[:, e:e + 1]
        out = (shared_out + routed_out) / (N_SHARED + TOP_K)
        return out.reshape(Bn, Tn, C)

    def _L2_cond_ref(h_t, z, W, b, alpha):
        import jax, jax.numpy as jnp
        import numpy as np
        LATENT = 128
        D = h_t.shape[-1]
        Wh = W[:, :D]
        Wz = W[:, D:]
        leak = 1.0 - alpha

        def step(h, z_t):
            gate = jax.nn.sigmoid(h @ Wh.T + z_t @ Wz.T + b)
            h_new = jnp.tanh(h * leak + gate * z_t)
            return (h_new, h_new)
        _, hs = jax.lax.scan(step, h_t, jnp.swapaxes(z, 0, 1))
        return jnp.swapaxes(hs, 0, 1)

    def _L3_cond_ref(word_hidden_states, image_hidden_states, attention_mask, c_attn_w, c_attn_b, c_proj_w, c_proj_b, uk_w, uk_b, uv_w, uv_b):
        import jax, jax.numpy as jnp
        import numpy as np
        EMBED = 128
        HEADS = 16
        HDIM = EMBED // HEADS
        MASK_OUT = -10000.0

        def _split_heads(t):
            B, T, _ = t.shape
            return t.reshape(B, T, HEADS, HDIM).transpose(0, 2, 1, 3)
        B, S, _ = word_hidden_states.shape
        qkv = word_hidden_states @ c_attn_w + c_attn_b
        q_word, k_word, v_word = jnp.split(qkv, 3, axis=-1)
        img = image_hidden_states[:, None, :]
        k_img = img @ uk_w.T + uk_b
        v_img = img @ uv_w.T + uv_b
        k = jnp.concatenate([k_img, k_word], axis=1)
        v = jnp.concatenate([v_img, v_word], axis=1)
        q = _split_heads(q_word)
        k = _split_heads(k)
        v = _split_heads(v)
        scores = jnp.einsum('bhqd,bhkd->bhqk', q, k) / jnp.sqrt(jnp.float32(HDIM))
        qi = jnp.arange(S)[:, None]
        kj = jnp.arange(S + 1)[None, :]
        causal = kj <= qi + 1
        scores = jnp.where(causal[None, None], scores, jnp.float32(MASK_OUT))
        zero_col = jnp.zeros(attention_mask.shape[:-1] + (1,), attention_mask.dtype)
        mask = jnp.concatenate([zero_col, attention_mask], axis=-1)
        scores = scores + mask
        attn = jax.nn.softmax(scores, axis=-1)
        out = jnp.einsum('bhqk,bhkd->bhqd', attn, v)
        out = out.transpose(0, 2, 1, 3).reshape(B, S, EMBED)
        out = out @ c_proj_w + c_proj_b
        return out
    x = x + _L0_cond_ref(x, cond_1024, L0_cond_router_W, L0_cond_router_bias, L0_cond_w1, L0_cond_w3, L0_cond_w2, L0_cond_W1e, L0_cond_W2e)
    x = x + _L1_cond_ref(x, cond_1024, L1_cond_W_router, L1_cond_router_bias, L1_cond_s_w1, L1_cond_s_w3, L1_cond_s_w2, L1_cond_r_w1, L1_cond_r_w2)
    x = x + _L2_cond_ref(cond_1024, x, L2_cond_W, L2_cond_b, L2_cond_alpha)
    x = x + _L3_cond_ref(x, cond_1024, mask_Bx1x1xS_ff0, L3_cond_c_attn_w, L3_cond_c_attn_b, L3_cond_c_proj_w, L3_cond_c_proj_b, L3_cond_uk_w, L3_cond_uk_b, L3_cond_uv_w, L3_cond_uv_b)
    return x

_drawn_inputs = setup_inputs


def setup_inputs(seed=0):
    import zlib

    import numpy as np

    out = dict(_drawn_inputs(seed))
    spreads = {'L0_cond_router_bias': (0.0, 0.8),
     'L1_cond_router_bias': (0.0, 0.8),
     'L2_cond_alpha': (0.10000000149011612, 0.6),
     'L3_cond_c_attn_b': (0.0, 0.508),
     'L3_cond_c_proj_b': (0.0, 0.8),
     'L3_cond_uk_b': (0.0, 2.0),
     'L3_cond_uv_b': (0.0, 2.0)}
    factors = {'L0_cond_router_W': 8.0,
     'L0_cond_w1': 8.0,
     'L0_cond_w3': 8.0,
     'L0_cond_w2': 8.0,
     'L0_cond_W1e': 8.0,
     'L0_cond_W2e': 8.0,
     'L1_cond_W_router': 8.0,
     'L1_cond_s_w1': 8.0,
     'L1_cond_s_w3': 8.0,
     'L1_cond_s_w2': 8.0,
     'L1_cond_r_w1': 8.0,
     'L1_cond_r_w2': 8.0,
     'L2_cond_b': 8.0,
     'L3_cond_c_attn_w': 6.16,
     'L3_cond_c_proj_w': 3.157,
     'L3_cond_uk_w': 30.322,
     'L3_cond_uv_w': 62.443}
    for name, (base, spread) in spreads.items():
        noise = np.random.default_rng([zlib.crc32(name.encode()), seed]).standard_normal(out[name].shape)
        drawn = base * np.exp(spread * noise) if base else spread * noise
        out[name] = jnp.asarray(drawn.astype(out[name].dtype))
    for name, factor in factors.items():
        out[name] = (out[name] * factor).astype(out[name].dtype)
    return out
```

```python
from contextlib import ExitStack

import numpy as np
import concourse.bass as bass
from concourse import mybir

F32 = mybir.dt.float32
BF16 = mybir.dt.bfloat16
F16 = mybir.dt.float16
U32 = mybir.dt.uint32
ACT = mybir.ActivationFunctionType
ALU = mybir.AluOpType
AX = mybir.AxisListType

P = 128
B, T, D = 8, 256, 128
E = 8
H, HD = 16, 8
G, J = 4, 4
HP = 32
SHARED = (2, 4)
SHARED_SCALE = (0.5 / 3.0, 0.5 / 8.0)
GATE_SCALE = (1.0 / 3.0, 1.0 / 4.0)
CHUNKS = (16, 48, 64, 64, 64)
STARTS = tuple(sum(CHUNKS[:i]) for i in range(len(CHUNKS)))
NC = len(CHUNKS)
QT = 128
NEG = -1.0e5
SC = float(1.0 / np.sqrt(HD))
EPS = 1e-9
XP = 32
ZR = 128
NHT, NHB, NHG = 3, 8, 4
PE_CAP, ACT_CAP, DVE_CAP = 900, 560, 1000


def columns(*parts):
    at, out = 0, {}
    for name, width in parts:
        out[name] = (at, width)
        at += width
    return out, at


SMALL, N_SMALL = columns(("cond", P), ("wrx0", E), ("wrt0", E), ("wrx1", E), ("wrt1", E), ("rb0", E), ("rb1", E),
                         ("alpha", 1), ("b2", 1), ("ident", P), ("iota", E))
SEL_AT = N_SMALL

FF0, N_FF0 = columns(("w1", 256), ("w3", 256), ("w2", 256), ("e1", E * P), ("e2", E * P))
FF1, N_FF1 = columns(("w1", 512), ("w3", 512), ("w2", 512), ("e1", E * P), ("e2", E * P))
REC, N_REC = columns(("wh", P), ("wz", P))
ATT, N_ATT = columns(("wq", G * P), ("wk", G * P), ("wv", P), ("wp", P), ("uk", G * P), ("uv", P), ("qb", G), ("kb", G),
                     ("ukb", G), ("pb", 1), ("uvb", 1), ("vb", P), ("causal", P), ("hm", J), ("hx", J), ("sq", 1), ("mq", 1),
                     ("sk", 1), ("mk", 1), ("hmk", G * H), ("hexp", P), ("maskt", B * 2))


def plan():
    units = []

    def add(key, pe, act, dve, bank, *needs):
        units.append((key, pe, act, dve, bank, needs))

    mm4 = lambda n: 4 * n / 2.4
    for c in range(NC):
        n = CHUNKS[c] * B
        k = n // P
        for l in range(2):
            src = (("YE", c, 0), "dve", "pe") if l else None
            x = [src] if src else [(("YE", c - 2, 1), "dve", "dve")] if c >= 2 else []
            half = [(0, min(2, k))] + ([(2, k)] if k > 2 else [])
            for r, (a, b) in enumerate(half):
                add(("R", c, l, r), 400 * (b - a), 0, 130, True, *x, *([(("RG", c - 1, l), "dve", "dve")] if c else []))
            add(("RT", c, l), 0, 220, 0, False, (("R", c, l, len(half) - 1), "dve", "act"))
            add(("RS", c, l), 0, 0, 80 * (2 + 2 * k), False, (("RT", c, l), "act", "dve"))
            add(("RG", c, l), 0, 0, 80 * 14, False, (("RS", c, l), "dve", "dve"))
            add(("GT", c, l), 60 * k, 0, 60 + n, True, (("RG", c, l), "dve", "pe"),
                *([(("M", c - 1, l, E - 1), "pe", "pe")] if c else []))
            for j in range(SHARED[l]):
                add(("SA", c, l, j), mm4(n), 60 + n * .84, 100 + n * 1.05, True, *x)
                add(("SB", c, l, j), mm4(n), 0, 100 + n * 1.05, True, (("SA", c, l, j), "dve", "dve"), *x)
                add(("Y", c, l, "s", j), mm4(n), 0, 0, False, (("SB", c, l, j), "dve", "pe"),
                    *([(("YE", c - 1, l), "dve", "pe")] if c else []))
            for e in range(E):
                add(("E", c, l, e), mm4(n), 60 + n * .84, 0, True, *x)
            for e in range(E):
                add(("M", c, l, e), n / 2.4, 0, 100 + n * 1.05, True, (("E", c, l, e), "act", "dve"),
                    (("GT", c, l), "dve", "pe"))
                add(("Y", c, l, "e", e), mm4(n), 0, 0, False, (("M", c, l, e), "dve", "pe"),
                    *([(("YE", c - 1, l), "dve", "pe")] if c else []))
            last = [("Y", c, l, "e", e) for e in range(E)] + [("Y", c, l, "s", j) for j in range(SHARED[l])]
            add(("YE", c, l), 0, 0, 100 + n * 1.05, False, *[(y, "pe", "dve") for y in last])
        add(("C", c), mm4(n) + 3 * n / 2.4, 0, 0, False, (("YE", c, 1), "dve", "pe"))
    for t in range(T // QT):
        kq = (("STEP", QT * (t + 1) - 1), "pool", "pe")
        for v in range(2):
            add(("V", t, v), 880, 0, 640, True, kq)
        for g in range(G):
            for h in range(2):
                add(("K", t, g, h), 860, 960, 640, True, kq)
        for g in range(G):
            for h in range(2):
                add(("Q", t, g, h), 860, 960, 1400, True, kq)
        prev = []
        for b in range(B):
            n_a = 4 if t == 0 else 8
            for a in range(n_a):
                add(("A", t, b, a), 430, 0, 660, True, (("K", t, G - 1, 1), "dve", "pe"), (("Q", t, G - 1, 1), "dve", "pe"))
            add(("MX", t, b), 220, 0, 320, True, (("A", t, b, n_a - 1), "dve", "dve"), (("Q", t, G - 1, 1), "dve", "pe"))
        for q in range(2):
            add(("IM", t, q), 1100, 500, 0, True, *[(("MX", t, b), "dve", "pe") for b in range(4 * q, 4 * q + 4)])
            add(("ID", t, q), 860, 0, 1300, True, (("IM", t, q), "act", "pe"))
        for b in range(B):
            for g in range(G):
                for kb in range(t + 1):
                    add(("S", t, b, g, kb), 440, 500, 0, True, (("MX", t, b), "dve", "pe"))
                    add(("AV", t, b, g, kb), 430, 0, 0, False, (("S", t, b, g, kb), "act", "pe"),
                        *([(("X", t, b - 1), "dve", "pe")] if b else [(("X", t - 1, B - 1), "dve", "pe")] if t else []))
            add(("X", t, b), 0, 0, 2500, False, (("AV", t, b, G - 1, t), "pe", "dve"), (("ID", t, b // 4), "dve", "dve"))
        for q in range(2):
            add(("O", t, q), 860, 0, 700, True, *[(("X", t, b), "dve", "pe") for b in range(4 * q, 4 * q + 4)])

    lag = {("dve", "pe"): 3, ("act", "pe"): 2, ("pe", "pe"): 0, ("dve", "act"): 2, ("act", "dve"): 0, ("dve", "dve"): 0,
           ("pe", "dve"): 0}
    slot_of, step_slot, order = {}, {}, []
    users, hg_users, hb_users = [], [], []
    left = list(units)
    s = step = 0
    while left or step < T:
        if step < T:
            c = chunk_of(step)
            if ("C", c) in slot_of and slot_of["C", c] < s:
                step_slot[step] = s
                step += 1
        pe = act = dve = 0
        passed = set()
        for u in list(left):
            key, up, ua, ud, bank, needs = u
            family = key[:3] if key[0] in ("R", "SA", "SB", "E", "M", "GT") else key[:2]
            if key[0] != "Y" and family in passed:
                continue
            passed.add(family)
            if (pe and up and pe + up > PE_CAP) or (act and ua and act + ua > ACT_CAP) or (dve and ud and dve + ud > DVE_CAP):
                continue
            ok = True
            for k, of, by in needs:
                if k[0] == "STEP":
                    ok = k[1] in step_slot and step_slot[k[1]] + 3 <= s
                elif k not in slot_of or slot_of[k] + lag[of, by] > s:
                    ok = False
                if not ok:
                    break
            if ok and key[0] == "C" and key[1] >= 2:
                end = STARTS[key[1] - 1] - 1
                ok = end in step_slot and step_slot[end] + 2 <= s
            if ok and bank and len(users) >= NHT:
                k = users[-NHT]
                ok = slot_of[k] + (2 if k[0] in ("E", "IM", "S") else 3) <= s
            if ok and key[0] in ("M", "SB") and len(hg_users) >= NHG:
                k = hg_users[-NHG]
                y = ("Y", k[1], k[2], "e", k[3]) if k[0] == "M" else ("Y", k[1], k[2], "s", k[3])
                ok = y in slot_of and slot_of[y] <= s + 1
            if ok and key[0] == "E" and len(hb_users) >= NHB:
                k = hb_users[-NHB]
                k = ("M",) + k[1:]
                ok = k in slot_of and slot_of[k] + 2 <= s
            if ok and key[0] == "SA":
                ok = not any(k[0] == "SA" and ("SB",) + k[1:] not in slot_of for k in slot_of)
            if ok and key[0] in ("S", "IM"):
                ok = ("YE", NC - 1, 1) in slot_of and slot_of["YE", NC - 1, 1] + 2 < s
            if ok and key[0] == "S":
                ok = sum(k[0] == "S" for k in slot_of) - sum(k[0] == "AV" for k in slot_of) < 4
            if not ok:
                continue
            passed.discard(family)
            slot_of[key] = s
            order.append((s, key))
            left.remove(u)
            pe, act, dve = pe + up, act + ua, dve + ud
            if bank:
                users.append(key)
            if key[0] in ("M", "SB"):
                hg_users.append(key)
            if key[0] == "E":
                hb_users.append(key)
            if pe >= PE_CAP:
                break
        s += 1
        assert s < 1000, (left[:3], users[-4:], hg_users[-5:], hb_users[-9:], step)
    info = {u[0]: u for u in units}
    bank_of = {k: i % NHT for i, k in enumerate(users)}
    before = {k: users[i - NHT] for i, k in enumerate(users) if i >= NHT}
    hg_of = {k: i for i, k in enumerate(hg_users)}
    hb_of = {k: i for i, k in enumerate(hb_users)}
    n_slots = s + 3
    parts = {"pe": [[] for _ in range(n_slots)], "act": [[] for _ in range(n_slots)], "dve": [[] for _ in range(n_slots)]}
    for at, key in order:
        for eng, later, cost in (("pe", 0, 1), ("act", 1, 2), ("dve", 2, 3)):
            if info[key][cost]:
                parts[eng][at + later].append(key)
    nth = {}
    for eng in parts:
        n = 0
        for units_of_slot in parts[eng]:
            for key in units_of_slot:
                n += 1
                nth[eng, key] = n
    steps = {at: t for t, at in step_slot.items()}
    pool = [(slot_of["YE", c, 1] + 2, "Z", c) for c in range(NC)]
    pool += [(step_slot[t0 + XP - 1] + 1, "X3", t0) for t0 in range(0, T, XP)]
    pool += [(max([slot_of["MX", t, b] + 2] + [slot_of["S", t2, b2, G - 1, t2] for t2, b2 in [divmod(t * B + b - 2, B)]
                                               if t or b >= 2]), "LM", t, b) for t in range(T // QT) for b in range(B)]
    parts["pool"] = [u[1:] for u in sorted(pool)]
    return parts, nth, steps, bank_of, before, hg_of, hb_of, n_slots


def chunk_of(t):
    return max(i for i in range(NC) if STARTS[i] <= t)


def build(nc, x_in, small_in, ff0_in, ff1_in, rec_in, att_in, maskr_in, out):
    parts, nth, steps, bank_of, before, hg_of, hb_of, n_slots = plan()

    with ExitStack() as ctx:
        def sb(name, shape, dt=F32):
            return ctx.enter_context(nc.sbuf_tensor(name, shape, dt))

        def ps(name):
            return ctx.enter_context(nc.psum_tensor(name, [P, 512], F32))

        def sem(name):
            return ctx.enter_context(nc.semaphore(name))

        x = sb("x", [P, T * B])
        small = sb("small", [P, N_SMALL])
        ff = (sb("ff0", [P, N_FF0]), sb("ff1", [P, N_FF1]))
        rec = sb("rec", [P, N_REC])
        att = sb("att", [P, N_ATT])
        ident = sb("ident", [P, P], BF16)
        sel = sb("sel", [P, E, P], BF16)
        ones = sb("ones", [P, HP])
        tc = sb("tc", [P, 2, E])
        lg = sb("lg", [P, 2, 4, E])
        th = sb("th", [P, 2, 4, E])
        sg = sb("sg", [P, 2, 4, E])
        sl = sb("sl", [P, 2, 4, E])
        mx8 = sb("mx8", [P, 2, 4, 8])
        ix8 = sb("ix8", [P, 2, 4, 8], U32)
        ixf = sb("ixf", [P, 2, 4, 2])
        pick = sb("pick", [P, 4, E])
        pick2 = sb("pick2", [P, 4, E])
        den2 = sb("den2", [P, 4])
        rcp2 = sb("rcp2", [P, 4])
        zer2 = sb("zer2", [P, 4])
        gr = sb("gr", [P, 4, E])
        g3 = sb("g3", [P, 2, 4, 3 * E], BF16)
        gt = sb("gt", [P, 2, 512], BF16)
        hb = sb("hb", [P, NHB, 512])
        hg = sb("hg", [P, NHG, 512])
        sth = sb("sth", [P, 512])
        sgl = sb("sgl", [P, 512])
        wh3 = sb("wh3", [P, 3, P], BF16)
        wr = sb("wr", [P, P])
        wr2 = sb("wr2", [P, P])
        b3 = sb("b3", [P, 3], BF16)
        br = sb("br", [P, 2])
        leak = sb("leak", [P, 1])
        d0 = sb("d0", [P, ZR, B, 2])
        d1 = sb("d1", [P, 2, B, 2])
        hs = sb("hs", [P, T + 1, B])
        hhi = sb("hhi", [P, 2, B], F16)
        hlo = sb("hlo", [P, 2, B], F16)
        x3 = sb("x3", [P, B, T])
        kp = sb("kp", [P, G, B, T], F16)
        maskr = kp[:].rearrange("p g b t -> p (g b t)").bitcast(F32).rearrange("p (x b t) -> p x b t", x=2, b=B)[:, 0]
        fq = sb("fq", [P, G, B, QT], F16)
        qz = sb("qz", [P, G, B, J, QT], F16)
        xs = sb("xs", [P, 2, 512])
        tt = sb("tt", [P, 2, 512], F16)
        fk = sb("fk", [P, G, B], F16)
        fx = sb("fx", [P, G, B])
        ft = sb("ft", [P, G, B], F16)
        kbd = sb("kbd", [P, G, B, H], F16)
        vimg = sb("vimg", [P, B])
        v = sb("v", [P, B, 2, P])
        sbq = sb("sbq", [P, G])
        sbk = sb("sbk", [P, G])
        mb = sb("mb", [P, B, 3, QT], BF16)
        cz = sb("cz", [P, P], BF16)
        wm = sb("wm", [P, B, H])
        mm = sb("mm", [P, B, H])
        mneg = sb("mneg", [P, B, H], BF16)
        lm = sb("lm", [P, 2, H, QT], BF16)
        eimg = sb("eimg", [P, 512])
        pt = hb[:, 0:4, :]
        dimg = hb[:, 4:6, :].rearrange("p a (b q) -> p (a b) q", q=QT)
        nimg = hb[:, 6:8, :].rearrange("p a (b q) -> p (a b) q", q=QT)
        on = hg[:, 0:2, :].rearrange("p a (b q) -> p (a b) q", q=QT)
        num = sb("num", [P, 2, QT])
        den = sb("den", [P, 2, QT])
        ob = sb("ob", [P, 2, 4, QT])

        hid = [ps(f"hid{i}") for i in range(NHT)]
        ybk = [ps("ybk0"), ps("ybk1")]
        cbk = [ps("cbk0"), ps("cbk1")]
        vbk = ps("vbk")
        vps = vbk[:, 0:2 * B]

        in_x = [sem(f"in_x{c}") for c in range(NC)]
        in_small, in_ff0, in_ff1, in_rec, in_att = (sem(f"in_{n}") for n in ("small", "ff0", "ff1", "rec", "att"))
        pe_done = sem("pe_done")
        act_done = sem("act_done")
        dve_done = sem("dve_done")
        dve_link = sem("dve_link")
        act_link = sem("act_link")
        pool_set = sem("pool_set")
        z_ready = sem("z_ready")
        x3_ready = sem("x3_ready")
        consts = sem("consts")
        cond_pe = sem("cond_pe")
        gate_pre = sem("gate_pre")
        gate_th = sem("gate_th")
        decay = sem("decay")
        blend = sem("blend")
        h_hi = sem("h_hi")
        h_full = sem("h_full")
        h_lo = sem("h_lo")
        maxes = sem("maxes")
        lm_ready = sem("lm_ready")
        stored = [sem("stored0"), sem("stored1")]

        def S(name):
            a, n = SMALL[name]
            return small[:, a:a + n]

        def F(l, name, i=None):
            a, n = (FF0, FF1)[l][name]
            return ff[l][:, a:a + n] if i is None else ff[l][:, a + i * P:a + i * P + P]

        def A(name, i=None, w=P):
            a, n = ATT[name]
            return att[:, a:a + n] if i is None else att[:, a + i * w:a + i * w + w]

        wh = rec[:, 0:P]
        wz = rec[:, P:2 * P]
        hm, hx = A("hm"), A("hx")
        first_y, last_y = {}, {}
        for slot in parts["pe"]:
            for key in slot:
                if key[0] == "Y":
                    first_y.setdefault(key[1:3], key)
                    last_y[key[1:3]] = key
        order_of = lambda kinds, eng: [k for slot in parts[eng] for k in slot if k[0] in kinds]
        hg_key = sorted(hg_of, key=hg_of.get)
        hb_key = sorted(hb_of, key=hb_of.get)
        kq_key, s_key, sa_key = order_of(("K", "Q"), "act"), order_of(("S",), "act"), order_of(("SA",), "act")
        kq_order = {k: i for i, k in enumerate(kq_key)}
        s_order = {k: i for i, k in enumerate(s_key)}

        def cols(c):
            return slice(STARTS[c] * B, (STARTS[c] + CHUNKS[c]) * B)

        block = ctx.enter_context(nc.Block())

        @block.sync
        def _(sp):
            sp.dma_start(small[:], small_in[:, 0:N_SMALL]).then_inc(in_small, 16)
            sp.dma_start(x3[:, 0:E * P // T, :].rearrange("p b t -> p (b t)"),
                         small_in[:, SEL_AT:SEL_AT + E * P]).then_inc(in_small, 16)
            sp.dma_start(x[:, cols(0)], x_in[:, cols(0)]).then_inc(in_x[0], 16)
            sp.dma_start(ff[0][:], ff0_in).then_inc(in_ff0, 16)
            sp.dma_start(ff[1][:], ff1_in).then_inc(in_ff1, 16)
            for c in range(1, NC):
                sp.dma_start(x[:, cols(c)], x_in[:, cols(c)]).then_inc(in_x[c], 16)
            for t in range(T // QT):
                for q in range(2):
                    sp.wait_ge(dve_done, nth["dve", ("O", t, q)])
                    sp.dma_start(out[:, 4 * q:4 * q + 4, t * QT:(t + 1) * QT],
                                 ob[:, q, :, :]).then_inc(stored[q], 16)
            for q in range(2):
                sp.wait_ge(stored[q], 16 * (T // QT))

        @block.gpsimd
        def _(pool):
            nc.gpsimd.memset(d0[:], 0.0).then_inc(pool_set, 1)
            nc.gpsimd.memset(gt[:], 0.0).then_inc(pool_set, 1)
            nc.gpsimd.memset(eimg[:], 0.0).then_inc(pool_set, 1)
            nc.gpsimd.memset(ones[:], 1.0).then_inc(pool_set, 1)
            pool.wait_ge(in_att, 32)
            C = A("causal").rearrange("p (o k) -> p o k", o=1)
            nc.gpsimd.tensor_scalar(maskr, maskr, 1.0 / SC, None, ALU.mult).then_inc(pool_set, 1)
            pool.wait_ge(pool_set, 5)
            nc.gpsimd.tensor_tensor(mb[:, :, 0, :], maskr[:, :, 0:QT], C.broadcast_to([P, B, QT]), ALU.add)
            nc.gpsimd.tensor_copy(mb[:, :, 1, :], maskr[:, :, 0:QT])
            nc.gpsimd.tensor_tensor(mb[:, :, 2, :], maskr[:, :, QT:T], C.broadcast_to([P, B, QT]), ALU.add)
            nc.gpsimd.tensor_copy(cz[:], A("causal")).then_inc(pool_set, 1)
            for kind, *key in parts["pool"]:
                if kind == "Z":
                    c, = key
                    pool.wait_ge(dve_done, nth["dve", ("YE", c, 1)])
                    if STARTS[c] + CHUNKS[c] > ZR:
                        pool.wait_ge(blend, STARTS[c] + CHUNKS[c] - ZR)
                    z0 = STARTS[c] % ZR
                    nc.gpsimd.tensor_scalar(d0[:, z0:z0 + CHUNKS[c], :, 1],
                                            x[:, cols(c)].rearrange("p (t b) -> p t b", b=B), 0.5, None,
                                            ALU.mult).then_inc(z_ready, 1)
                elif kind == "X3":
                    t0, = key
                    pool.wait_ge(h_full, t0 + XP)
                    nc.gpsimd.tensor_tensor(x3[:, :, t0:t0 + XP].rearrange("p b t -> p t b"),
                                            x[:, t0 * B:(t0 + XP) * B].rearrange("p (t b) -> p t b", b=B),
                                            hs[:, t0 + 1:t0 + XP + 1, :], ALU.add).then_inc(x3_ready, 1)
                else:
                    t, b = key
                    pool.wait_ge(dve_done, nth["dve", ("MX", t, b)])
                    if t or b >= 2:
                        t2, b2 = divmod(t * B + b - 2, B)
                        pool.wait_ge(pe_done, nth["pe", ("S", t2, b2, G - 1, t2)])
                    for g in range(G):
                        i = nc.gpsimd.tensor_tensor(
                            lm[:, b % 2, J * g:J * g + J, :],
                            cz[:].rearrange("p (o k) -> p o k", o=1).broadcast_to([P, J, QT]),
                            mneg[:, b, J * g:J * g + J].rearrange("p (j o) -> p j o", o=1).broadcast_to([P, J, QT]), ALU.add)
                    i.then_inc(lm_ready, 1)

        @block.scalar
        def _(act):
            act.dma_start(rec[:], rec_in).then_inc(in_rec, 16)
            act.dma_start(hs[:, 0, :], small_in[:, SMALL["cond"][0]:SMALL["cond"][0] + B]).then_inc(in_rec, 16)
            act.dma_start(att[:], att_in).then_inc(in_att, 16)
            act.dma_start(maskr.rearrange("p b t -> p (b t)"), maskr_in).then_inc(in_att, 16)

            def unit(key):
                kind = key[0]
                if ("pe", key) in nth:
                    act.wait_ge(pe_done, nth["pe", key])
                if kind == "RT":
                    _, c, l = key
                    k = CHUNKS[c] * B // P
                    act.wait_ge(dve_done, nth["dve", ("R", c, l, 1 if k > 2 else 0)])
                    nc.scalar.activation(th[:, l, 0:k, :], lg[:, l, 0:k, :], ACT.Tanh, scale=0.5).then_inc(act_done, 1)
                elif kind == "SA":
                    _, c, l, j = key
                    n = CHUNKS[c] * B
                    i = sa_key.index(key)
                    if i:
                        act.wait_ge(dve_done, nth["dve", sa_key[i - 1]])
                    nc.scalar.activation(sth[:, 0:n], hid[bank_of[key]][:, 0:n], ACT.Tanh, scale=0.5).then_inc(act_done, 1)
                elif kind == "E":
                    _, c, l, e = key
                    n = CHUNKS[c] * B
                    i = hb_of[key]
                    if i >= NHB:
                        act.wait_ge(dve_done, nth["dve", ("M",) + hb_key[i - NHB][1:]])
                    nc.scalar.activation(hb[:, i % NHB, 0:n], hid[bank_of[key]][:, 0:n], ACT.Gelu).then_inc(act_done, 1)
                elif kind in ("K", "Q"):
                    _, t, g, h = key
                    i = kq_order[key]
                    if i >= 2:
                        act.wait_ge(dve_done, nth["dve", kq_key[i - 2]])
                    bias = A("kb" if kind == "K" else "qb", g, 1)
                    sign = A("sk" if kind == "K" else "sq")
                    nc.scalar.activation(xs[:, i % 2, :], hid[bank_of[key]][:], ACT.Identity, bias=bias)
                    nc.scalar.activation(tt[:, i % 2, :], hid[bank_of[key]][:], ACT.Identity, bias=(sbk if kind == "K" else sbq)[:, g:g + 1],
                                         scale=sign).then_inc(act_done, 1)
                elif kind == "IM":
                    _, t, q = key
                    act.wait_ge(dve_done, nth["dve", ("YE", NC - 1, 1)])
                    if (t, q) != (0, 0):
                        prev = ("ID", t, 0) if q else ("ID", t - 1, 1)
                        act.wait_ge(pe_done, nth["pe", prev])
                    else:
                        act.wait_ge(pool_set, 3)
                    nc.scalar.activation(eimg[0:H, :], hid[bank_of[key]][0:H, :], ACT.Exp, scale=SC).then_inc(act_done, 1)
                elif kind == "S":
                    _, t, b, g, kb = key
                    i = s_order[key]
                    if i >= 4:
                        act.wait_ge(pe_done, nth["pe", ("AV",) + s_key[i - 4][1:]])
                    nc.scalar.activation(pt[:, i % 4, :], hid[bank_of[key]][:], ACT.Exp,
                                         bias=A("maskt", b * 2 + kb, 1), scale=SC).then_inc(act_done, 1)

            act.wait_ge(consts, 1)
            for s in range(n_slots):
                t = steps.get(s)
                if t is not None:
                    act.wait_ge(gate_pre, t + 1)
                    c = chunk_of(t)
                    o = (t - STARTS[c]) * B
                    nc.scalar.activation(d1[:, t % 2, :, 0], cbk[c % 2][:, o:o + B], ACT.Tanh,
                                         scale=0.5).then_inc(gate_th, 1)
                for key in parts["act"][s]:
                    unit(key)
                if t is not None:
                    act.wait_ge(blend, t + 1)
                    new = vps.rearrange("p (b o) -> p b o", o=2)[:, :, 1]
                    if t + 1 < T:
                        nc.scalar.activation(hhi[:, (t + 1) % 2, :], new, ACT.Tanh).then_inc(h_hi, 1)
                    nc.scalar.activation(hs[:, t + 1, :], new, ACT.Tanh).then_inc(h_full, 1)

        @block.tensor
        def _(pe):
            def free(key):
                if key in before:
                    k = before[key]
                    eng = "act" if k[0] in ("E", "IM", "S") else "dve"
                    pe.wait_ge(act_done if eng == "act" else dve_done, nth[eng, k])

            def unit(key):
                kind = key[0]
                if key in bank_of:
                    free(key)
                    hk = hid[bank_of[key]]
                if kind == "R":
                    _, c, l, r = key
                    k = CHUNKS[c] * B // P
                    x_ready(c, l)
                    for i in range(2 * r, min(2 * r + 2, k)):
                        a = STARTS[c] * B + i * P
                        m = pe.matmul(hk[:, i * E:i * E + E], x[:, a:a + P], S(f"wrx{l}"), start=True, stop=True)
                elif kind == "GT":
                    _, c, l = key
                    k = CHUNKS[c] * B // P
                    pe.wait_ge(dve_done, nth["dve", ("RG", c, l)])
                    for i in range(k):
                        m = pe.matmul(hk[0:3 * E, i * P:i * P + P], g3[:, l, i, :], ident[:], start=True, stop=True)
                elif kind in ("SA", "SB"):
                    _, c, l, j = key
                    x_ready(c, l)
                    m = pe.matmul(hk[:, 0:CHUNKS[c] * B], F(l, "w1" if kind == "SA" else "w3", j), x[:, cols(c)],
                                  start=True, stop=True)
                elif kind == "E":
                    _, c, l, e = key
                    x_ready(c, l)
                    m = pe.matmul(hk[:, 0:CHUNKS[c] * B], F(l, "e1", e), x[:, cols(c)], start=True, stop=True)
                elif kind == "M":
                    _, c, l, e = key
                    n = CHUNKS[c] * B
                    pe.wait_ge(dve_done, nth["dve", ("GT", c, l)])
                    m = pe.matmul(hk[:, 0:n], sel[:, e, :], gt[:, l, 0:n], start=True, stop=True)
                elif kind == "Y":
                    _, c, l, of, e = key
                    n = CHUNKS[c] * B
                    shared = of == "s"
                    made = ("SB" if shared else "M", c, l, e)
                    pe.wait_ge(dve_done, nth["dve", made])
                    first = first_y[c, l] == key
                    if first and c:
                        pe.wait_ge(dve_done, nth["dve", ("YE", c - 1, l)])
                    m = pe.matmul(ybk[l][:, 0:n], F(l, "w2" if shared else "e2", e), hg[:, hg_of[made] % NHG, 0:n],
                                  start=first, stop=last_y[c, l] == key)
                elif kind == "C":
                    _, c = key
                    n = CHUNKS[c] * B
                    pe.wait_ge(dve_done, nth["dve", ("YE", c, 1)])
                    if c >= 2:
                        pe.wait_ge(gate_th, STARTS[c - 1])
                    cb = cbk[c % 2][:, 0:n]
                    pe.matmul(cb, wz, x[:, cols(c)], start=True, stop=True)
                    for i in range(3):
                        m = pe.matmul(cb, ident[:], b3[:, i:i + 1].broadcast_to([P, n]), start=False, stop=True,
                                      skip_group_check=True)
                elif kind in ("K", "Q"):
                    _, t, g, h = key
                    t0 = t * QT + 64 * h
                    pe.wait_ge(x3_ready, t0 // 32 + 2)
                    m = pe.matmul(hk[:], A("wk" if kind == "K" else "wq", g), x3[:, :, t0:t0 + 64], start=True, stop=True)
                elif kind == "V":
                    _, t, q = key
                    pe.wait_ge(x3_ready, 4 * (t + 1))
                    for i in range(4):
                        m = pe.matmul(hk[:, i * P:i * P + P], x3[:, 4 * q + i, t * QT:(t + 1) * QT], A("wv"),
                                      start=True, stop=True)
                elif kind == "A":
                    _, t, b, a = key
                    pe.wait_ge(dve_done, nth["dve", ("K", t, G - 1, 1)])
                    pe.wait_ge(dve_done, nth["dve", ("Q", t, G - 1, 1)])
                    if (t, b, a) == (0, 0, 0):
                        pe.wait_ge(pool_set, 6)
                    if t == 0:
                        pe.matmul(hk[:], ident[:], mb[:, b, 0:1, :].broadcast_to([P, J, QT]), start=True, stop=True)
                        for j in range(J):
                            m = pe.matmul(hk[:, j * QT:j * QT + QT], qz[:, a, b, j, :], kp[:, a, b, 0:QT],
                                          start=False, stop=True, skip_group_check=True)
                    else:
                        g, j0 = a // 2, 2 * (a % 2)
                        for i in range(2):
                            pe.matmul(hk[:, i * T:i * T + T], ident[:], mb[:, b, 1:3, :].rearrange("p a k -> p (a k)"),
                                      start=i == 0, stop=True, skip_group_check=True)
                        for i in range(2):
                            m = pe.matmul(hk[:, i * T:i * T + T], qz[:, g, b, j0 + i, :], kp[:, g, b, :],
                                          start=False, stop=True, skip_group_check=True)
                elif kind == "MX":
                    _, t, b = key
                    for g in range(G):
                        m = pe.matmul(hk[:, 0:H], fq[:, g, b, :], kbd[:, g, b, :], start=g == 0, stop=g == G - 1)
                elif kind == "IM":
                    _, t, q = key
                    for i in range(4):
                        b = 4 * q + i
                        pe.wait_ge(dve_done, nth["dve", ("MX", t, b)])
                        pe.matmul(hk[0:H, i * QT:i * QT + QT], mneg[:, b, :], ident[:], start=i == 0, stop=True,
                                  skip_group_check=True)
                        for g in range(G):
                            m = pe.matmul(hk[0:H, i * QT:i * QT + QT], kbd[:, g, b, :], fq[:, g, b, :], start=False,
                                          stop=True, skip_group_check=True)
                elif kind == "ID":
                    _, t, q = key
                    pe.wait_ge(act_done, nth["act", ("IM", t, q)])
                    m = pe.matmul(hk[:], A("hexp"), eimg[:], start=True, stop=True)
                elif kind == "S":
                    _, t, b, g, kb = key
                    pe.wait_ge(dve_done, nth["dve", ("MX", t, b)])
                    pe.matmul(hk[:], kp[:, g, b, kb * QT:kb * QT + QT], qz[:, g, b, :, :].rearrange("p j q -> p (j q)"),
                              start=True, stop=True)
                    if kb == t:
                        pe.wait_ge(lm_ready, t * B + b + 1)
                    for j in range(J):
                        hh = J * g + j
                        w = lm[:, b % 2, hh, :] if kb == t else mneg[:, b, hh:hh + 1].broadcast_to([P, QT])
                        m = pe.matmul(hk[:, j * QT:j * QT + QT], w, ident[:], start=False, stop=True,
                                      skip_group_check=True)
                elif kind == "AV":
                    _, t, b, g, kb = key
                    pe.wait_ge(act_done, nth["act", ("S", t, b, g, kb)])
                    pe.wait_ge(dve_done, nth["dve", ("V", t, 1)])
                    if g == 0 and kb == 0 and (t or b):
                        pe.wait_ge(dve_done, nth["dve", ("X", t, b - 1) if b else ("X", t - 1, B - 1)])
                    p = pt[:, s_order["S", t, b, g, kb] % 4, :]
                    r = slice(HP * g, HP * g + HP)
                    pe.matmul(ybk[0][r, :], v[:, b, kb, r], p, start=kb == 0, stop=kb == t)
                    m = pe.matmul(ybk[1][r, :], ones[:], p, start=kb == 0, stop=kb == t)
                elif kind == "O":
                    _, t, q = key
                    pe.wait_ge(dve_done, nth["dve", ("X", t, 4 * q + 3)])
                    m = pe.matmul(hk[:], A("wp"), on[:, 4 * q:4 * q + 4, :], start=True, stop=True)
                m.then_inc(pe_done, 1)

            def x_ready(c, l):
                if l:
                    pe.wait_ge(dve_done, nth["dve", ("YE", c, 0)])
                else:
                    pe.wait_ge(in_x[c], 16)
                if c == 0:
                    pe.wait_ge(in_ff1 if l else in_ff0, 16)

            pe.wait_ge(in_small, 32)
            for l in range(2):
                m = pe.matmul(hid[0][:, l * E:l * E + E], S("cond"), S(f"wrt{l}"), start=True, stop=True)
            m.then_inc(cond_pe, 1)
            pe.wait_ge(in_att, 32)
            for g in range(G):
                m = pe.matmul(hid[1][:, g * B:g * B + B], A("uk", g), S("cond")[:, 0:B], start=True, stop=True)
            pe.matmul(hid[1][:, G * B:G * B + B], A("uv"), S("cond")[:, 0:B], start=True, stop=True).then_inc(cond_pe, 1)
            pe.wait_ge(in_rec, 32)
            pe.wait_ge(consts, 1)
            pe.wait_ge(pool_set, 4)
            for s in range(n_slots):
                t = steps.get(s)
                if t is not None:
                    c = chunk_of(t)
                    o = (t - STARTS[c]) * B
                    pre = cbk[c % 2][:, o:o + B]
                    if t:
                        pe.wait_ge(h_hi, t)
                    for i in (2, 1, 0):
                        pe.matmul(pre, wh3[:, i, :], hhi[:, t % 2, :], start=False, stop=True, skip_group_check=True)
                    pe.wait_ge(h_lo, t + 1)
                    pe.matmul(pre, wh3[:, 1, :], hlo[:, t % 2, :], start=False, stop=True, skip_group_check=True)
                    pe.matmul(pre, wh3[:, 0, :], hlo[:, t % 2, :], start=False, stop=True,
                              skip_group_check=True).then_inc(gate_pre, 1)
                for key in parts["pe"][s]:
                    unit(key)

        @block.vector
        def _(dve):
            chain = [0]

            def link(ins):
                chain[0] += 1
                ins.then_inc(dve_link, 1)
                dve.wait_ge(dve_link, chain[0])

            tts = nc.vector.tensor_tensor
            tsc = nc.vector.tensor_scalar
            stt = nc.vector.scalar_tensor_tensor

            dve.wait_ge(in_small, 32)
            nc.vector.tensor_copy(ident[:], S("ident"))
            nc.vector.tensor_copy(sel[:].rearrange("p e m -> p (e m)"), x3[:, 0:E * P // T, :].rearrange("p b t -> p (b t)"))
            tsc(leak[:], S("alpha"), -1.0, 1.0, ALU.mult, ALU.add)
            dve.wait_ge(in_rec, 32)
            link(nc.vector.tensor_copy(wh3[:, 0, :], wh))
            link(tts(wr[:], wh, wh3[:, 0, :], ALU.subtract))
            link(nc.vector.tensor_copy(wh3[:, 1, :], wr[:]))
            link(tts(wr2[:], wr[:], wh3[:, 1, :], ALU.subtract))
            nc.vector.tensor_copy(wh3[:, 2, :], wr2[:])
            link(nc.vector.tensor_copy(b3[:, 0:1], S("b2")))
            link(tts(br[:, 0:1], S("b2"), b3[:, 0:1], ALU.subtract))
            link(nc.vector.tensor_copy(b3[:, 1:2], br[:, 0:1]))
            link(tts(br[:, 1:2], br[:, 0:1], b3[:, 1:2], ALU.subtract))
            nc.vector.tensor_copy(b3[:, 2:3], br[:, 1:2])
            link(nc.vector.tensor_copy(hhi[:, 0, :], hs[:, 0, :]))
            tts(hlo[:, 0, :], hs[:, 0, :], hhi[:, 0, :], ALU.subtract).then_inc(h_lo, 1)
            dve.wait_ge(cond_pe, 1)
            nc.vector.tensor_copy(tc[:].rearrange("p l e -> p (l e)"), hid[0][:, 0:2 * E])
            dve.wait_ge(cond_pe, 2)
            dve.wait_ge(in_att, 32)
            link(tts(fx[:], hid[1][:, 0:G * B].rearrange("p (g b) -> p g b", g=G),
                     A("ukb").rearrange("p (g o) -> p g o", o=1).broadcast_to([P, G, B]), ALU.add))
            link(tsc(ft[:], fx[:], A("sk"), None, ALU.mult))
            link(stt(fk[:], fx[:], A("mk"), ft[:], ALU.mult, ALU.add))
            for g in range(G):
                tts(kbd[:, g, :, :], fk[:, g, :].rearrange("p (b o) -> p b o", o=1).broadcast_to([P, B, H]),
                    A("hmk", g, H).rearrange("p (o h) -> p o h", o=1).broadcast_to([P, B, H]), ALU.mult)
            for g in range(G):
                tsc(sbq[:, g:g + 1], A("qb", g, 1), A("sq"), None, ALU.mult)
                tsc(sbk[:, g:g + 1], A("kb", g, 1), A("sk"), None, ALU.mult)
            tsc(vimg[:], hid[1][:, G * B:G * B + B], A("uvb"), None, ALU.add).then_inc(consts, 1)
            dve.wait_ge(consts, 1)

            def unit(key, half):
                kind = key[0]
                last = half != 0
                if ("pe", key) in nth:
                    dve.wait_ge(pe_done, nth["pe", key])
                if key in bank_of:
                    hk = hid[bank_of[key]]
                if kind not in ("GT", "SA", "M") and half != 1 and nth["dve", key] > 1:
                    dve.wait_ge(dve_done, nth["dve", key] - 1)
                if kind in HALVED:
                    n = 512 if kind == "O" else CHUNKS[key[1]] * B
                    w = slice(0, n) if half is None else slice(half * n // 2, (half + 1) * n // 2)
                if kind == "R":
                    _, c, l, r = key
                    k = CHUNKS[c] * B // P
                    a, b = 2 * r, min(2 * r + 2, k)
                    if c:
                        dve.wait_ge(act_done, nth["act", ("RT", c - 1, l)])
                    i = tts(lg[:, l, a:b, :], hk[:, a * E:b * E].rearrange("p (k e) -> p k e", e=E),
                            tc[:, l:l + 1, :].broadcast_to([P, b - a, E]), ALU.add)
                elif kind == "RS":
                    _, c, l = key
                    k = CHUNKS[c] * B // P
                    dve.wait_ge(act_done, nth["act", ("RT", c, l)])
                    link(tsc(sg[:, l, 0:k, :], th[:, l, 0:k, :], 0.5, 0.5, ALU.mult, ALU.add))
                    link(tts(sl[:, l, 0:k, :], sg[:, l, 0:k, :],
                             S(f"rb{l}").rearrange("p (o e) -> p o e", o=1).broadcast_to([P, k, E]), ALU.add))
                    for i in range(k):
                        m = nc.vector.max(mx8[:, l, i, :], sl[:, l, i, :])
                    link(m)
                    for i in range(k):
                        m = nc.vector.max_index(ix8[:, l, i, :], mx8[:, l, i, :], sl[:, l, i, :])
                    link(m)
                    i = nc.vector.tensor_copy(ixf[:, l, 0:k, :], ix8[:, l, 0:k, 0:2])
                elif kind == "RG":
                    _, c, l = key
                    k = CHUNKS[c] * B // P
                    dve.wait_ge(dve_done, nth["dve", ("RS", c, l)])
                    if c:
                        dve.wait_ge(pe_done, nth["pe", ("GT", c - 1, l)])
                    io = S("iota").rearrange("p (o e) -> p o e", o=1).broadcast_to([P, k, E])
                    wide = lambda a: a.rearrange("p (k o) -> p k o", o=1).broadcast_to([P, k, E])
                    tts(pick[:, 0:k, :], io, ixf[:, l, 0:k, 0:1].broadcast_to([P, k, E]), ALU.is_equal)
                    link(tts(pick2[:, 0:k, :], io, ixf[:, l, 0:k, 1:2].broadcast_to([P, k, E]), ALU.is_equal))
                    link(tts(pick[:, 0:k, :], pick[:, 0:k, :], pick2[:, 0:k, :], ALU.add))
                    link(tts(pick2[:, 0:k, :], pick[:, 0:k, :], sg[:, l, 0:k, :], ALU.mult))
                    link(nc.vector.tensor_reduce(den2[:, 0:k], pick2[:, 0:k, :], AX.X, ALU.add))
                    tsc(zer2[:, 0:k], den2[:, 0:k], EPS, 0.5 * GATE_SCALE[l], ALU.is_le, ALU.mult)
                    link(tsc(rcp2[:, 0:k], den2[:, 0:k], EPS, None, ALU.add))
                    link(nc.vector.reciprocal(rcp2[:, 0:k], rcp2[:, 0:k]))
                    link(stt(rcp2[:, 0:k], den2[:, 0:k], EPS, rcp2[:, 0:k], ALU.is_gt, ALU.mult))
                    tts(pick[:, 0:k, :], pick[:, 0:k, :], wide(zer2[:, 0:k]), ALU.mult)
                    link(tts(pick2[:, 0:k, :], pick2[:, 0:k, :], wide(rcp2[:, 0:k]), ALU.mult))
                    link(stt(gr[:, 0:k, :], pick2[:, 0:k, :], GATE_SCALE[l], pick[:, 0:k, :], ALU.mult, ALU.add))
                    link(nc.vector.tensor_copy(g3[:, l, 0:k, 0:E], gr[:, 0:k, :]))
                    link(tts(gr[:, 0:k, :], gr[:, 0:k, :], g3[:, l, 0:k, 0:E], ALU.subtract))
                    link(nc.vector.tensor_copy(g3[:, l, 0:k, E:2 * E], gr[:, 0:k, :]))
                    i = tts(g3[:, l, 0:k, 2 * E:3 * E], gr[:, 0:k, :], g3[:, l, 0:k, E:2 * E], ALU.subtract)
                elif kind == "GT":
                    _, c, l = key
                    if c and half != 1:
                        dve.wait_ge(pe_done, nth["pe", ("M", c - 1, l, E - 1)])
                    i = nc.vector.tensor_copy(gt[0:3 * E, l, w], hk[0:3 * E, w])
                elif kind == "SA":
                    dve.wait_ge(act_done, nth["act", key])
                    j = sa_key.index(key)
                    if j:
                        dve.wait_ge(dve_done, nth["dve", ("SB",) + sa_key[j - 1][1:]])
                    i = stt(sgl[:, w], sth[:, w], 1.0, hk[:, w], ALU.add, ALU.mult)
                elif kind == "SB":
                    _, c, l, j = key
                    dve.wait_ge(dve_done, nth["dve", ("SA", c, l, j)])
                    hg_free(key)
                    i = stt(hg[:, hg_of[key] % NHG, w], hk[:, w], SHARED_SCALE[l], sgl[:, w], ALU.mult, ALU.mult)
                elif kind == "M":
                    _, c, l, e = key
                    dve.wait_ge(act_done, nth["act", ("E", c, l, e)])
                    hg_free(key)
                    i = tts(hg[:, hg_of[key] % NHG, w], hb[:, hb_of["E", c, l, e] % NHB, w], hk[:, w], ALU.mult)
                elif kind == "YE":
                    _, c, l = key
                    a = STARTS[c] * B
                    dve.wait_ge(pe_done, nth["pe", last_y[c, l]])
                    ww = slice(a + w.start, a + w.stop)
                    i = tts(x[:, ww], x[:, ww], ybk[l][:, w], ALU.add)
                elif kind in ("K", "Q"):
                    _, t, g, h = key
                    t0 = t * QT + 64 * h
                    i2 = kq_order[key] % 2
                    dve.wait_ge(act_done, nth["act", key])
                    xv = xs[:, i2, :].rearrange("p (b t) -> p b t", b=B)
                    tv = tt[:, i2, :].rearrange("p (b t) -> p b t", b=B)
                    if kind == "K":
                        i = stt(kp[:, g, :, t0:t0 + 64], xv, A("mk"), tv, ALU.mult, ALU.add)
                    else:
                        if t:
                            dve.wait_ge(pe_done, nth["pe", ("S", t - 1, B - 1, G - 1, t - 1)])
                        q0 = 64 * h
                        link(stt(fq[:, g, :, q0:q0 + 64], xv, A("mq"), tv, ALU.mult, ALU.add))
                        for j in range(J):
                            i = tsc(qz[:, g, :, j, q0:q0 + 64], fq[:, g, :, q0:q0 + 64], hm[:, j:j + 1], None, ALU.mult)
                elif kind == "V":
                    _, t, q = key
                    i = tts(v[:, 4 * q:4 * q + 4, t, :], hk[:].rearrange("p (b d) -> p b d", b=4),
                            A("vb").rearrange("p (o d) -> p o d", o=1).broadcast_to([P, 4, P]), ALU.add)
                elif kind == "A":
                    _, t, b, a = key
                    nh = J if t == 0 else 2
                    i = nc.vector.tensor_reduce(wm[:, b, a * nh:(a + 1) * nh],
                                                hk[:].rearrange("p (h k) -> p h k", h=nh), AX.X, ALU.max)
                elif kind == "MX":
                    _, t, b = key
                    dve.wait_ge(dve_done, nth["dve", ("A", t, b, (4 if t == 0 else 8) - 1)])
                    if t:
                        dve.wait_ge(pe_done, nth["pe", ("S", t - 1, b, G - 1, t - 1)])
                        dve.wait_ge(lm_ready, (t - 1) * B + b + 1)
                    link(tts(mm[:, b, :], hk[:, 0:H], wm[:, b, :], ALU.max))
                    i = tsc(mneg[:, b, :], mm[:, b, :], -1.0, None, ALU.mult)
                elif kind == "ID":
                    _, t, q = key
                    d = hk[:].rearrange("p (b q) -> p b q", b=4)
                    if t:
                        dve.wait_ge(dve_done, nth["dve", ("X", t - 1, B - 1)])
                    nc.vector.tensor_copy(dimg[:, 4 * q:4 * q + 4, :], d)
                    i = tts(nimg[:, 4 * q:4 * q + 4, :], d,
                            vimg[:, 4 * q:4 * q + 4].rearrange("p (b o) -> p b o", o=1).broadcast_to([P, 4, QT]), ALU.mult)
                elif kind == "X":
                    _, t, b = key
                    dve.wait_ge(pe_done, nth["pe", ("AV", t, b, G - 1, t)])
                    dve.wait_ge(dve_done, nth["dve", ("ID", t, b // 4)])
                    if t and b % 4 == 0:
                        dve.wait_ge(pe_done, nth["pe", ("O", t - 1, b // 4)])
                    for j in range(J):
                        w = slice(j * QT, j * QT + QT)
                        nsrc = nimg[:, b, :] if j == 0 else num[:, (j - 1) % 2, :]
                        dsrc = dimg[:, b, :] if j == 0 else den[:, (j - 1) % 2, :]
                        stt(num[:, j % 2, :], ybk[0][:, w], hx[:, j:j + 1], nsrc, ALU.mult, ALU.add)
                        link(stt(den[:, j % 2, :], ybk[1][:, w], hx[:, j:j + 1], dsrc, ALU.mult, ALU.add))
                    link(nc.vector.reciprocal(den[:, 0, :], den[:, 1, :]))
                    i = tts(on[:, b, :], num[:, 1, :], den[:, 0, :], ALU.mult)
                elif kind == "O":
                    _, t, q = key
                    h0, h1 = (0, 4) if half is None else (2 * half, 2 * half + 2)
                    bb = slice(4 * q + h0, 4 * q + h1)
                    if t:
                        dve.wait_ge(stored[q], 16 * t)
                    i = stt(ob[:, q, h0:h1, :], hk[:, w].rearrange("p (b q) -> p b q", q=QT), A("pb"),
                            x3[:, bb, t * QT:(t + 1) * QT], ALU.add, ALU.add)
                if last:
                    i.then_inc(dve_done, 1)

            def hg_free(key):
                i = hg_of[key]
                if i >= NHG:
                    k = hg_key[i - NHG]
                    y = ("Y", k[1], k[2], "e" if k[0] == "M" else "s", k[3])
                    dve.wait_ge(pe_done, nth["pe", y])

            for s in range(n_slots):
                t = steps.get(s)
                units = parts["dve"][s]
                if t is None:
                    for key in units:
                        unit(key, None)
                    continue
                if t:
                    dve.wait_ge(h_hi, t)
                    dve.wait_ge(h_full, t)
                    tts(hlo[:, t % 2, :], hs[:, t, :], hhi[:, t % 2, :], ALU.subtract).then_inc(h_lo, 1)
                dve.wait_ge(z_ready, chunk_of(t) + 1)
                stt(d1[:, t % 2, :, 1], hs[:, t, :], leak[:], d0[:, t % ZR, :, 1], ALU.mult, ALU.add).then_inc(decay, 1)
                first = [k for i, k in enumerate(units) if i < len(units) // 2]
                rest = units[len(units) // 2:]
                cut = len(units) % 2 == 1 and rest[0][0] in HALVED
                for key in first:
                    unit(key, None)
                if cut:
                    unit(rest[0], 0)
                dve.wait_ge(decay, t + 1)
                dve.wait_ge(gate_th, t + 1)
                nc.vector.tensor_tensor_scan(vps, d0[:, t % ZR].rearrange("p b o -> p (b o)"),
                                             d1[:, t % 2].rearrange("p b o -> p (b o)"), 0.0, ALU.mult,
                                             ALU.add).then_inc(blend, 1)
                if cut:
                    unit(rest[0], 1)
                    rest = rest[1:]
                for key in rest:
                    unit(key, None)


HALVED = ("GT", "SA", "SB", "M", "YE", "O")



def padded(a):
    lead = a.shape[:-2]
    out = np.zeros(lead + (G, J, HP), a.dtype)
    for r in range(3):
        out[..., r * HD:(r + 1) * HD] = a.reshape(lead + (G, J, HD))
    return out.reshape(lead + (G * J * HP,))


def constants():
    p = np.arange(P)
    one = lambda cond: cond.astype(np.float32)
    sel = one(np.arange(E)[None, :, None] == np.where(p < 3 * E, p % E, -1)[:, None, None]) * np.ones((1, 1, P), np.float32)
    lo_q, lo_k = one((p % HP) // HD == 2), one((p % HP) // HD == 1)
    h = np.arange(H)
    hmk = np.stack([one(h[None, :] == (J * g + p // HP)[:, None]) for g in range(G)], 1)
    return {
        "ident": np.eye(P, dtype=np.float32), "iota": np.tile(np.arange(E, dtype=np.float32), (P, 1)),
        "sel": sel.reshape(P, E * P),
        "causal": one(p[None, :] > p[:, None]) * np.float32(NEG),
        "hm": one(p[:, None] // HP == np.arange(J)), "hx": one((p[:, None] % HP) // HD == np.arange(J)),
        "sq": (1 - 2 * lo_q)[:, None], "mq": lo_q[:, None], "sk": (1 - 2 * lo_k)[:, None], "mk": lo_k[:, None],
        "hmk": hmk.reshape(P, G * H), "hexp": one(p[:, None] == p[None, :] // HD),
    }


def kernel(**inputs):
    import concourse.bacc as bacc
    from concourse.bass_utils import run_bass_kernel_spmd

    a = {k: np.asarray(v) for k, v in inputs.items()}
    con = constants()
    rows = lambda w: np.ascontiguousarray(np.broadcast_to(w, (P,) + w.shape)).reshape(P, -1)
    wide = lambda w: np.ascontiguousarray(w).reshape(P, -1)
    tiles = lambda w: wide(w.transpose(1, 0, 2))

    def pack(layout, total, blocks):
        out = np.zeros((P, total), np.float32)
        for name, (at, width) in layout.items():
            out[:, at:at + width] = (blocks if name in blocks else con)[name]
        return out

    L0, L1, L2, L3 = (lambda n, l=l: a[f"L{l}_cond_{n}"] for l in range(4))
    small = pack(SMALL | {"sel": (SEL_AT, E * P)}, N_SMALL + E * P, {
        "cond": np.tile(a["cond_1024"].T, (1, P // B)), "wrx0": L0("router_W")[:D], "wrt0": L0("router_W")[D:],
        "wrx1": L1("W_router")[:, :D].T, "wrt1": L1("W_router")[:, D:].T,
        "rb0": rows(L0("router_bias")), "rb1": rows(L1("router_bias")),
        "alpha": L2("alpha")[:, None], "b2": L2("b")[:, None]})
    ff0 = pack(FF0, N_FF0, {"w1": L0("w1"), "w3": L0("w3"), "w2": tiles(L0("w2").reshape(2, P, D)),
                            "e1": tiles(L0("W1e")), "e2": tiles(L0("W2e"))})
    ff1 = pack(FF1, N_FF1, {"w1": wide(L1("s_w1").transpose(2, 0, 1)), "w3": wide(L1("s_w3").transpose(2, 0, 1)),
                            "w2": tiles(L1("s_w2").transpose(0, 2, 1).reshape(4, P, D)),
                            "e1": tiles(L1("r_w1").transpose(0, 2, 1)), "e2": tiles(L1("r_w2").transpose(0, 2, 1))})
    rec = pack({"wh": (0, P), "wz": (P, P)}, N_REC, {"wh": L2("W")[:, :D].T, "wz": L2("W")[:, D:].T})
    w, wb = L3("c_attn_w"), L3("c_attn_b")
    col = lambda v: padded(v.reshape(H, HD)).reshape(G, P).T
    att = pack(ATT, N_ATT, {
        "wq": padded(w[:, :D].reshape(D, H, HD)), "wk": padded(w[:, D:2 * D].reshape(D, H, HD)), "wv": w[:, 2 * D:],
        "wp": L3("c_proj_w"), "uk": padded(L3("uk_w").T.reshape(D, H, HD)), "uv": L3("uv_w").T,
        "qb": col(wb[:D]), "kb": col(wb[D:2 * D]), "ukb": col(L3("uk_b")), "pb": L3("c_proj_b")[:, None],
        "uvb": L3("uv_b")[:, None], "vb": rows(wb[2 * D:]),
        "maskt": wide(a["mask_Bx1x1xS_ff0"].reshape(B, 2, P).transpose(2, 0, 1))})
    arrays = {"x_in": wide(a["x"].transpose(2, 1, 0)), "small_in": small, "ff0_in": ff0, "ff1_in": ff1, "rec_in": rec,
              "att_in": att, "maskr_in": rows(a["mask_Bx1x1xS_ff0"].reshape(B * T))}

    nc = bacc.Bacc("TRN2", target_bir_lowering=False, num_devices=1)
    args = [nc.dram_tensor(n, v.shape, mybir.dt.from_np(v.dtype), kind="ExternalInput").ap() for n, v in arrays.items()]
    out = nc.dram_tensor("out_dram", (P, B, T), F32, kind="ExternalOutput").ap()
    build(nc, *args, out)
    r = run_bass_kernel_spmd(nc, [arrays], core_ids=[0])
    return np.ascontiguousarray(r.results[0]["out_dram"].transpose(1, 2, 0))
```

```python
from contextlib import ExitStack

import numpy as np
import concourse.bass as bass
from concourse import mybir

F32 = mybir.dt.float32
BF16 = mybir.dt.bfloat16
F16 = mybir.dt.float16
U32 = mybir.dt.uint32
ACT = mybir.ActivationFunctionType
ALU = mybir.AluOpType
AX = mybir.AxisListType

P = 128
B, T, D = 8, 256, 128
E = 8
H, HD = 16, 8
G, J = 4, 4
HP = 32
SHARED = (2, 4)
SHARED_SCALE = (0.5 / 3.0, 0.5 / 8.0)
GATE_SCALE = (1.0 / 3.0, 1.0 / 4.0)
CHUNKS = (16, 16, 32, 32, 32, 32, 32, 32, 32)
STARTS = tuple(sum(CHUNKS[:i]) for i in range(len(CHUNKS)))
NC = len(CHUNKS)
QT = 128
NEG = -1.0e5
SC = float(1.0 / np.sqrt(HD))
EPS = 1e-9
XP = 32
ZR = 128
NHT, NHB, NHG = 3, 8, 4
AHEAD = (4, 2)
NPT = 6
CAPS = {"before": (1000, 1000, 1000), "in": (1100, 900, 1100), "behind": (1800, 1050, 1500)}


def columns(*parts):
    at, out = 0, {}
    for *name, width in parts:
        out[name[0] if len(name) == 1 else tuple(name)] = (at, width)
        at += width
    return out, at


SMALL, N_SMALL = columns(("cond", P), ("wrx0", E), ("wrt0", E), ("wrx1", E), ("wrt1", E), ("rb0", E), ("rb1", E),
                         ("alpha", 1), ("b2", 1), ("ident", P), ("iota", E), ("selc", E))

UP, N_UP = columns(("w1", 0, 256), ("w3", 0, 256), ("e1", 0, E * P), ("w1", 1, 512), ("w3", 1, 512), ("e1", 1, E * P))
DOWN, N_DOWN = columns(("w2", 0, 256), ("e2", 0, E * P), ("w2", 1, 512), ("e2", 1, E * P))
PIECES = ((0, 0, 512), (0, 512, 1536), (1, 1536, 2560), (1, 2560, 3584))
WS = 256.0
GS = 256.0
REC, N_REC = columns(("wh", P), ("wz", P))
ATT, N_ATT = columns(("wq", G * P), ("wk", G * P), ("wv", P), ("wp", P), ("uk", G * P), ("uv", P), ("qb", G), ("kb", G),
                     ("ukb", G), ("pb", 1), ("uvb", 1), ("vb", P), ("causal", P), ("hm", J), ("hx", J), ("sq", 1), ("mq", 1),
                     ("sk", 1), ("mk", 1), ("hmk", G * H), ("hexp", P), ("maskt", B * 2))


def plan():
    units = []

    def add(key, pe, act, dve, bank, *needs):
        units.append((key, pe, act, dve, bank, needs))

    mm4 = lambda n: 4 * n / 2.4
    mm3 = lambda n: 3 * n / 2.4
    for i, (l, a, b) in enumerate(PIECES):
        add(("W", l, i), 0, 200 + (b - a) * .9, 60 + (b - a) * 1.05, False)
    for c in range(NC):
        n = CHUNKS[c] * B
        k = n // P
        for l in range(2):
            if l == 0:
                add(("XS", c), 0, 0, 0, False, *[(u, "pe", "pool") for u in x_users(c - 2, 0)])
            x = [(("YE", c, 0), "dve", "pe")] if l else [(("XS", c), "pool", "pe")]
            if l == 0 and c >= 2:
                x.append((("YE", c - 2, 1), "dve", "dve"))
            w = [(("W", l, 2 * l), "dve", "pe")] if c == 0 else []
            we = [(("W", l, 2 * l + 1), "dve", "pe")] if c == 0 else []
            half = [(0, min(2, k))] + ([(2, k)] if k > 2 else [])
            for r, (a, b) in enumerate(half):
                add(("R", c, l, r), 190 * (b - a), 0, 130, True, *x, *([(("RG", c - 1, l), "pool", "dve")] if c else []))
            add(("RT", c, l), 0, 220, 0, False, (("R", c, l, len(half) - 1), "dve", "act"))
            add(("RS", c, l), 0, 0, 400 + 80 * (1 + 2 * k), False, (("RT", c, l), "act", "dve"))
            add(("RD", c, l), 0, 0, 800, False, (("RS", c, l), "dve", "dve"))
            add(("RC", c, l), 0, 0, 700, False, (("RD", c, l), "dve", "dve"))
            add(("RG", c, l), 0, 0, 0, False, (("RC", c, l), "dve", "pool"))
            add(("GT", c, l), 60 * k, 0, 60 + n, True, (("RG", c, l), "pool", "pe"),
                *([(("M", c - 1, l, E * CHUNKS[c - 1] * B // 512 - 1), "pe", "pe")] if c else []))
            f = 512 // n
            fs = min(f, SHARED[l])
            wide = 60 + fs * n * .84, 100 + fs * n * 1.05
            for i in range(SHARED[l] // fs):
                add(("SA", c, l, i), fs * mm3(n), *wide, True, *x, *w)
                add(("SB", c, l, i), fs * mm3(n), 0, wide[1], True, (("SA", c, l, i), "dve", "dve"), *x)
                add(("Y", c, l, "s", i), fs * mm4(n), 0, 0, False, (("SB", c, l, i), "dve", "pe"),
                    *([(("YE", c - 1, l), "dve", "pe")] if c else []))
            for i in range(E // f):
                add(("E", c, l, i), f * mm3(n), 490, 0, True, *x, *we)
            for i in range(E // f):
                add(("M", c, l, i), 213, 0, 640, True, (("E", c, l, i), "act", "dve"), (("GT", c, l), "dve", "pe"))
                add(("Y", c, l, "e", i), f * mm4(n), 0, 0, False, (("M", c, l, i), "dve", "pe"),
                    *([(("YE", c - 1, l), "dve", "pe")] if c else []))
            last = [("Y", c, l, "e", i) for i in range(E // f)] + [("Y", c, l, "s", i) for i in range(SHARED[l] // fs)]
            add(("YE", c, l), 0, 0, (100 + n * 1.05) * (1 if l else 2.6), False, *[(y, "pe", "dve") for y in last],
                *([(u, "pe", "dve") for u in x_users(c - 1, 1)] if l == 0 else []))
        add(("C", c), mm4(n) + 2 * n / 2.4, 0, 0, False, (("YE", c, 1), "dve", "pe"))
        if c == 2:
            add(("IK",), 600, 0, 2500, True, (("C", 1), "pe", "pe"))
    for t in range(T // QT):
        kq = (("STEP", QT * (t + 1) - 1), "pool", "pe")
        for v in range(2):
            add(("V", t, v), 880, 0, 640, True, kq)
        for h in range(2):
            for g in range(G):
                add(("K", t, g, h), 860, 1240, 660, True, (("STEP", QT * t + 64 * h + 63), "pool", "pe"), (("IK",), "dve", "act"))
        for h in range(2):
            for g in range(G):
                add(("Q", t, g, h), 860, 1240, 660, True, (("STEP", QT * t + 64 * h + 63), "pool", "pe"), (("IK",), "dve", "act"),
                    *([(("S", t - 1, B - 1, G - 1, t - 1), "pe", "dve")] if t else []))
                for i in range(2):
                    add(("QZ", t, g, h, i), 0, 0, 530, False, (("Q", t, g, h), "dve", "dve"))
        n_a = 4 if t == 0 else 8

        def maxima(b):
            for a in range(n_a):
                add(("A", t, b, a), 430, 0, 660, True, (("K", t, G - 1, 1), "dve", "pe"), (("QZ", t, G - 1, 1, 1), "dve", "pe"))
            add(("MX", t, b), 220, 0, 320, True, (("A", t, b, n_a - 1), "dve", "dve"), (("Q", t, G - 1, 1), "dve", "pe"))

        def image(q):
            add(("IM", t, q), 550, 300, 0, True, *[(("MX", t, b), "dve", "pe") for b in (2 * q, 2 * q + 1)])
            add(("ID", t, q), 430, 0, 650, True, (("IM", t, q), "act", "pe"))

        for b in range(AHEAD[t]):
            maxima(b)
            if b % 2:
                image(b // 2)
        for b in range(B):
            for g in range(G):
                for kb in range(t + 1):
                    add(("S", t, b, g, kb), 440, 500, 0, True, (("MX", t, b), "dve", "pe"))
                    add(("AV", t, b, g, kb), 430, 0, 0, False, (("S", t, b, g, kb), "act", "pe"),
                        *([(("X", t, b - 1 - t, 1), "dve", "pe")] if b > t else [(("X", t - 1, B - 1, 1), "dve", "pe")] if t else []))
            if b + AHEAD[t] < B:
                maxima(b + AHEAD[t])
                if (b + AHEAD[t]) % 2:
                    image((b + AHEAD[t]) // 2)
            add(("X", t, b, 0), 0, 0, 1050, False, (("AV", t, b, G - 1, t), "pe", "dve"), (("ID", t, b // 2), "dve", "dve"))
            add(("X", t, b, 1), 0, 0, 1050, False, (("X", t, b, 0), "dve", "dve"))
            add(("X", t, b, 2), 0, 0, 1100, False, (("X", t, b, 1), "dve", "dve"))
            if b % 4 == 3:
                q = b // 4
                add(("O", t, q), 860, 0, 700, True, *[(("X", t, b, 2), "dve", "pe") for b in range(4 * q, 4 * q + 4)])

    info = {u[0]: u for u in units}
    later = {k: {"pe": 0, "act": 1, "dve": 2 if u[2] else 1, "pool": 1} for k, u in info.items()}
    apart = lambda of, by: 0 if of == by else 3 if of == "pool" else 1
    slot_of, step_slot, order = {}, {}, []
    bank_of, before, user, last_use = {}, {}, [None] * (NHT + 1), [0] * (NHT + 1)
    hg_users, hb_users = [], []
    used = {eng: [0] * 1100 for eng in ("pe", "act", "dve")}
    left = list(units)
    s = step = 0
    while left or step < T:
        if step < T:
            c = chunk_of(step)
            if ("C", c) in slot_of and slot_of["C", c] < s:
                step_slot[step] = s
                step += 1
        phase = ("before" if not step or step < T and step_slot[step - 1] != s else
                 "behind" if step == T and step_slot[T - 1] + 1 < s else "in")
        caps = dict(zip(("pe", "act", "dve"), CAPS[phase]))
        passed = set()
        for u in list(left):
            key, up, ua, ud, bank, needs = u
            family = key[:3] if key[0] in ("R", "SA", "SB", "E", "M", "GT") else key[:2]
            if key[0] != "Y" and family in passed:
                continue
            passed.add(family)
            lat = later[key]
            if any(cost and used[eng][s + lat[eng]] and used[eng][s + lat[eng]] + cost > caps[eng]
                   for eng, cost in (("pe", up), ("act", ua), ("dve", ud))):
                continue
            ok = True
            for k, of, by in needs:
                if k[0] == "STEP":
                    ok = k[1] in step_slot and step_slot[k[1]] + 3 <= s
                elif k not in slot_of or slot_of[k] + later[k][of] + apart(of, by) > s + lat[by]:
                    ok = False
                if not ok:
                    break
            if ok and key[0] == "C" and key[1] >= 2:
                end = STARTS[key[1] - 1] - 1
                ok = end in step_slot and step_slot[end] + 2 <= s
            if ok and bank:
                at = min(range(NHT + (step == T and phase == "behind")), key=lambda i: last_use[i])
                ok = last_use[at] <= s
            if ok and key[0] in ("M", "SB") and len(hg_users) >= NHG:
                k = hg_users[-NHG]
                y = ("Y", k[1], k[2], "e", k[3]) if k[0] == "M" else ("Y", k[1], k[2], "s", k[3])
                ok = y in slot_of and slot_of[y] + 1 <= s + lat["dve"]
            if ok and key[0] == "E" and len(hb_users) >= NHB:
                k = hb_users[-NHB]
                k = ("M",) + k[1:]
                ok = k in slot_of and slot_of[k] + later[k]["dve"] <= s
            if ok and key[0] == "SA":
                ok = not any(k[0] == "SA" and ("SB",) + k[1:] not in slot_of for k in slot_of)
            if ok and key[0] == "S" and key[4] == key[1]:
                _, t, b, g, _ = key
                ok = slot_of["MX", t, b] + 5 <= s
                if ok and b >= 2:
                    ok = slot_of["S", t, b - 2, G - 1, t] + 4 <= s
            if ok and key[0] in ("S", "IM"):
                ok = ("YE", NC - 1, 1) in slot_of and slot_of["YE", NC - 1, 1] + 1 < s
            if ok and key[0] == "AV" and key[1] and key[2] % 2:
                ok = step == T and phase == "behind"
            if ok and key[0] == "S":
                ok = sum(k[0] == "S" for k in slot_of) - sum(k[0] == "AV" for k in slot_of) < NPT
            if not ok:
                continue
            passed.discard(family)
            slot_of[key] = s
            order.append((s, key))
            left.remove(u)
            for eng, cost in (("pe", up), ("act", ua), ("dve", ud)):
                used[eng][s + lat[eng]] += cost
            if bank:
                bank_of[key], before[key] = at, user[at]
                user[at], last_use[at] = key, s + lat["act" if key[0] in ("E", "IM", "S") else "dve"] + 1
            if key[0] in ("M", "SB"):
                hg_users.append(key)
            if key[0] == "E":
                hb_users.append(key)
        s += 1
        assert s < 1000, (left[:3], hg_users[-5:], hb_users[-9:], step)
    hg_of = {k: i for i, k in enumerate(hg_users)}
    hb_of = {k: i for i, k in enumerate(hb_users)}
    n_slots = s + 3
    parts = {"pe": [[] for _ in range(n_slots)], "act": [[] for _ in range(n_slots)], "dve": [[] for _ in range(n_slots)]}
    for at, key in order:
        for eng, cost in (("pe", 1), ("act", 2), ("dve", 3)):
            if info[key][cost]:
                parts[eng][at + later[key][eng]].append(key)
    nth = {}
    for eng in parts:
        n = 0
        for units_of_slot in parts[eng]:
            for key in units_of_slot:
                n += 1
                nth[eng, key] = n
    steps = {at: t for t, at in step_slot.items()}
    pool = [(slot_of["XS", c], "XS", c) for c in range(NC)]
    pool += [(slot_of[k] + 1, *k) for k in slot_of if k[0] == "RG"]
    pool += [(slot_of["YE", c, 1] + 2, "Z", c) for c in range(NC)]
    pool += [(slot_of["IK",] + 1 + 8 * i, "MB", i) for i in range(4)]
    pool += [(step_slot[t0 + XP - 1] + 1, "X3", t0) for t0 in range(0, T, XP)]
    pool += [(max([slot_of["MX", t, b] + 2] + [slot_of["S", t2, b2, G - 1, t2] for t2, b2 in [divmod(t * B + b - 2, B)]
                                               if t or b >= 2]), "LM", t, b) for t in range(T // QT) for b in range(B)]
    parts["pool"] = [u[1:] for u in sorted(pool)]
    for key in parts["pool"]:
        if key[0] == "RG":
            nth["pool", key] = sum(k[0] == "pool" for k in nth) + 1
    return parts, nth, steps, bank_of, before, hg_of, hb_of, n_slots


def x_users(c, l):
    if c < 0:
        return []
    n = CHUNKS[c] * B
    f = 512 // n
    return ([("R", c, l, r) for r in range((n // P + 1) // 2)] + [("E", c, l, i) for i in range(E // f)] +
            [(s, c, l, i) for s in ("SA", "SB") for i in range(SHARED[l] // min(f, SHARED[l]))])


def chunk_of(t):
    return max(i for i in range(NC) if STARTS[i] <= t)


def build(nc, x_in, small_in, up_in, down_in, rec_in, att_in, maskr_in, out):
    parts, nth, steps, bank_of, before, hg_of, hb_of, n_slots = plan()

    with ExitStack() as ctx:
        def sb(name, shape, dt=F32):
            return ctx.enter_context(nc.sbuf_tensor(name, shape, dt))

        def ps(name):
            return ctx.enter_context(nc.psum_tensor(name, [P, 512], F32))

        def sem(name):
            return ctx.enter_context(nc.semaphore(name))

        x = sb("x", [P, T * B])
        small = sb("small", [P, N_SMALL])
        up = sb("up", [P, 2, N_UP], F16)
        down = sb("down", [P, N_DOWN])
        xsp0 = sb("xsp0", [P, 2, 2, 256], F16)
        xsp1 = sb("xsp1", [P, 2, 256], F16)
        wrx = sb("wrx", [P, 2, 2, E], F16)
        rec = sb("rec", [P, N_REC])
        att = sb("att", [P, N_ATT])
        ident = sb("ident", [P, P], BF16)
        sel = sb("sel", [P, E, P], F16)
        ones = sb("ones", [P, HP])
        tc = sb("tc", [P, 2, E])
        lg = sb("lg", [P, 2, 4, E])
        th = sb("th", [P, 2, 4, E])
        sg = sb("sg", [P, 2, 4, E])
        sl = sb("sl", [P, 2, 4, E])
        mx8 = sb("mx8", [P, 2, 4, 8])
        ix8 = sb("ix8", [P, 2, 4, 8], U32)
        rb5 = sb("rb5", [P, 2, E])
        pick = sb("pick", [P, 2, 4, E])
        pick2 = sb("pick2", [P, 2, 4, E])
        den2 = sb("den2", [P, 2, 4])
        rcp2 = sb("rcp2", [P, 2, 4])
        zer2 = sb("zer2", [P, 2, 4])
        gr = sb("gr", [P, 4, E])
        g2 = sb("g2", [P, 2, 4, 2 * E], F16)
        gt = sb("gt", [P, 2, 512], F16)
        id16 = sb("id16", [P, P], F16)
        hb = sb("hb", [P, NHB, 512])
        hg = sb("hg", [P, NHG, 512])
        silu = sb("silu", [P, 2, 512])
        sth, sgl = silu[:, 0], silu[:, 1]
        wh3 = sb("wh3", [P, 3, P], BF16)
        b2 = sb("b2", [P, 2], F16)
        leak = sb("leak", [P, 1])
        d0 = sb("d0", [P, ZR, B, 2])
        d1 = sb("d1", [P, 2, B, 2])
        hs = sb("hs", [P, T + 1, B])
        hhi = sb("hhi", [P, 2, B], F16)
        hlo = sb("hlo", [P, 2, B], F16)
        x3 = sb("x3", [P, B, T])
        kp = sb("kp", [P, G, B, T], F16)
        maskr = kp[:].rearrange("p g b t -> p (g b t)").bitcast(F32).rearrange("p (x b t) -> p x b t", x=2, b=B)[:, 0]
        fq = sb("fq", [P, G, B, QT], F16)
        qz = sb("qz", [P, G, B, J, QT], F16)
        xs = sb("xs", [P, 2, 512])
        tt = sb("tt", [P, 2, 512], F16)
        fk = sb("fk", [P, G, B], F16)
        fx = sb("fx", [P, G, B])
        ft = sb("ft", [P, G, B], F16)
        kbd = sb("kbd", [P, G, B, H], F16)
        vimg = sb("vimg", [P, B])
        v = sb("v", [P, B, 2, P])
        sbq = sb("sbq", [P, G])
        sbk = sb("sbk", [P, G])
        mb = sb("mb", [P, B, 3, QT], BF16)
        cz = sb("cz", [P, P], BF16)
        wm = sb("wm", [P, B, H])
        mm = sb("mm", [P, B, H])
        mneg = sb("mneg", [P, B, H], BF16)
        lm = sb("lm", [P, 2, H, QT], BF16)
        eimg = sb("eimg", [P, 2 * QT])
        pt = hb[:, 0:NPT, :]
        dimg = hg[:, 2:4, :].rearrange("p a (b q) -> p (a b) q", q=QT)
        nimg = hb[:, 6:8, :].rearrange("p a (b q) -> p (a b) q", q=QT)
        on = hg[:, 0:2, :].rearrange("p a (b q) -> p (a b) q", q=QT)
        num = sb("num", [P, 2, QT])
        den = sb("den", [P, 2, QT])
        wr, wr2 = num[:, 0], den[:, 0]
        ob = silu[:].rearrange("p a (b q) -> p a b q", b=4)
        raw = qz[:].rearrange("p g b j q -> p (g b j q)").bitcast(F32)

        ybk = [ps("ybk0"), ps("ybk1")]
        cbk = [ps("cbk0"), ps("cbk1")]
        vbk = ps("vbk")
        hid = [ps(f"hid{i}") for i in range(NHT)] + [vbk]
        vps = vbk[:, 0:2 * B]

        in_x = [sem(f"in_x{c}") for c in range(NC)]
        in_up = [sem(f"in_up{i}") for i in range(len(PIECES))]
        in_down = [sem(f"in_down{l}") for l in range(2)]
        in_small, in_rec, in_att = (sem(f"in_{n}") for n in ("small", "rec", "att"))
        pe_done = sem("pe_done")
        act_done = sem("act_done")
        dve_done = sem("dve_done")
        dve_link = sem("dve_link")
        act_link = sem("act_link")
        masks = sem("masks")
        pool_set = sem("pool_set")
        x_hi = sem("x_hi")
        x_split = sem("x_split")
        gates_made = sem("gates_made")
        pool_link = sem("pool_link")
        z_ready = sem("z_ready")
        x3_ready = sem("x3_ready")
        consts = sem("consts")
        cond_pe = sem("cond_pe")
        gate_pre = sem("gate_pre")
        gate_th = sem("gate_th")
        decay = sem("decay")
        blend = sem("blend")
        h_hi = sem("h_hi")
        h_full = sem("h_full")
        h_lo = sem("h_lo")
        maxes = sem("maxes")
        lm_ready = sem("lm_ready")
        stored = [sem("stored0"), sem("stored1")]

        def S(name):
            a, n = SMALL[name]
            return small[:, a:a + n]

        def D(l, name, i):
            a, _ = DOWN[name, l]
            return down[:, a + i * P:a + i * P + P]

        def x_part(c, l, part, cols):
            return xsp1[:, part, cols] if l else xsp0[:, c % 2, part, cols]

        def A(name, i=None, w=P):
            a, n = ATT[name]
            return att[:, a:a + n] if i is None else att[:, a + i * w:a + i * w + w]

        wh = rec[:, 0:P]
        wz = rec[:, P:2 * P]
        hm, hx = A("hm"), A("hx")
        first_y, last_y = {}, {}
        for slot in parts["pe"]:
            for key in slot:
                if key[0] == "Y":
                    first_y.setdefault(key[1:3], key)
                    last_y[key[1:3]] = key
        order_of = lambda kinds, eng: [k for slot in parts[eng] for k in slot if k[0] in kinds]
        hg_key = sorted(hg_of, key=hg_of.get)
        hb_key = sorted(hb_of, key=hb_of.get)
        kq_key, s_key, sa_key = order_of(("K", "Q"), "act"), order_of(("S",), "act"), order_of(("SA",), "act")
        kq_order = {k: i for i, k in enumerate(kq_key)}
        s_order = {k: i for i, k in enumerate(s_key)}

        def cols(c):
            return slice(STARTS[c] * B, (STARTS[c] + CHUNKS[c]) * B)

        block = ctx.enter_context(nc.Block())

        @block.sync
        def _(sp):
            sp.dma_start(small[:], small_in).then_inc(in_small, 16)
            d1_at = DOWN["w2", 1][0]
            for i in (0, 1):
                sp.dma_start(raw[:, PIECES[i][1]:PIECES[i][2]], up_in[:, PIECES[i][1]:PIECES[i][2]]).then_inc(in_up[i], 16)
            sp.dma_start(down[:, 0:d1_at], down_in[:, 0:d1_at]).then_inc(in_down[0], 16)
            sp.dma_start(x[:, cols(1)], x_in[:, cols(1)]).then_inc(in_x[1], 16)
            for i in (2, 3):
                sp.dma_start(raw[:, PIECES[i][1]:PIECES[i][2]], up_in[:, PIECES[i][1]:PIECES[i][2]]).then_inc(in_up[i], 16)
            sp.dma_start(down[:, d1_at:], down_in[:, d1_at:]).then_inc(in_down[1], 16)
            for c in range(2, NC):
                sp.dma_start(x[:, cols(c)], x_in[:, cols(c)]).then_inc(in_x[c], 16)
            sp.dma_start(att[:], att_in).then_inc(in_att, 16)
            sp.dma_start(maskr.rearrange("p b t -> p (b t)"), maskr_in).then_inc(in_att, 16)
            for t in range(T // QT):
                for q in range(2):
                    sp.wait_ge(dve_done, nth["dve", ("O", t, q)])
                    sp.dma_start(out[:, 4 * q:4 * q + 4, t * QT:(t + 1) * QT],
                                 ob[:, q, :, :]).then_inc(stored[q], 16)
            for q in range(2):
                sp.wait_ge(stored[q], 16 * (T // QT))

        @block.gpsimd
        def _(pool):
            def split_x(c):
                n = CHUNKS[c] * B
                pool.wait_ge(in_x[c], 16)
                if c >= 2:
                    pool.wait_ge(pe_done, max(nth["pe", u] for u in x_users(c - 2, 0)))
                nc.gpsimd.tensor_copy(xsp0[:, c % 2, 0, 0:n], x[:, cols(c)]).then_inc(x_hi, 1)
                pool.wait_ge(x_hi, c + 1)
                nc.gpsimd.tensor_tensor(xsp0[:, c % 2, 1, 0:n], x[:, cols(c)], xsp0[:, c % 2, 0, 0:n],
                                        ALU.subtract).then_inc(x_split, 1)

            nc.gpsimd.memset(d0[:], 0.0).then_inc(pool_set, 1)
            nc.gpsimd.memset(gt[:], 0.0).then_inc(pool_set, 1)
            nc.gpsimd.memset(eimg[:], 0.0).then_inc(pool_set, 1)
            nc.gpsimd.memset(ones[:], 1.0).then_inc(pool_set, 1)
            for c in (0, 1):
                split_x(c)
            chain = [0]

            def link(ins):
                chain[0] += 1
                ins.then_inc(pool_link, 1)
                pool.wait_ge(pool_link, chain[0])

            tts, tsc = nc.gpsimd.tensor_tensor, nc.gpsimd.tensor_scalar
            for kind, *key in parts["pool"]:
                if kind == "XS":
                    if key[0] >= 2:
                        split_x(key[0])
                elif kind == "MB":
                    i, = key
                    if i == 0:
                        pool.wait_ge(in_att, 32)
                        link(nc.gpsimd.tensor_copy(cz[:], A("causal")))
                    C = A("causal").rearrange("p (o k) -> p o k", o=1).broadcast_to([P, 2, QT])
                    r = slice(2 * i, 2 * i + 2)
                    link(tsc(maskr[:, r], maskr[:, r], 1.0 / SC, None, ALU.mult))
                    tts(mb[:, r, 0, :], maskr[:, r, 0:QT], C, ALU.add)
                    nc.gpsimd.tensor_copy(mb[:, r, 1, :], maskr[:, r, 0:QT])
                    tts(mb[:, r, 2, :], maskr[:, r, QT:T], C, ALU.add).then_inc(masks, 1)
                elif kind == "RG":
                    c, l = key
                    k = CHUNKS[c] * B // P
                    pool.wait_ge(dve_done, nth["dve", ("RC", c, l)])
                    if c:
                        pool.wait_ge(pe_done, nth["pe", ("GT", c - 1, l)])
                    if nth["pool", ("RG", c, l)] > 1:
                        pool.wait_ge(gates_made, nth["pool", ("RG", c, l)] - 1)
                    wide = lambda a: a.rearrange("p (k o) -> p k o", o=1).broadcast_to([P, k, E])
                    link(tts(gr[:, 0:k, :], sg[:, l, 0:k, :], wide(rcp2[:, l, 0:k]), ALU.mult))
                    link(tts(gr[:, 0:k, :], gr[:, 0:k, :], wide(zer2[:, l, 0:k]), ALU.add))
                    link(tts(gr[:, 0:k, :], gr[:, 0:k, :], pick[:, l, 0:k, :], ALU.mult))
                    link(nc.gpsimd.tensor_copy(g2[:, l, 0:k, 0:E], gr[:, 0:k, :]))
                    tts(g2[:, l, 0:k, E:2 * E], gr[:, 0:k, :], g2[:, l, 0:k, 0:E], ALU.subtract).then_inc(gates_made, 1)
                elif kind == "Z":
                    c, = key
                    pool.wait_ge(dve_done, nth["dve", ("YE", c, 1)])
                    if STARTS[c] + CHUNKS[c] > ZR:
                        pool.wait_ge(blend, STARTS[c] + CHUNKS[c] - ZR)
                    z0 = STARTS[c] % ZR
                    nc.gpsimd.tensor_scalar(d0[:, z0:z0 + CHUNKS[c], :, 1],
                                            x[:, cols(c)].rearrange("p (t b) -> p t b", b=B), 0.5, None,
                                            ALU.mult).then_inc(z_ready, 1)
                elif kind == "X3":
                    t0, = key
                    pool.wait_ge(h_full, t0 + XP)
                    nc.gpsimd.tensor_tensor(x3[:, :, t0:t0 + XP].rearrange("p b t -> p t b"),
                                            x[:, t0 * B:(t0 + XP) * B].rearrange("p (t b) -> p t b", b=B),
                                            hs[:, t0 + 1:t0 + XP + 1, :], ALU.add).then_inc(x3_ready, 1)
                else:
                    t, b = key
                    pool.wait_ge(dve_done, nth["dve", ("MX", t, b)])
                    if t or b >= 2:
                        t2, b2 = divmod(t * B + b - 2, B)
                        pool.wait_ge(pe_done, nth["pe", ("S", t2, b2, G - 1, t2)])
                    for g in range(G):
                        i = nc.gpsimd.tensor_tensor(
                            lm[:, b % 2, J * g:J * g + J, :],
                            cz[:].rearrange("p (o k) -> p o k", o=1).broadcast_to([P, J, QT]),
                            mneg[:, b, J * g:J * g + J].rearrange("p (j o) -> p j o", o=1).broadcast_to([P, J, QT]), ALU.add)
                    i.then_inc(lm_ready, 1)

        @block.scalar
        def _(act):
            act.dma_start(x[:, cols(0)], x_in[:, cols(0)]).then_inc(in_x[0], 16)
            act.dma_start(rec[:], rec_in).then_inc(in_rec, 16)
            act.dma_start(hs[:, 0, :], small_in[:, SMALL["cond"][0]:SMALL["cond"][0] + B]).then_inc(in_rec, 16)

            def unit(key, half=None):
                kind = key[0]
                if ("pe", key) in nth and half != 1:
                    act.wait_ge(pe_done, nth["pe", key])
                if kind == "W":
                    _, l, i = key
                    a, b = PIECES[i][1:]
                    act.wait_ge(in_up[i], 16)
                    nc.scalar.activation(up[:, 0, a:b], raw[:, a:b], ACT.Copy, scale=WS).then_inc(act_done, 1)
                elif kind == "RT":
                    _, c, l = key
                    k = CHUNKS[c] * B // P
                    act.wait_ge(dve_done, nth["dve", ("R", c, l, 1 if k > 2 else 0)])
                    nc.scalar.activation(th[:, l, 0:k, :], lg[:, l, 0:k, :], ACT.Tanh, scale=0.5).then_inc(act_done, 1)
                elif kind == "SA":
                    _, c, l, j = key
                    n = min(512, SHARED[l] * CHUNKS[c] * B)
                    i = sa_key.index(key)
                    if i:
                        act.wait_ge(dve_done, nth["dve", sa_key[i - 1]])
                    nc.scalar.activation(sth[:, 0:n], hid[bank_of[key]][:, 0:n], ACT.Tanh,
                                         scale=0.5 / WS).then_inc(act_done, 1)
                elif kind == "E":
                    _, c, l, e = key
                    i = hb_of[key]
                    if i >= NHB:
                        act.wait_ge(dve_done, nth["dve", ("M",) + hb_key[i - NHB][1:]])
                    nc.scalar.activation(hb[:, i % NHB, :], hid[bank_of[key]][:], ACT.Gelu, scale=1 / WS).then_inc(act_done, 1)
                elif kind in ("K", "Q"):
                    _, t, g, h = key
                    i = kq_order[key]
                    if half != 1:
                        if i == 0:
                            act.wait_ge(dve_done, nth["dve", ("IK",)])
                        if i >= 2:
                            act.wait_ge(dve_done, nth["dve", kq_key[i - 2]])
                        nc.scalar.activation(xs[:, i % 2, :], hid[bank_of[key]][:], ACT.Identity,
                                             bias=A("kb" if kind == "K" else "qb", g, 1))
                    if half != 0:
                        nc.scalar.activation(tt[:, i % 2, :], hid[bank_of[key]][:], ACT.Identity,
                                             bias=(sbk if kind == "K" else sbq)[:, g:g + 1],
                                             scale=A("sk" if kind == "K" else "sq")).then_inc(act_done, 1)
                elif kind == "IM":
                    _, t, q = key
                    act.wait_ge(dve_done, nth["dve", ("YE", NC - 1, 1)])
                    if (t, q) != (0, 0):
                        prev = ("ID", t, q - 1) if q else ("ID", t - 1, B // 2 - 1)
                        act.wait_ge(pe_done, nth["pe", prev])
                    else:
                        act.wait_ge(pool_set, 3)
                    nc.scalar.activation(eimg[0:H, :], hid[bank_of[key]][0:H, 0:2 * QT], ACT.Exp, scale=SC).then_inc(act_done, 1)
                elif kind == "S":
                    _, t, b, g, kb = key
                    i = s_order[key]
                    if i >= NPT:
                        act.wait_ge(pe_done, nth["pe", ("AV",) + s_key[i - NPT][1:]])
                    nc.scalar.activation(pt[:, i % NPT, :], hid[bank_of[key]][:], ACT.Exp,
                                         bias=A("maskt", b * 2 + kb, 1), scale=SC).then_inc(act_done, 1)

            act.wait_ge(consts, 1)
            for s in range(n_slots):
                t = steps.get(s)
                if t is not None:
                    act.wait_ge(gate_pre, t + 1)
                    c = chunk_of(t)
                    o = (t - STARTS[c]) * B
                    nc.scalar.activation(d1[:, t % 2, :, 0], cbk[c % 2][:, o:o + B], ACT.Tanh,
                                         scale=0.5).then_inc(gate_th, 1)
                units = parts["act"][s]
                cut = t is not None and len(units) == 1 and units[0][0] in ("K", "Q")
                for key in units:
                    unit(key, 0 if cut else None)
                if t is not None:
                    act.wait_ge(blend, t + 1)
                    new = vps.rearrange("p (b o) -> p b o", o=2)[:, :, 1]
                    if t + 1 < T:
                        nc.scalar.activation(hhi[:, (t + 1) % 2, :], new, ACT.Tanh).then_inc(h_hi, 1)
                    nc.scalar.activation(hs[:, t + 1, :], new, ACT.Tanh).then_inc(h_full, 1)
                if cut:
                    unit(units[0], 1)

        @block.tensor
        def _(pe):
            def free(key):
                k = before[key]
                if bank_of[key] == NHT:
                    pe.wait_ge(h_full, T)
                if k:
                    eng = "act" if k[0] in ("E", "IM", "S") else "dve"
                    pe.wait_ge(act_done if eng == "act" else dve_done, nth[eng, k])

            def unit(key):
                kind = key[0]
                if key in bank_of:
                    free(key)
                    hk = hid[bank_of[key]]
                if kind == "IK":
                    pe.wait_ge(in_att, 32)
                    for g in range(G):
                        pe.matmul(hk[:, g * B:g * B + B], A("uk", g), S("cond")[:, 0:B], start=True, stop=True)
                    m = pe.matmul(hk[:, G * B:G * B + B], A("uv"), S("cond")[:, 0:B], start=True, stop=True)
                elif kind == "R":
                    _, c, l, r = key
                    k = CHUNKS[c] * B // P
                    x_ready(kind, c, l)
                    for i in range(2 * r, min(2 * r + 2, k)):
                        for j, (px, pw) in enumerate(((0, 0), (0, 1), (1, 0))):
                            m = pe.matmul(hk[:, i * E:i * E + E], x_part(c, l, px, slice(i * P, i * P + P)), wrx[:, l, pw],
                                          start=j == 0, stop=j == 2)
                elif kind == "GT":
                    _, c, l = key
                    k = CHUNKS[c] * B // P
                    pe.wait_ge(gates_made, nth["pool", ("RG", c, l)])
                    for i in range(k):
                        m = pe.matmul(hk[0:2 * E, i * P:i * P + P], g2[:, l, i, :], id16[:], start=True, stop=True)
                elif kind in ("SA", "SB"):
                    _, c, l, j = key
                    x_ready(kind, c, l)
                    n = CHUNKS[c] * B
                    f = min(512 // n, SHARED[l])
                    for i in range(f):
                        m = times_x(hk[:, i * n:i * n + n], c, l, "w1" if kind == "SA" else "w3", j * f + i)
                elif kind == "E":
                    _, c, l, e = key
                    x_ready(kind, c, l)
                    n = CHUNKS[c] * B
                    f = 512 // n
                    for i in range(f):
                        m = times_x(hk[:, i * n:i * n + n], c, l, "e1", e * f + i)
                elif kind == "M":
                    _, c, l, e = key
                    n = CHUNKS[c] * B
                    pe.wait_ge(dve_done, nth["dve", ("GT", c, l)])
                    f = 512 // n
                    for i in range(f):
                        m = pe.matmul(hk[:, i * n:i * n + n], sel[:, e * f + i, :], gt[:, l, 0:n], start=True, stop=True)
                elif kind == "Y":
                    _, c, l, of, e = key
                    n = CHUNKS[c] * B
                    shared = of == "s"
                    made = ("SB" if shared else "M", c, l, e)
                    pe.wait_ge(dve_done, nth["dve", made])
                    first = first_y[c, l] == key
                    if first and c:
                        pe.wait_ge(dve_done, nth["dve", ("YE", c - 1, l)])
                    if c == 0 and first:
                        pe.wait_ge(in_down[l], 16)
                    f = min(512 // n, SHARED[l]) if shared else 512 // n
                    for i in range(f):
                        m = pe.matmul(ybk[l][:, 0:n], D(l, "w2" if shared else "e2", e * f + i),
                                      hg[:, hg_of[made] % NHG, i * n:i * n + n], start=first and i == 0,
                                      stop=last_y[c, l] == key and i == f - 1)
                elif kind == "C":
                    _, c = key
                    n = CHUNKS[c] * B
                    pe.wait_ge(dve_done, nth["dve", ("YE", c, 1)])
                    if c >= 2:
                        pe.wait_ge(gate_th, STARTS[c - 1])
                    cb = cbk[c % 2][:, 0:n]
                    pe.matmul(cb, wz, x[:, cols(c)], start=True, stop=True)
                    for i in range(2):
                        m = pe.matmul(cb, id16[:], b2[:, i:i + 1].broadcast_to([P, n]), start=False, stop=True,
                                      skip_group_check=True)
                elif kind in ("K", "Q"):
                    _, t, g, h = key
                    t0 = t * QT + 64 * h
                    pe.wait_ge(x3_ready, t0 // 32 + 2)
                    m = pe.matmul(hk[:], A("wk" if kind == "K" else "wq", g), x3[:, :, t0:t0 + 64], start=True, stop=True)
                elif kind == "V":
                    _, t, q = key
                    pe.wait_ge(x3_ready, 4 * (t + 1))
                    for i in range(4):
                        m = pe.matmul(hk[:, i * P:i * P + P], x3[:, 4 * q + i, t * QT:(t + 1) * QT], A("wv"),
                                      start=True, stop=True)
                elif kind == "A":
                    _, t, b, a = key
                    pe.wait_ge(dve_done, nth["dve", ("K", t, G - 1, 1)])
                    pe.wait_ge(dve_done, nth["dve", ("QZ", t, G - 1, 1, 1)])
                    if (t, b, a) == (0, 0, 0):
                        pe.wait_ge(masks, 4)
                    if t == 0:
                        pe.matmul(hk[:], ident[:], mb[:, b, 0:1, :].broadcast_to([P, J, QT]), start=True, stop=True)
                        for j in range(J):
                            m = pe.matmul(hk[:, j * QT:j * QT + QT], qz[:, a, b, j, :], kp[:, a, b, 0:QT],
                                          start=False, stop=True, skip_group_check=True)
                    else:
                        g, j0 = a // 2, 2 * (a % 2)
                        for i in range(2):
                            pe.matmul(hk[:, i * T:i * T + T], ident[:], mb[:, b, 1:3, :].rearrange("p a k -> p (a k)"),
                                      start=i == 0, stop=True, skip_group_check=True)
                        for i in range(2):
                            m = pe.matmul(hk[:, i * T:i * T + T], qz[:, g, b, j0 + i, :], kp[:, g, b, :],
                                          start=False, stop=True, skip_group_check=True)
                elif kind == "MX":
                    _, t, b = key
                    for g in range(G):
                        m = pe.matmul(hk[:, 0:H], fq[:, g, b, :], kbd[:, g, b, :], start=g == 0, stop=g == G - 1)
                elif kind == "IM":
                    _, t, q = key
                    for i in range(2):
                        b = 2 * q + i
                        pe.wait_ge(dve_done, nth["dve", ("MX", t, b)])
                        pe.matmul(hk[0:H, i * QT:i * QT + QT], mneg[:, b, :], ident[:], start=i == 0, stop=True,
                                  skip_group_check=True)
                        for g in range(G):
                            m = pe.matmul(hk[0:H, i * QT:i * QT + QT], kbd[:, g, b, :], fq[:, g, b, :], start=False,
                                          stop=True, skip_group_check=True)
                elif kind == "ID":
                    _, t, q = key
                    pe.wait_ge(act_done, nth["act", ("IM", t, q)])
                    m = pe.matmul(hk[:, 0:2 * QT], A("hexp"), eimg[:], start=True, stop=True)
                elif kind == "S":
                    _, t, b, g, kb = key
                    pe.wait_ge(dve_done, nth["dve", ("MX", t, b)])
                    pe.matmul(hk[:], kp[:, g, b, kb * QT:kb * QT + QT], qz[:, g, b, :, :].rearrange("p j q -> p (j q)"),
                              start=True, stop=True)
                    if kb == t:
                        pe.wait_ge(lm_ready, t * B + b + 1)
                    for j in range(J):
                        hh = J * g + j
                        w = lm[:, b % 2, hh, :] if kb == t else mneg[:, b, hh:hh + 1].broadcast_to([P, QT])
                        m = pe.matmul(hk[:, j * QT:j * QT + QT], w, ident[:], start=False, stop=True,
                                      skip_group_check=True)
                elif kind == "AV":
                    _, t, b, g, kb = key
                    pe.wait_ge(act_done, nth["act", ("S", t, b, g, kb)])
                    pe.wait_ge(dve_done, nth["dve", ("V", t, 1)])
                    if g == 0 and kb == 0 and (t or b):
                        pe.wait_ge(dve_done, nth["dve", ("X", t, b - 1 - t, 1) if b > t else ("X", t - 1, B - 1, 1)])
                        if t:
                            pe.wait_ge(h_full, T)
                    nbk, dbk = cbk if t and b % 2 else ybk
                    p = pt[:, s_order["S", t, b, g, kb] % NPT, :]
                    r = slice(HP * g, HP * g + HP)
                    pe.matmul(nbk[r, :], v[:, b, kb, r], p, start=kb == 0, stop=kb == t)
                    m = pe.matmul(dbk[r, :], ones[:], p, start=kb == 0, stop=kb == t)
                elif kind == "O":
                    _, t, q = key
                    pe.wait_ge(dve_done, nth["dve", ("X", t, 4 * q + 3, 2)])
                    m = pe.matmul(hk[:], A("wp"), on[:, 4 * q:4 * q + 4, :], start=True, stop=True)
                m.then_inc(pe_done, 1)

            def x_ready(kind, c, l):
                if l:
                    pe.wait_ge(dve_done, nth["dve", ("YE", c, 0)])
                else:
                    pe.wait_ge(x_split, c + 1)
                if c == 0 and kind[0] in "SE":
                    pe.wait_ge(dve_done, nth["dve", ("W", l, 2 * l + (kind == "E"))])

            def times_x(into, c, l, name, i):
                a, n = UP[name, l][0] + i * P, CHUNKS[c] * B
                for j, (pw, px) in enumerate(((0, 0), (0, 1), (1, 0))):
                    m = pe.matmul(into, up[:, pw, a:a + P], x_part(c, l, px, slice(0, n)), start=j == 0, stop=j == 2)
                return m

            pe.wait_ge(in_small, 16)
            for l in range(2):
                m = pe.matmul(hid[0][:, l * E:l * E + E], S("cond"), S(f"wrt{l}"), start=True, stop=True)
            m.then_inc(cond_pe, 1)
            pe.wait_ge(in_rec, 32)
            pe.wait_ge(consts, 1)
            pe.wait_ge(pool_set, 4)
            for s in range(n_slots):
                t = steps.get(s)
                if t is not None:
                    c = chunk_of(t)
                    o = (t - STARTS[c]) * B
                    pre = cbk[c % 2][:, o:o + B]
                    if t:
                        pe.wait_ge(h_hi, t)
                    for i in (2, 1, 0):
                        pe.matmul(pre, wh3[:, i, :], hhi[:, t % 2, :], start=False, stop=True, skip_group_check=True)
                    pe.wait_ge(h_lo, t + 1)
                    pe.matmul(pre, wh3[:, 1, :], hlo[:, t % 2, :], start=False, stop=True, skip_group_check=True)
                    pe.matmul(pre, wh3[:, 0, :], hlo[:, t % 2, :], start=False, stop=True,
                              skip_group_check=True).then_inc(gate_pre, 1)
                for key in parts["pe"][s]:
                    unit(key)

        @block.vector
        def _(dve):
            chain = [0]

            def link(ins):
                chain[0] += 1
                ins.then_inc(dve_link, 1)
                dve.wait_ge(dve_link, chain[0])

            tts = nc.vector.tensor_tensor
            tsc = nc.vector.tensor_scalar
            stt = nc.vector.scalar_tensor_tensor

            dve.wait_ge(in_small, 16)
            nc.vector.tensor_copy(ident[:], S("ident"))
            nc.vector.tensor_copy(id16[:], S("ident"))
            for l in range(2):
                tsc(rb5[:, l], S(f"rb{l}"), 0.5, None, ALU.add)
            nc.vector.tensor_copy(sel[:], S("selc").rearrange("p (e o) -> p e o", o=1).broadcast_to([P, E, P]))
            tsc(leak[:], S("alpha"), -1.0, 1.0, ALU.mult, ALU.add)
            for l in range(2):
                link(nc.vector.tensor_copy(wrx[:, l, 0, :], S(f"wrx{l}")))
                tts(wrx[:, l, 1, :], S(f"wrx{l}"), wrx[:, l, 0, :], ALU.subtract)
            dve.wait_ge(in_rec, 32)
            link(nc.vector.tensor_copy(wh3[:, 0, :], wh))
            link(tts(wr[:], wh, wh3[:, 0, :], ALU.subtract))
            link(nc.vector.tensor_copy(wh3[:, 1, :], wr[:]))
            link(tts(wr2[:], wr[:], wh3[:, 1, :], ALU.subtract))
            nc.vector.tensor_copy(wh3[:, 2, :], wr2[:])
            link(nc.vector.tensor_copy(b2[:, 0:1], S("b2")))
            tts(b2[:, 1:2], S("b2"), b2[:, 0:1], ALU.subtract)
            link(nc.vector.tensor_copy(hhi[:, 0, :], hs[:, 0, :]))
            tts(hlo[:, 0, :], hs[:, 0, :], hhi[:, 0, :], ALU.subtract).then_inc(h_lo, 1)
            dve.wait_ge(cond_pe, 1)
            tc_copy = nc.vector.tensor_copy(tc[:].rearrange("p l e -> p (l e)"), hid[0][:, 0:2 * E])
            tc_copy.then_inc(consts, 1)
            dve.wait_ge(consts, 1)

            def unit(key, half):
                kind = key[0]
                last = half != 0
                if ("pe", key) in nth:
                    dve.wait_ge(pe_done, nth["pe", key])
                if key in bank_of:
                    hk = hid[bank_of[key]]
                if kind not in ("GT", "SA", "M") and half != 1 and nth["dve", key] > 1:
                    dve.wait_ge(dve_done, nth["dve", key] - 1)
                if kind in HALVED:
                    n = 512 if kind in ("O", "M") else CHUNKS[key[1]] * B
                    if kind in ("SA", "SB"):
                        n = min(512, SHARED[key[2]] * n)
                    w = slice(0, n) if half is None else slice(half * n // 2, (half + 1) * n // 2)
                if kind == "W":
                    _, l, i = key
                    a, b = PIECES[i][1:]
                    dve.wait_ge(act_done, nth["act", key])
                    i = stt(up[:, 1, a:b], raw[:, a:b], WS, up[:, 0, a:b], ALU.mult, ALU.subtract)
                elif kind == "IK":
                    link(tts(fx[:], hk[:, 0:G * B].rearrange("p (g b) -> p g b", g=G),
                             A("ukb").rearrange("p (g o) -> p g o", o=1).broadcast_to([P, G, B]), ALU.add))
                    link(tsc(ft[:], fx[:], A("sk"), None, ALU.mult))
                    link(stt(fk[:], fx[:], A("mk"), ft[:], ALU.mult, ALU.add))
                    for g in range(G):
                        tts(kbd[:, g, :, :], fk[:, g, :].rearrange("p (b o) -> p b o", o=1).broadcast_to([P, B, H]),
                            A("hmk", g, H).rearrange("p (o h) -> p o h", o=1).broadcast_to([P, B, H]), ALU.mult)
                    tsc(sbq[:], A("qb"), A("sq"), None, ALU.mult)
                    tsc(sbk[:], A("kb"), A("sk"), None, ALU.mult)
                    i = tsc(vimg[:], hk[:, G * B:G * B + B], A("uvb"), None, ALU.add)
                elif kind == "R":
                    _, c, l, r = key
                    k = CHUNKS[c] * B // P
                    a, b = 2 * r, min(2 * r + 2, k)
                    if c:
                        dve.wait_ge(act_done, nth["act", ("RT", c - 1, l)])
                    i = tts(lg[:, l, a:b, :], hk[:, a * E:b * E].rearrange("p (k e) -> p k e", e=E),
                            tc[:, l:l + 1, :].broadcast_to([P, b - a, E]), ALU.add)
                elif kind == "RS":
                    _, c, l = key
                    k = CHUNKS[c] * B // P
                    dve.wait_ge(act_done, nth["act", ("RT", c, l)])
                    if c:
                        dve.wait_ge(gates_made, nth["pool", ("RG", c - 1, l)])
                    tsc(sg[:, l, 0:k, :], th[:, l, 0:k, :], 0.5, 0.5, ALU.mult, ALU.add)
                    link(stt(sl[:, l, 0:k, :], th[:, l, 0:k, :], 0.5,
                             rb5[:, l:l + 1, :].broadcast_to([P, k, E]), ALU.mult, ALU.add))
                    for i in range(k):
                        m = nc.vector.max(mx8[:, l, i, :], sl[:, l, i, :])
                    link(m)
                    for i in range(k):
                        m = nc.vector.max_index(ix8[:, l, i, :], mx8[:, l, i, :], sl[:, l, i, :])
                    i = m
                elif kind == "RD":
                    _, c, l = key
                    k = CHUNKS[c] * B // P
                    io = S("iota").rearrange("p (o e) -> p o e", o=1).broadcast_to([P, k, E])
                    one, two = pick[:, l, 0:k, :], pick2[:, l, 0:k, :]
                    tts(one, io, ix8[:, l, 0:k, 0:1].broadcast_to([P, k, E]), ALU.is_equal)
                    link(tts(two, io, ix8[:, l, 0:k, 1:2].broadcast_to([P, k, E]), ALU.is_equal))
                    link(tts(one, one, two, ALU.add))
                    link(tts(two, one, sg[:, l, 0:k, :], ALU.mult))
                    i = nc.vector.tensor_reduce(den2[:, l, 0:k], two, AX.X, ALU.add)
                elif kind == "RC":
                    _, c, l = key
                    k = CHUNKS[c] * B // P
                    total, factor = den2[:, l, 0:k], rcp2[:, l, 0:k]
                    tsc(zer2[:, l, 0:k], total, EPS, 0.5 * GATE_SCALE[l] * GS, ALU.is_le, ALU.mult)
                    link(tsc(factor, total, EPS, 1 / (GATE_SCALE[l] * GS), ALU.add, ALU.mult))
                    link(nc.vector.reciprocal(factor, factor))
                    i = stt(factor, total, EPS, factor, ALU.is_gt, ALU.mult)
                elif kind == "GT":
                    _, c, l = key
                    if c and half != 1:
                        dve.wait_ge(pe_done, nth["pe", ("M", c - 1, l, E * CHUNKS[c - 1] * B // 512 - 1)])
                    i = nc.vector.tensor_copy(gt[0:2 * E, l, w], hk[0:2 * E, w])
                elif kind == "SA":
                    dve.wait_ge(act_done, nth["act", key])
                    j = sa_key.index(key)
                    if j:
                        dve.wait_ge(dve_done, nth["dve", ("SB",) + sa_key[j - 1][1:]])
                    i = stt(sgl[:, w], sth[:, w], 1.0, hk[:, w], ALU.add, ALU.mult)
                elif kind == "SB":
                    _, c, l, j = key
                    dve.wait_ge(dve_done, nth["dve", ("SA", c, l, j)])
                    hg_free(key)
                    i = stt(hg[:, hg_of[key] % NHG, w], hk[:, w], SHARED_SCALE[l] * GS / WS ** 2, sgl[:, w], ALU.mult, ALU.mult)
                elif kind == "M":
                    _, c, l, e = key
                    dve.wait_ge(act_done, nth["act", ("E", c, l, e)])
                    hg_free(key)
                    i = tts(hg[:, hg_of[key] % NHG, w], hb[:, hb_of["E", c, l, e] % NHB, w], hk[:, w], ALU.mult)
                elif kind == "YE":
                    _, c, l = key
                    a = STARTS[c] * B
                    dve.wait_ge(pe_done, nth["pe", last_y[c, l]])
                    ww = slice(a + w.start, a + w.stop)
                    if l == 0:
                        if c and half != 1:
                            dve.wait_ge(pe_done, max(nth["pe", u] for u in x_users(c - 1, 1)))
                        stt(xsp1[:, 0, w], ybk[l][:, w], 1 / GS, x[:, ww], ALU.mult, ALU.add)
                        link(stt(x[:, ww], ybk[l][:, w], 1 / GS, x[:, ww], ALU.mult, ALU.add))
                        i = tts(xsp1[:, 1, w], x[:, ww], xsp1[:, 0, w], ALU.subtract)
                    else:
                        i = stt(x[:, ww], ybk[l][:, w], 1 / GS, x[:, ww], ALU.mult, ALU.add)
                elif kind in ("K", "Q"):
                    _, t, g, h = key
                    t0 = t * QT + 64 * h
                    i2 = kq_order[key] % 2
                    if kind == "K":
                        dve.wait_ge(masks, 4)
                    dve.wait_ge(act_done, nth["act", key])
                    xv = xs[:, i2, :].rearrange("p (b t) -> p b t", b=B)
                    tv = tt[:, i2, :].rearrange("p (b t) -> p b t", b=B)
                    if kind == "K":
                        i = stt(kp[:, g, :, t0:t0 + 64], xv, A("mk"), tv, ALU.mult, ALU.add)
                    else:
                        if t:
                            dve.wait_ge(pe_done, nth["pe", ("S", t - 1, B - 1, G - 1, t - 1)])
                        q0 = 64 * h
                        i = stt(fq[:, g, :, q0:q0 + 64], xv, A("mq"), tv, ALU.mult, ALU.add)
                elif kind == "QZ":
                    _, t, g, h, i2 = key
                    q0 = 64 * h
                    dve.wait_ge(dve_done, nth["dve", ("Q", t, g, h)])
                    for j in (2 * i2, 2 * i2 + 1):
                        i = tsc(qz[:, g, :, j, q0:q0 + 64], fq[:, g, :, q0:q0 + 64], hm[:, j:j + 1], None, ALU.mult)
                elif kind == "V":
                    _, t, q = key
                    i = tts(v[:, 4 * q:4 * q + 4, t, :], hk[:].rearrange("p (b d) -> p b d", b=4),
                            A("vb").rearrange("p (o d) -> p o d", o=1).broadcast_to([P, 4, P]), ALU.add)
                elif kind == "A":
                    _, t, b, a = key
                    nh = J if t == 0 else 2
                    i = nc.vector.tensor_reduce(wm[:, b, a * nh:(a + 1) * nh],
                                                hk[:].rearrange("p (h k) -> p h k", h=nh), AX.X, ALU.max)
                elif kind == "MX":
                    _, t, b = key
                    dve.wait_ge(dve_done, nth["dve", ("A", t, b, (4 if t == 0 else 8) - 1)])
                    if t:
                        dve.wait_ge(pe_done, nth["pe", ("S", t - 1, b, G - 1, t - 1)])
                        dve.wait_ge(lm_ready, (t - 1) * B + b + 1)
                    link(tts(mm[:, b, :], hk[:, 0:H], wm[:, b, :], ALU.max))
                    i = tsc(mneg[:, b, :], mm[:, b, :], -1.0, None, ALU.mult)
                elif kind == "ID":
                    _, t, q = key
                    d = hk[:, 0:2 * QT].rearrange("p (b q) -> p b q", b=2)
                    r = slice(2 * q, 2 * q + 2)
                    if t:
                        dve.wait_ge(dve_done, nth["dve", ("X", t - 1, B - 1, 1)])
                    nc.vector.tensor_copy(dimg[:, r, :], d)
                    i = tts(nimg[:, r, :], d,
                            vimg[:, r].rearrange("p (b o) -> p b o", o=1).broadcast_to([P, 2, QT]), ALU.mult)
                elif kind == "X":
                    _, t, b, part = key
                    dve.wait_ge(pe_done, nth["pe", ("AV", t, b, G - 1, t)])
                    dve.wait_ge(dve_done, nth["dve", ("ID", t, b // 2)])
                    nbk, dbk = cbk if t and b % 2 else ybk
                    if part < 2:
                        for j in (2 * part, 2 * part + 1):
                            w = slice(j * QT, j * QT + QT)
                            for bank, sums, image in ((dbk, den, dimg), (nbk, num, nimg)):
                                if j % 2:
                                    dve.wait_ge(dve_link, chain[0] - 1 if sums is den else chain[0])
                                i = stt(sums[:, j % 2, :], bank[:, w], hx[:, j:j + 1],
                                        sums[:, (j - 1) % 2, :] if j else image[:, b, :], ALU.mult, ALU.add)
                                if j % 2 == 0:
                                    chain[0] += 1
                                    i.then_inc(dve_link, 1)
                    else:
                        if t and b % 4 == 0:
                            dve.wait_ge(pe_done, nth["pe", ("O", t - 1, b // 4)])
                        link(nc.vector.reciprocal(den[:, 0, :], den[:, 1, :]))
                        i = tts(on[:, b, :], num[:, 1, :], den[:, 0, :], ALU.mult)
                elif kind == "O":
                    _, t, q = key
                    h0, h1 = (0, 4) if half is None else (2 * half, 2 * half + 2)
                    bb = slice(4 * q + h0, 4 * q + h1)
                    if t:
                        dve.wait_ge(stored[q], 16 * t)
                    i = stt(ob[:, q, h0:h1, :], hk[:, w].rearrange("p (b q) -> p b q", q=QT), A("pb"),
                            x3[:, bb, t * QT:(t + 1) * QT], ALU.add, ALU.add)
                if last:
                    i.then_inc(dve_done, 1)

            def hg_free(key):
                i = hg_of[key]
                if i >= NHG:
                    k = hg_key[i - NHG]
                    y = ("Y", k[1], k[2], "e" if k[0] == "M" else "s", k[3])
                    dve.wait_ge(pe_done, nth["pe", y])

            for s in range(n_slots):
                t = steps.get(s)
                units = parts["dve"][s]
                if t is None:
                    for key in units:
                        unit(key, None)
                    continue
                if t:
                    dve.wait_ge(h_full, t)
                    tts(hlo[:, t % 2, :], hs[:, t, :], hhi[:, t % 2, :], ALU.subtract).then_inc(h_lo, 1)
                dve.wait_ge(z_ready, chunk_of(t) + 1)
                stt(d1[:, t % 2, :, 1], hs[:, t, :], leak[:], d0[:, t % ZR, :, 1], ALU.mult, ALU.add).then_inc(decay, 1)
                first = [k for i, k in enumerate(units) if i < len(units) // 2]
                rest = units[len(units) // 2:]
                cut = len(units) % 2 == 1 and rest[0][0] in HALVED
                for key in first:
                    unit(key, None)
                if cut:
                    unit(rest[0], 0)
                dve.wait_ge(gate_th, t + 1)
                dve.wait_ge(decay, t + 1)
                nc.vector.tensor_tensor_scan(vps, d0[:, t % ZR].rearrange("p b o -> p (b o)"),
                                             d1[:, t % 2].rearrange("p b o -> p (b o)"), 0.0, ALU.mult,
                                             ALU.add).then_inc(blend, 1)
                if cut:
                    unit(rest[0], 1)
                    rest = rest[1:]
                for key in rest:
                    unit(key, None)


HALVED = ("GT", "SA", "SB", "M", "YE", "O")



def padded(a):
    lead = a.shape[:-2]
    out = np.zeros(lead + (G, J, HP), a.dtype)
    for r in range(3):
        out[..., r * HD:(r + 1) * HD] = a.reshape(lead + (G, J, HD))
    return out.reshape(lead + (G * J * HP,))


def constants():
    p = np.arange(P)
    one = lambda cond: cond.astype(np.float32)
    selc = one(np.arange(E) == np.where(p < 2 * E, p % E, -1)[:, None])
    lo_q, lo_k = one((p % HP) // HD == 2), one((p % HP) // HD == 1)
    h = np.arange(H)
    hmk = np.stack([one(h[None, :] == (J * g + p // HP)[:, None]) for g in range(G)], 1)
    return {
        "ident": np.eye(P, dtype=np.float32), "iota": np.tile(np.arange(E, dtype=np.float32), (P, 1)),
        "selc": selc,
        "causal": one(p[None, :] > p[:, None]) * np.float32(NEG),
        "hm": one(p[:, None] // HP == np.arange(J)), "hx": one((p[:, None] % HP) // HD == np.arange(J)),
        "sq": (1 - 2 * lo_q)[:, None], "mq": lo_q[:, None], "sk": (1 - 2 * lo_k)[:, None], "mk": lo_k[:, None],
        "hmk": hmk.reshape(P, G * H), "hexp": one(p[:, None] == p[None, :] // HD),
    }


def kernel(**inputs):
    import concourse.bacc as bacc
    from concourse.bass_utils import run_bass_kernel_spmd

    a = {k: np.asarray(v) for k, v in inputs.items()}
    con = constants()
    rows = lambda w: np.ascontiguousarray(np.broadcast_to(w, (P,) + w.shape)).reshape(P, -1)
    wide = lambda w: np.ascontiguousarray(w).reshape(P, -1)
    tiles = lambda w: wide(w.transpose(1, 0, 2))

    def pack(layout, total, blocks):
        out = np.zeros((P, total), np.float32)
        for name, (at, width) in layout.items():
            out[:, at:at + width] = (blocks if name in blocks else con)[name]
        return out

    L0, L1, L2, L3 = (lambda n, l=l: a[f"L{l}_cond_{n}"] for l in range(4))
    small = pack(SMALL, N_SMALL, {
        "cond": np.tile(a["cond_1024"].T, (1, P // B)), "wrx0": L0("router_W")[:D], "wrt0": L0("router_W")[D:],
        "wrx1": L1("W_router")[:, :D].T, "wrt1": L1("W_router")[:, D:].T,
        "rb0": rows(L0("router_bias")), "rb1": rows(L1("router_bias")),
        "alpha": L2("alpha")[:, None], "b2": L2("b")[:, None]})
    up = pack(UP, N_UP, {
        ("w1", 0): L0("w1"), ("w3", 0): L0("w3"), ("e1", 0): tiles(L0("W1e")),
        ("w1", 1): wide(L1("s_w1").transpose(2, 0, 1)), ("w3", 1): wide(L1("s_w3").transpose(2, 0, 1)),
        ("e1", 1): tiles(L1("r_w1").transpose(0, 2, 1))})
    down = pack(DOWN, N_DOWN, {
        ("w2", 0): tiles(L0("w2").reshape(2, P, D)), ("e2", 0): tiles(L0("W2e")),
        ("w2", 1): tiles(L1("s_w2").transpose(0, 2, 1).reshape(4, P, D)), ("e2", 1): tiles(L1("r_w2").transpose(0, 2, 1))})
    rec = pack({"wh": (0, P), "wz": (P, P)}, N_REC, {"wh": L2("W")[:, :D].T, "wz": L2("W")[:, D:].T})
    w, wb = L3("c_attn_w"), L3("c_attn_b")
    col = lambda v: padded(v.reshape(H, HD)).reshape(G, P).T
    att = pack(ATT, N_ATT, {
        "wq": padded(w[:, :D].reshape(D, H, HD)), "wk": padded(w[:, D:2 * D].reshape(D, H, HD)), "wv": w[:, 2 * D:],
        "wp": L3("c_proj_w"), "uk": padded(L3("uk_w").T.reshape(D, H, HD)), "uv": L3("uv_w").T,
        "qb": col(wb[:D]), "kb": col(wb[D:2 * D]), "ukb": col(L3("uk_b")), "pb": L3("c_proj_b")[:, None],
        "uvb": L3("uv_b")[:, None], "vb": rows(wb[2 * D:]),
        "maskt": wide(a["mask_Bx1x1xS_ff0"].reshape(B, 2, P).transpose(2, 0, 1))})
    arrays = {"x_in": wide(a["x"].transpose(2, 1, 0)), "small_in": small, "up_in": up, "down_in": down, "rec_in": rec,
              "att_in": att, "maskr_in": rows(a["mask_Bx1x1xS_ff0"].reshape(B * T))}

    nc = bacc.Bacc("TRN2", target_bir_lowering=False, num_devices=1)
    args = [nc.dram_tensor(n, v.shape, mybir.dt.from_np(v.dtype), kind="ExternalInput").ap() for n, v in arrays.items()]
    out = nc.dram_tensor("out_dram", (P, B, T), F32, kind="ExternalOutput").ap()
    build(nc, *args, out)
    r = run_bass_kernel_spmd(nc, [arrays], core_ids=[0])
    return np.ascontiguousarray(r.results[0]["out_dram"].transpose(1, 2, 0))
```

```python
from contextlib import ExitStack

import numpy as np
import concourse.bass as bass
from concourse import mybir

F32 = mybir.dt.float32
BF16 = mybir.dt.bfloat16
F16 = mybir.dt.float16
U32 = mybir.dt.uint32
ACT = mybir.ActivationFunctionType
ALU = mybir.AluOpType
AX = mybir.AxisListType

P = 128
B, T, D = 8, 256, 128
E = 8
H, HD = 16, 8
G, J = 4, 4
HP = 32
SHARED = (2, 4)
SHARED_SCALE = (0.5 / 3.0, 0.5 / 8.0)
GATE_SCALE = (1.0 / 3.0, 1.0 / 4.0)
CHUNKS = (32,) * 8
STARTS = tuple(sum(CHUNKS[:i]) for i in range(len(CHUNKS)))
NC = len(CHUNKS)
QT = 128
NEG = -1.0e5
SC = float(1.0 / np.sqrt(HD))
EPS = 1e-9
XP = 32
ZR = 128
NHT, NHB, NHG = 3, 8, 4
AHEAD = (4, 2)
QZ_ACT = ((), (0, 1, 2, 3))
NPT = 6
CAPS = {"before": (1100, 1100, 1100), "in": (1200, 1200, 1200), "behind": (1800, 2100, 2000)}
ACT_LAST = ("E", "IM", "S", "K", "Q")
LATE = ("E", "S", "K", "Q")


def columns(*parts):
    at, out = 0, {}
    for *name, width in parts:
        out[name[0] if len(name) == 1 else tuple(name)] = (at, width)
        at += width
    return out, at


SMALL, N_SMALL = columns(("cond", P), ("wrx0", E), ("wrt0", E), ("wrx1", E), ("wrt1", E), ("rb0", E), ("rb1", E),
                         ("alpha", 1), ("b2", 1), ("ident", P), ("iota", E), ("selc", E))

UP, N_UP = columns(("w1", 0, 256), ("w3", 0, 256), ("e1", 0, E * P), ("w1", 1, 512), ("w3", 1, 512), ("e1", 1, E * P))
DOWN, N_DOWN = columns(("w2", 0, 256), ("e2", 0, E * P), ("w2", 1, 512), ("e2", 1, E * P))
PIECES = ((0, 0, 512), (0, 512, 1536), (1, 1536, 2560), (1, 2560, 3584))
WS = 256.0
GS = 256.0
REC, N_REC = columns(("wh", P), ("wz", P))
ATT, N_ATT = columns(("wq", P), ("wk", P), ("wv", P), ("wp", P), ("uk", G * P), ("uv", P), ("qb", 1), ("kb", 1),
                     ("ukb", G), ("pb", 1), ("uvb", 1), ("vb", P), ("causal", P), ("hm", J), ("hx", J),
                     ("sk", 1), ("mk", 1), ("hmk", G * H), ("hexp", P), ("maskt", B * 2))


def plan():
    units = []

    def add(key, pe, act, dve, bank, *needs):
        units.append((key, pe, act, dve, bank, needs))

    mm4 = lambda n: 4 * n / 2.4
    mm3 = lambda n: 3 * n / 2.4
    for i, (l, a, b) in enumerate(PIECES):
        add(("W", l, i), 0, 200 + (b - a) * .9, 60 + (b - a) * 1.05, False,
            *([(("RC", 0, 0), "dve", "act")] if l else []))
    for c in range(NC):
        n = CHUNKS[c] * B
        k = n // P
        for l in range(2):
            if l == 0:
                add(("XS", c), 0, 0, 0, False, *[(u, "pe", "pool") for u in x_users(c - 2, 0)])
            x = [(("YL", c), "dve", "pe")] if l else [(("XS", c), "pool", "pe")]
            if l == 0 and c >= 2:
                x.append((("YE", c - 2, 1), "dve", "dve"))
            w = [(("W", l, 2 * l), "dve", "pe")] if c == 0 else []
            we = [(("W", l, 2 * l + 1), "dve", "pe")] if c == 0 else []
            half = [(0, min(2, k))] + ([(2, k)] if k > 2 else [])
            for r, (a, b) in enumerate(half):
                add(("R", c, l, r), 190 * (b - a), 0, 130, True, *x, *([(("RG", c - 1, l), "pool", "dve")] if c else []))
            add(("RT", c, l), 0, 220, 0, False, (("R", c, l, len(half) - 1), "dve", "act"))
            add(("RS", c, l), 0, 0, 400 + 80 * (1 + 2 * k), False, (("RT", c, l), "act", "dve"))
            add(("RD", c, l), 0, 0, 800, False, (("RS", c, l), "dve", "dve"))
            add(("RC", c, l), 0, 0, 700, False, (("RD", c, l), "dve", "dve"))
            add(("RG", c, l), 0, 0, 0, False, (("RC", c, l), "dve", "pool"))
            add(("GT", c, l), 60 * k, 0, 60 + n, True, (("RG", c, l), "pool", "pe"),
                *([(("M", c - 1, l, E * CHUNKS[c - 1] * B // 512 - 1), "pe", "pe")] if c else []))
            f = 512 // n
            fs = min(f, SHARED[l])
            wide = 60 + fs * n * .84, 100 + fs * n * 1.05
            for i in range(SHARED[l] // fs):
                add(("SA", c, l, i), fs * mm3(n), *wide, True, *x, *w)
                add(("SB", c, l, i), fs * mm3(n), 0, wide[1], True, (("SA", c, l, i), "dve", "dve"), *x)
                add(("Y", c, l, "s", i), fs * mm4(n), 0, 0, False, (("SB", c, l, i), "dve", "pe"),
                    *([(("YE", c - 1, l), "dve", "pe")] if c else []))
            for i in range(E // f):
                add(("E", c, l, i), f * mm3(n), 490, 0, True, *x, *we)
            for i in range(E // f):
                add(("M", c, l, i), 213, 0, 640, True, (("E", c, l, i), "act", "dve"), (("GT", c, l), "dve", "pe"))
                add(("Y", c, l, "e", i), f * mm4(n), 0, 0, False, (("M", c, l, i), "dve", "pe"),
                    *([(("YE", c - 1, l), "dve", "pe")] if c else []))
            last = [("Y", c, l, "e", i) for i in range(E // f)] + [("Y", c, l, "s", i) for i in range(SHARED[l] // fs)]
            add(("YE", c, l), 0, 0, (100 + n * 1.05) * (1 if l else 2), False, *[(y, "pe", "dve") for y in last],
                *([(u, "pe", "dve") for u in x_users(c - 1, 1)] if l == 0 else []))
            if l == 0:
                add(("YL", c), 0, 0, 100 + n * 1.05, False, (("YE", c, 0), "dve", "dve"))
        add(("C", c), mm4(n) + 2 * n / 2.4, 0, 0, False, (("YE", c, 1), "dve", "pe"), (("WH", 2), "dve", "pe"))
        if c == 0:
            for i in range(3):
                add(("WH", i), 0, 0, 700, False, (("E", 0, 1, 0), "pe", "dve"))
        if c == 2:
            add(("IK",), 600, 0, 2500, True, (("C", 1), "pe", "pe"))
    projections = []

    def keys_and_queries(t):
        kq = (("STEP", QT * (t + 1) - 1), "pool", "pe")
        for i in range(2):
            add(("V", t, i), 880, 0, 640, True, kq)
        for kind in "KQ":
            for h in range(2):
                i = len(projections)
                add((kind + "P", t, h), 860, 575, 665, True, (("STEP", QT * t + 64 * h + 63), "pool", "pe"), (("IK",), "dve", "act"),
                    *([((*projections[i - 2][:2], G - 1, projections[i - 2][2]), "pe", "act")] if i >= 2 else []))
                projections.append((kind, t, h))
                if kind == "K":
                    for g in range(G):
                        add((kind, t, g, h), 430, 485, 0, True, ((kind + "P", t, h), "dve", "pe"))
        for g in range(G):
            for h in range(2):
                add(("Q", t, g, h), 430, 485, 0, True, (("QP", t, h), "dve", "pe"),
                    *([(("S", t - 1, B - 1, G - 1, t - 1), "pe", "act")] if t else []))
                for i in range(2):
                    eng = "act" if g in QZ_ACT[t] and i else "dve"
                    add(("QZ", t, g, h, i), 0, *((1000, 0) if eng == "act" else (0, 530)), False, (("Q", t, g, h), "act", eng))

    keys_and_queries(0)
    for t in range(T // QT):
        n_a = 4 if t == 0 else 8

        def maximum(b, a):
            g = a // (t + 1)
            add(("A", t, b, a), 430, 0, 660, True, (("K", t, g, 1), "act", "pe"),
                *[(("QZ", t, g, 1, i), "act" if g in QZ_ACT[t] and i else "dve", "pe") for i in range(2)])

        def image_maximum(b):
            add(("MX", t, b), 220, 0, 320, True, (("A", t, b, n_a - 1), "dve", "dve"))

        def image(q):
            add(("IM", t, q), 550, 300, 0, True, *[(("MX", t, b), "dve", "pe") for b in (2 * q, 2 * q + 1)])
            add(("ID", t, q), 430, 0, 650, True, (("IM", t, q), "act", "pe"))

        if t == 0:
            keys_and_queries(1)
        for b in range(AHEAD[t]):
            for a in range(n_a):
                maximum(b, a)
            image_maximum(b)
            if b % 2:
                image(b // 2)
        for b in range(B):
            for g in range(G):
                for kb in range(t + 1):
                    add(("S", t, b, g, kb), 440, 500, 0, True, (("MX", t, b), "dve", "pe"))
                    add(("AV", t, b, g, kb), 430, 0, 0, False, (("S", t, b, g, kb), "act", "pe"),
                        *([(("X", t, b - 1 - t, 1), "dve", "pe")] if b > t else [(("X", t - 1, B - 1, 1), "dve", "pe")] if t else []))
                    if b + AHEAD[t] < B:
                        maximum(b + AHEAD[t], (t + 1) * g + kb)
            if b + AHEAD[t] < B:
                image_maximum(b + AHEAD[t])
                if (b + AHEAD[t]) % 2:
                    image((b + AHEAD[t]) // 2)
            add(("X", t, b, 0), 0, 0, 1050, False, (("AV", t, b, G - 1, t), "pe", "dve"), (("ID", t, b // 2), "dve", "dve"))
            add(("X", t, b, 1), 0, 0, 1050, False, (("X", t, b, 0), "dve", "dve"))
            add(("X", t, b, 2), 0, 0, 880, False, (("X", t, b, 1), "dve", "dve"))
            add(("X", t, b, 3), 0, 0, 210, False, (("X", t, b, 2), "dve", "dve"))
            if b % 4 == 3:
                q = b // 4
                add(("O", t, q), 860, 0, 700, True, *[(("X", t, b, 3), "dve", "pe") for b in range(4 * q, 4 * q + 4)])

    info = {u[0]: u for u in units}
    later = {k: {"pe": 0, "act": 1, "dve": 2 if u[2] else 1, "pool": 1} for k, u in info.items()}
    def apart(k, of, by):
        return 0 if of == by else 3 if of == "pool" else 2 if of == "act" and k[0] in LATE and step < T else 1
    slot_of, step_slot, order = {}, {}, []
    bank_of, before, user, last_use = {}, {}, [None] * (NHT + 1), [0] * (NHT + 1)
    hg_users, hb_users = [], []
    used = {eng: [0] * 1100 for eng in ("pe", "act", "dve")}
    left = list(units)
    s = step = 0
    while left or step < T:
        if step < T:
            c = chunk_of(step)
            if ("C", c) in slot_of and slot_of["C", c] < s:
                step_slot[step] = s
                step += 1
        phase = ("before" if not step or step < T and step_slot[step - 1] != s else
                 "behind" if step == T and step_slot[T - 1] + 1 < s else "in")
        caps = dict(zip(("pe", "act", "dve"), CAPS[phase]))
        passed = set()
        for u in list(left):
            key, up, ua, ud, bank, needs = u
            family = key[:3] if key[0] in ("R", "SA", "SB", "E", "M", "GT") else "P" if key[0] in ("KP", "QP") else key[:2]
            if key[0] != "Y" and family in passed:
                continue
            passed.add(family)
            lat = later[key]
            if any(cost and used[eng][s + lat[eng]] and used[eng][s + lat[eng]] + cost > caps[eng]
                   for eng, cost in (("pe", up), ("act", ua), ("dve", ud))):
                continue
            ok = True
            for k, of, by in needs:
                if k[0] == "STEP":
                    ok = k[1] in step_slot and step_slot[k[1]] + 3 <= s
                elif k not in slot_of or slot_of[k] + later[k][of] + apart(k, of, by) > s + lat[by]:
                    ok = False
                if not ok:
                    break
            if ok and key[0] == "C" and key[1] >= 2:
                end = STARTS[key[1] - 1] - 1
                ok = end in step_slot and step_slot[end] + 2 <= s
            if ok and ("C", 0) not in slot_of and key[0] not in ("W", "WH", "XS", "C"):
                ok = key[1] <= 1 and ("W", 0, 0) in slot_of
            if ok and bank:
                at = min(range(NHT + (step == T and phase == "behind")), key=lambda i: last_use[i])
                ok = last_use[at] <= s
            if ok and key[0] in ("M", "SB") and len(hg_users) >= NHG:
                k = hg_users[-NHG]
                y = ("Y", k[1], k[2], "e", k[3]) if k[0] == "M" else ("Y", k[1], k[2], "s", k[3])
                ok = y in slot_of and slot_of[y] + 1 <= s + lat["dve"]
            if ok and key[0] in ("M", "SB") and key[1]:
                ok = all(("M", key[1] - 1, key[2], i) in slot_of for i in range(E * CHUNKS[key[1] - 1] * B // 512))
            if ok and key[0] == "E" and len(hb_users) >= NHB:
                k = hb_users[-NHB]
                k = ("M",) + k[1:]
                ok = k in slot_of and slot_of[k] + later[k]["dve"] <= s
            if ok and key[0] == "SA":
                ok = not any(k[0] == "SA" and ("SB",) + k[1:] not in slot_of for k in slot_of)
            if ok and key[0] == "S" and key[4] == key[1]:
                _, t, b, g, _ = key
                ok = slot_of["MX", t, b] + 5 <= s
                if ok and b >= 2:
                    ok = slot_of["S", t, b - 2, G - 1, t] + 4 <= s
            if ok and key[0] in ("S", "IM"):
                ok = ("YE", NC - 1, 1) in slot_of and slot_of["YE", NC - 1, 1] + 1 < s
            if ok and key[0] == "AV" and key[1] and key[2] % 2:
                ok = step == T and phase == "behind"
            if ok and key[0] == "S":
                ok = sum(k[0] == "S" for k in slot_of) - sum(k[0] == "AV" for k in slot_of) < NPT
            if not ok:
                continue
            passed.discard(family)
            slot_of[key] = s
            order.append((s, key))
            left.remove(u)
            for eng, cost in (("pe", up), ("act", ua), ("dve", ud)):
                used[eng][s + lat[eng]] += cost
            if bank:
                bank_of[key], before[key] = at, user[at]
                user[at], last_use[at] = key, s + lat["act" if key[0] in ACT_LAST else "dve"] + 1
            if key[0] in ("M", "SB"):
                hg_users.append(key)
            if key[0] == "E":
                hb_users.append(key)
        s += 1
        assert s < 1000, (left[:3], hg_users[-5:], hb_users[-9:], step)
    hg_of = {k: i for i, k in enumerate(hg_users)}
    hb_of = {k: i for i, k in enumerate(hb_users)}
    n_slots = s + 3
    parts = {"pe": [[] for _ in range(n_slots)], "act": [[] for _ in range(n_slots)], "dve": [[] for _ in range(n_slots)]}
    for at, key in order:
        for eng, cost in (("pe", 1), ("act", 2), ("dve", 3)):
            if info[key][cost]:
                parts[eng][at + later[key][eng]].append(key)
    for at in step_slot.values():
        parts["act"][at].sort(key=lambda k: k[0] in LATE)
    nth = {}
    for eng in parts:
        n = 0
        for units_of_slot in parts[eng]:
            for key in units_of_slot:
                n += 1
                nth[eng, key] = n
    steps = {at: t for t, at in step_slot.items()}
    pool = [(slot_of["XS", c], "XS", c) for c in range(NC)]
    pool += [(slot_of[k] + 1, *k) for k in slot_of if k[0] == "RG"]
    pool += [(slot_of["YE", c, 1] + 2, "Z", c) for c in range(NC)]
    pool += [(slot_of["IK",] + 1 + 8 * i, "MB", i) for i in range(4)]
    pool += [(step_slot[t0 + XP - 1] + 1, "X3", t0) for t0 in range(0, T, XP)]
    pool += [(max([slot_of["MX", t, b] + 2] + [slot_of["S", t2, b2, G - 1, t2] for t2, b2 in [divmod(t * B + b - 2, B)]
                                               if t or b >= 2]), "LM", t, b) for t in range(T // QT) for b in range(B)]
    parts["pool"] = [u[1:] for u in sorted(pool)]
    for key in parts["pool"]:
        if key[0] == "RG":
            nth["pool", key] = sum(k[0] == "pool" for k in nth) + 1
    return parts, nth, steps, bank_of, before, hg_of, hb_of, n_slots


def x_users(c, l):
    if c < 0:
        return []
    n = CHUNKS[c] * B
    f = 512 // n
    return ([("R", c, l, r) for r in range((n // P + 1) // 2)] + [("E", c, l, i) for i in range(E // f)] +
            [(s, c, l, i) for s in ("SA", "SB") for i in range(SHARED[l] // min(f, SHARED[l]))])


def chunk_of(t):
    return max(i for i in range(NC) if STARTS[i] <= t)


def build(nc, x_in, small_in, up_in, down_in, rec_in, att_in, maskr_in, out):
    parts, nth, steps, bank_of, before, hg_of, hb_of, n_slots = plan()

    with ExitStack() as ctx:
        def sb(name, shape, dt=F32):
            return ctx.enter_context(nc.sbuf_tensor(name, shape, dt))

        def ps(name):
            return ctx.enter_context(nc.psum_tensor(name, [P, 512], F32))

        def sem(name):
            return ctx.enter_context(nc.semaphore(name))

        x = sb("x", [P, T * B])
        small = sb("small", [P, N_SMALL])
        up = sb("up", [P, 2, N_UP], F16)
        down = sb("down", [P, N_DOWN])
        xsp0 = sb("xsp0", [P, 2, 2, 256], F16)
        xsp1 = sb("xsp1", [P, 2, 256], F16)
        wrx = sb("wrx", [P, 2, 2, E], F16)
        rec = sb("rec", [P, N_REC])
        att = sb("att", [P, N_ATT])
        ident = sb("ident", [P, P], BF16)
        sel = sb("sel", [P, E, P], F16)
        ones = sb("ones", [P, HP])
        tc = sb("tc", [P, 2, E])
        lg = sb("lg", [P, 2, 4, E])
        th = sb("th", [P, 2, 4, E])
        sg = sb("sg", [P, 2, 4, E])
        sl = sb("sl", [P, 2, 4, E])
        mx8 = sb("mx8", [P, 2, 4, 8])
        ix8 = sb("ix8", [P, 2, 4, 8], U32)
        rb5 = sb("rb5", [P, 2, E])
        pick = sb("pick", [P, 2, 4, E])
        pick2 = sb("pick2", [P, 2, 4, E])
        den2 = sb("den2", [P, 2, 4])
        rcp2 = sb("rcp2", [P, 2, 4])
        zer2 = sb("zer2", [P, 2, 4])
        gr = sb("gr", [P, 4, E])
        g2 = sb("g2", [P, 2, 4, 2 * E], F16)
        gt = sb("gt", [P, 2, 512], F16)
        id16 = sb("id16", [P, P], F16)
        hb = sb("hb", [P, NHB, 512])
        hg = sb("hg", [P, NHG, 512])
        silu = sb("silu", [P, 2, 512])
        sth, sgl = silu[:, 0], silu[:, 1]
        wh3 = sb("wh3", [P, 3, P], BF16)
        b2 = sb("b2", [P, 2], F16)
        leak = sb("leak", [P, 1])
        warm = sb("warm", [P, 1])
        d0 = sb("d0", [P, ZR, B, 2])
        d1 = sb("d1", [P, 2, B, 2])
        hs = sb("hs", [P, T + 1, B])
        hhi = sb("hhi", [P, 2, B], F16)
        hlo = sb("hlo", [P, 2, B], F16)
        x3 = sb("x3", [P, B, T])
        kp = sb("kp", [P, G, B, T], F16)
        maskr = kp[:].rearrange("p g b t -> p (g b t)").bitcast(F32).rearrange("p (x b t) -> p x b t", x=2, b=B)[:, 0]
        fq = sb("fq", [P, G, B, QT], F16)
        qz = sb("qz", [P, G, B, J, QT], F16)
        kq = sb("kq", [P, 2, 2, 512], F16)
        spread = sb("spread", [P, 2, 2, G * P], F16)
        fk = sb("fk", [P, G, B], F16)
        fx = sb("fx", [P, G, B])
        ft = sb("ft", [P, G, B], F16)
        kbd = sb("kbd", [P, G, B, H], F16)
        vimg = sb("vimg", [P, B])
        v = sb("v", [P, B, 2, P])
        mb = sb("mb", [P, B, 3, QT], BF16)
        cz = sb("cz", [P, P], BF16)
        wm = sb("wm", [P, B, H])
        mm = sb("mm", [P, B, H])
        mneg = sb("mneg", [P, B, H], BF16)
        lm = sb("lm", [P, 2, H, QT], BF16)
        eimg = sb("eimg", [P, 2 * QT])
        pt = hb[:, 0:NPT, :]
        dimg = hg[:, 2:4, :].rearrange("p a (b q) -> p (a b) q", q=QT)
        nimg = hb[:, 6:8, :].rearrange("p a (b q) -> p (a b) q", q=QT)
        on = hg[:, 0:2, :].rearrange("p a (b q) -> p (a b) q", q=QT)
        num = sb("num", [P, 2, QT])
        den = sb("den", [P, 2, QT])
        wr, wr2 = num[:, 0], den[:, 0]
        ob = silu[:].rearrange("p a (b q) -> p a b q", b=4)
        raw = qz[:].rearrange("p g b j q -> p (g b j q)").bitcast(F32)

        ybk = [ps("ybk0"), ps("ybk1")]
        cbk = [ps("cbk0"), ps("cbk1")]
        vbk = ps("vbk")
        hid = [ps(f"hid{i}") for i in range(NHT)] + [vbk]
        vps = vbk[:, 0:2 * B]

        in_x = [sem(f"in_x{c}") for c in range(NC)]
        in_up = [sem(f"in_up{i}") for i in range(len(PIECES))]
        in_down = [sem(f"in_down{l}") for l in range(2)]
        in_small, in_rec, in_att = (sem(f"in_{n}") for n in ("small", "rec", "att"))
        pe_done = sem("pe_done")
        act_done = sem("act_done")
        dve_done = sem("dve_done")
        dve_link = sem("dve_link")
        act_link = sem("act_link")
        masks = sem("masks")
        pool_set = sem("pool_set")
        x_hi = sem("x_hi")
        x_split = sem("x_split")
        gates_made = sem("gates_made")
        pool_link = sem("pool_link")
        z_ready = sem("z_ready")
        x3_ready = sem("x3_ready")
        consts = sem("consts")
        cond_pe = sem("cond_pe")
        gate_pre = sem("gate_pre")
        gate_th = sem("gate_th")
        decay = sem("decay")
        blend = sem("blend")
        h_hi = sem("h_hi")
        h_full = sem("h_full")
        h_lo = sem("h_lo")
        maxes = sem("maxes")
        lm_ready = sem("lm_ready")
        stored = [sem("stored0"), sem("stored1")]

        def S(name):
            a, n = SMALL[name]
            return small[:, a:a + n]

        def D(l, name, i):
            a, _ = DOWN[name, l]
            return down[:, a + i * P:a + i * P + P]

        def x_part(c, l, part, cols):
            return xsp1[:, part, cols] if l else xsp0[:, c % 2, part, cols]

        def A(name, i=None, w=P):
            a, n = ATT[name]
            return att[:, a:a + n] if i is None else att[:, a + i * w:a + i * w + w]

        wh = rec[:, 0:P]
        wz = rec[:, P:2 * P]
        hm, hx = A("hm"), A("hx")
        first_y, last_y = {}, {}
        for slot in parts["pe"]:
            for key in slot:
                if key[0] == "Y":
                    first_y.setdefault(key[1:3], key)
                    last_y[key[1:3]] = key
        order_of = lambda kinds, eng: [k for slot in parts[eng] for k in slot if k[0] in kinds]
        hg_key = sorted(hg_of, key=hg_of.get)
        hb_key = sorted(hb_of, key=hb_of.get)
        kq_key, s_key, sa_key = order_of(("KP", "QP"), "act"), order_of(("S",), "act"), order_of(("SA",), "act")
        kq_order = {k: i for i, k in enumerate(kq_key)}
        s_order = {k: i for i, k in enumerate(s_key)}

        def cols(c):
            return slice(STARTS[c] * B, (STARTS[c] + CHUNKS[c]) * B)

        block = ctx.enter_context(nc.Block())

        @block.sync
        def _(sp):
            sp.dma_start(small[:], small_in).then_inc(in_small, 16)
            d1_at = DOWN["w2", 1][0]
            for i in (0, 1):
                sp.dma_start(raw[:, PIECES[i][1]:PIECES[i][2]], up_in[:, PIECES[i][1]:PIECES[i][2]]).then_inc(in_up[i], 16)
            sp.dma_start(down[:, 0:d1_at], down_in[:, 0:d1_at]).then_inc(in_down[0], 16)
            sp.dma_start(x[:, cols(1)], x_in[:, cols(1)]).then_inc(in_x[1], 16)
            for i in (2, 3):
                sp.dma_start(raw[:, PIECES[i][1]:PIECES[i][2]], up_in[:, PIECES[i][1]:PIECES[i][2]]).then_inc(in_up[i], 16)
            sp.dma_start(down[:, d1_at:], down_in[:, d1_at:]).then_inc(in_down[1], 16)
            for c in range(2, NC):
                sp.dma_start(x[:, cols(c)], x_in[:, cols(c)]).then_inc(in_x[c], 16)
            sp.dma_start(att[:], att_in).then_inc(in_att, 16)
            sp.dma_start(maskr.rearrange("p b t -> p (b t)"), maskr_in).then_inc(in_att, 16)
            for t in range(T // QT):
                for q in range(2):
                    sp.wait_ge(dve_done, nth["dve", ("O", t, q)])
                    sp.dma_start(out[:, 4 * q:4 * q + 4, t * QT:(t + 1) * QT],
                                 ob[:, q, :, :]).then_inc(stored[q], 16)
            for q in range(2):
                sp.wait_ge(stored[q], 16 * (T // QT))

        @block.gpsimd
        def _(pool):
            def split_x(c):
                n = CHUNKS[c] * B
                pool.wait_ge(in_x[c], 16)
                if c >= 2:
                    pool.wait_ge(pe_done, max(nth["pe", u] for u in x_users(c - 2, 0)))
                nc.gpsimd.tensor_copy(xsp0[:, c % 2, 0, 0:n], x[:, cols(c)]).then_inc(x_hi, 1)
                pool.wait_ge(x_hi, c + 1)
                nc.gpsimd.tensor_tensor(xsp0[:, c % 2, 1, 0:n], x[:, cols(c)], xsp0[:, c % 2, 0, 0:n],
                                        ALU.subtract).then_inc(x_split, 1)

            nc.gpsimd.memset(d0[:], 0.0).then_inc(pool_set, 1)
            nc.gpsimd.memset(gt[:], 0.0).then_inc(pool_set, 1)
            nc.gpsimd.memset(eimg[:], 0.0).then_inc(pool_set, 1)
            nc.gpsimd.memset(ones[:], 1.0).then_inc(pool_set, 1)
            nc.gpsimd.memset(spread[:], 0.0).then_inc(pool_set, 1)
            for c in (0, 1):
                split_x(c)
            chain = [0]

            def link(ins):
                chain[0] += 1
                ins.then_inc(pool_link, 1)
                pool.wait_ge(pool_link, chain[0])

            tts, tsc = nc.gpsimd.tensor_tensor, nc.gpsimd.tensor_scalar
            for kind, *key in parts["pool"]:
                if kind == "XS":
                    if key[0] >= 2:
                        split_x(key[0])
                elif kind == "MB":
                    i, = key
                    if i == 0:
                        pool.wait_ge(in_att, 32)
                        link(nc.gpsimd.tensor_copy(cz[:], A("causal")))
                    C = A("causal").rearrange("p (o k) -> p o k", o=1).broadcast_to([P, 2, QT])
                    r = slice(2 * i, 2 * i + 2)
                    link(tsc(maskr[:, r], maskr[:, r], 1.0 / SC, None, ALU.mult))
                    tts(mb[:, r, 0, :], maskr[:, r, 0:QT], C, ALU.add)
                    nc.gpsimd.tensor_copy(mb[:, r, 1, :], maskr[:, r, 0:QT])
                    tts(mb[:, r, 2, :], maskr[:, r, QT:T], C, ALU.add).then_inc(masks, 1)
                elif kind == "RG":
                    c, l = key
                    k = CHUNKS[c] * B // P
                    pool.wait_ge(dve_done, nth["dve", ("RC", c, l)])
                    if c:
                        pool.wait_ge(pe_done, nth["pe", ("GT", c - 1, l)])
                    if nth["pool", ("RG", c, l)] > 1:
                        pool.wait_ge(gates_made, nth["pool", ("RG", c, l)] - 1)
                    wide = lambda a: a.rearrange("p (k o) -> p k o", o=1).broadcast_to([P, k, E])
                    link(tts(gr[:, 0:k, :], sg[:, l, 0:k, :], wide(rcp2[:, l, 0:k]), ALU.mult))
                    link(tts(gr[:, 0:k, :], gr[:, 0:k, :], wide(zer2[:, l, 0:k]), ALU.add))
                    link(tts(gr[:, 0:k, :], gr[:, 0:k, :], pick[:, l, 0:k, :], ALU.mult))
                    link(nc.gpsimd.tensor_copy(g2[:, l, 0:k, 0:E], gr[:, 0:k, :]))
                    tts(g2[:, l, 0:k, E:2 * E], gr[:, 0:k, :], g2[:, l, 0:k, 0:E], ALU.subtract).then_inc(gates_made, 1)
                elif kind == "Z":
                    c, = key
                    pool.wait_ge(dve_done, nth["dve", ("YE", c, 1)])
                    if STARTS[c] + CHUNKS[c] > ZR:
                        pool.wait_ge(blend, STARTS[c] + CHUNKS[c] - ZR)
                    z0 = STARTS[c] % ZR
                    nc.gpsimd.tensor_scalar(d0[:, z0:z0 + CHUNKS[c], :, 1],
                                            x[:, cols(c)].rearrange("p (t b) -> p t b", b=B), 0.5, None,
                                            ALU.mult).then_inc(z_ready, 1)
                elif kind == "X3":
                    t0, = key
                    pool.wait_ge(h_full, t0 + XP)
                    nc.gpsimd.tensor_tensor(x3[:, :, t0:t0 + XP].rearrange("p b t -> p t b"),
                                            x[:, t0 * B:(t0 + XP) * B].rearrange("p (t b) -> p t b", b=B),
                                            hs[:, t0 + 1:t0 + XP + 1, :], ALU.add).then_inc(x3_ready, 1)
                else:
                    t, b = key
                    pool.wait_ge(dve_done, nth["dve", ("MX", t, b)])
                    if t or b >= 2:
                        t2, b2 = divmod(t * B + b - 2, B)
                        pool.wait_ge(pe_done, nth["pe", ("S", t2, b2, G - 1, t2)])
                    for g in range(G):
                        i = nc.gpsimd.tensor_tensor(
                            lm[:, b % 2, J * g:J * g + J, :],
                            cz[:].rearrange("p (o k) -> p o k", o=1).broadcast_to([P, J, QT]),
                            mneg[:, b, J * g:J * g + J].rearrange("p (j o) -> p j o", o=1).broadcast_to([P, J, QT]), ALU.add)
                    i.then_inc(lm_ready, 1)

        @block.scalar
        def _(act):
            act.dma_start(x[:, cols(0)], x_in[:, cols(0)]).then_inc(in_x[0], 16)
            act.dma_start(rec[:], rec_in).then_inc(in_rec, 16)
            act.dma_start(hs[:, 0, :], small_in[:, SMALL["cond"][0]:SMALL["cond"][0] + B]).then_inc(in_rec, 16)

            act.wait_ge(in_rec, 32)
            nc.scalar.activation(warm[:, 0:1], hs[:, 0, 0:1], ACT.Gelu)

            def unit(key):
                kind = key[0]
                if ("pe", key) in nth:
                    act.wait_ge(pe_done, nth["pe", key])
                if kind == "W":
                    _, l, i = key
                    a, b = PIECES[i][1:]
                    act.wait_ge(in_up[i], 16)
                    nc.scalar.activation(up[:, 0, a:b], raw[:, a:b], ACT.Copy, scale=WS).then_inc(act_done, 1)
                elif kind == "RT":
                    _, c, l = key
                    k = CHUNKS[c] * B // P
                    act.wait_ge(dve_done, nth["dve", ("R", c, l, 1 if k > 2 else 0)])
                    nc.scalar.activation(th[:, l, 0:k, :], lg[:, l, 0:k, :], ACT.Tanh, scale=0.5).then_inc(act_done, 1)
                elif kind == "SA":
                    _, c, l, j = key
                    n = min(512, SHARED[l] * CHUNKS[c] * B)
                    i = sa_key.index(key)
                    if i:
                        act.wait_ge(dve_done, nth["dve", sa_key[i - 1]])
                    nc.scalar.activation(sth[:, 0:n], hid[bank_of[key]][:, 0:n], ACT.Tanh,
                                         scale=0.5 / WS).then_inc(act_done, 1)
                elif kind == "E":
                    _, c, l, e = key
                    i = hb_of[key]
                    if i >= NHB:
                        act.wait_ge(dve_done, nth["dve", ("M",) + hb_key[i - NHB][1:]])
                    nc.scalar.activation(hb[:, i % NHB, :], hid[bank_of[key]][:], ACT.Gelu, scale=1 / WS).then_inc(act_done, 1)
                elif kind in ("KP", "QP"):
                    i = kq_order[key]
                    if i >= 2:
                        k = kq_key[i - 2]
                        act.wait_ge(pe_done, nth["pe", (k[0][0], k[1], G - 1, k[2])])
                    nc.scalar.activation(kq[:, i % 2, 0, :], hid[bank_of[key]][:], ACT.Identity,
                                         bias=A("kb" if kind == "KP" else "qb")).then_inc(act_done, 1)
                elif kind in ("K", "Q"):
                    _, t, g, h = key
                    if kind == "K":
                        act.wait_ge(masks, 4)
                        into = kp[:, g, :, t * QT + 64 * h:t * QT + 64 * h + 64]
                    else:
                        if t:
                            act.wait_ge(pe_done, nth["pe", ("S", t - 1, B - 1, G - 1, t - 1)])
                        into = fq[:, g, :, 64 * h:64 * h + 64]
                    nc.scalar.activation(into, hid[bank_of[key]][:].rearrange("p (b t) -> p b t", b=B),
                                         ACT.Copy).then_inc(act_done, 1)
                elif kind == "QZ":
                    _, t, g, h, half = key
                    q = slice(64 * h, 64 * h + 64)
                    act.wait_ge(act_done, nth["act", ("Q", t, g, h)])
                    for j in (2 * half, 2 * half + 1):
                        i = nc.scalar.activation(qz[:, g, :, j, q], fq[:, g, :, q], ACT.Copy, scale=hm[:, j:j + 1])
                    i.then_inc(act_done, 1)
                elif kind == "IM":
                    _, t, q = key
                    act.wait_ge(dve_done, nth["dve", ("YE", NC - 1, 1)])
                    if (t, q) != (0, 0):
                        prev = ("ID", t, q - 1) if q else ("ID", t - 1, B // 2 - 1)
                        act.wait_ge(pe_done, nth["pe", prev])
                    else:
                        act.wait_ge(pool_set, 3)
                    nc.scalar.activation(eimg[0:H, :], hid[bank_of[key]][0:H, 0:2 * QT], ACT.Exp, scale=SC).then_inc(act_done, 1)
                elif kind == "S":
                    _, t, b, g, kb = key
                    i = s_order[key]
                    if i >= NPT:
                        act.wait_ge(pe_done, nth["pe", ("AV",) + s_key[i - NPT][1:]])
                    nc.scalar.activation(pt[:, i % NPT, :], hid[bank_of[key]][:], ACT.Exp,
                                         bias=A("maskt", b * 2 + kb, 1), scale=SC).then_inc(act_done, 1)

            for s in range(n_slots):
                t = steps.get(s)
                if t is not None:
                    act.wait_ge(gate_pre, t + 1)
                    c = chunk_of(t)
                    o = (t - STARTS[c]) * B
                    nc.scalar.activation(d1[:, t % 2, :, 0], cbk[c % 2][:, o:o + B], ACT.Tanh,
                                         scale=0.5).then_inc(gate_th, 1)
                units = parts["act"][s]
                early = [k for k in units if t is None or k[0] not in LATE]
                for key in early:
                    unit(key)
                if t is not None:
                    act.wait_ge(blend, t + 1)
                    new = vps.rearrange("p (b o) -> p b o", o=2)[:, :, 1]
                    if t + 1 < T:
                        nc.scalar.activation(hhi[:, (t + 1) % 2, :], new, ACT.Tanh).then_inc(h_hi, 1)
                    nc.scalar.activation(hs[:, t + 1, :], new, ACT.Tanh).then_inc(h_full, 1)
                for key in units:
                    if key not in early:
                        unit(key)

        @block.tensor
        def _(pe):
            def free(key):
                k = before[key]
                if bank_of[key] == NHT:
                    pe.wait_ge(h_full, T)
                if k:
                    eng = "act" if k[0] in ACT_LAST else "dve"
                    pe.wait_ge(act_done if eng == "act" else dve_done, nth[eng, k])

            def unit(key):
                kind = key[0]
                if key in bank_of:
                    free(key)
                    hk = hid[bank_of[key]]
                if kind == "IK":
                    pe.wait_ge(in_att, 32)
                    for g in range(G):
                        pe.matmul(hk[:, g * B:g * B + B], A("uk", g), S("cond")[:, 0:B], start=True, stop=True)
                    m = pe.matmul(hk[:, G * B:G * B + B], A("uv"), S("cond")[:, 0:B], start=True, stop=True)
                elif kind == "R":
                    _, c, l, r = key
                    k = CHUNKS[c] * B // P
                    x_ready(kind, c, l)
                    for i in range(2 * r, min(2 * r + 2, k)):
                        for j, (px, pw) in enumerate(((0, 0), (0, 1), (1, 0))):
                            m = pe.matmul(hk[:, i * E:i * E + E], x_part(c, l, px, slice(i * P, i * P + P)), wrx[:, l, pw],
                                          start=j == 0, stop=j == 2)
                elif kind == "GT":
                    _, c, l = key
                    k = CHUNKS[c] * B // P
                    pe.wait_ge(gates_made, nth["pool", ("RG", c, l)])
                    for i in range(k):
                        m = pe.matmul(hk[0:2 * E, i * P:i * P + P], g2[:, l, i, :], id16[:], start=True, stop=True)
                elif kind in ("SA", "SB"):
                    _, c, l, j = key
                    x_ready(kind, c, l)
                    n = CHUNKS[c] * B
                    f = min(512 // n, SHARED[l])
                    for i in range(f):
                        m = times_x(hk[:, i * n:i * n + n], c, l, "w1" if kind == "SA" else "w3", j * f + i)
                elif kind == "E":
                    _, c, l, e = key
                    x_ready(kind, c, l)
                    n = CHUNKS[c] * B
                    f = 512 // n
                    for i in range(f):
                        m = times_x(hk[:, i * n:i * n + n], c, l, "e1", e * f + i)
                elif kind == "M":
                    _, c, l, e = key
                    n = CHUNKS[c] * B
                    pe.wait_ge(dve_done, nth["dve", ("GT", c, l)])
                    f = 512 // n
                    for i in range(f):
                        m = pe.matmul(hk[:, i * n:i * n + n], sel[:, e * f + i, :], gt[:, l, 0:n], start=True, stop=True)
                elif kind == "Y":
                    _, c, l, of, e = key
                    n = CHUNKS[c] * B
                    shared = of == "s"
                    made = ("SB" if shared else "M", c, l, e)
                    pe.wait_ge(dve_done, nth["dve", made])
                    first = first_y[c, l] == key
                    if first and c:
                        pe.wait_ge(dve_done, nth["dve", ("YE", c - 1, l)])
                    if c == 0 and first:
                        pe.wait_ge(in_down[l], 16)
                    f = min(512 // n, SHARED[l]) if shared else 512 // n
                    for i in range(f):
                        m = pe.matmul(ybk[l][:, 0:n], D(l, "w2" if shared else "e2", e * f + i),
                                      hg[:, hg_of[made] % NHG, i * n:i * n + n], start=first and i == 0,
                                      stop=last_y[c, l] == key and i == f - 1)
                elif kind == "C":
                    _, c = key
                    n = CHUNKS[c] * B
                    pe.wait_ge(dve_done, nth["dve", ("YE", c, 1)])
                    pe.wait_ge(dve_done, nth["dve", ("WH", 2)])
                    if c >= 2:
                        pe.wait_ge(gate_th, STARTS[c - 1])
                    cb = cbk[c % 2][:, 0:n]
                    pe.matmul(cb, wz, x[:, cols(c)], start=True, stop=True)
                    for i in range(2):
                        m = pe.matmul(cb, id16[:], b2[:, i:i + 1].broadcast_to([P, n]), start=False, stop=True,
                                      skip_group_check=True)
                elif kind in ("KP", "QP"):
                    _, t, h = key
                    t0 = t * QT + 64 * h
                    pe.wait_ge(x3_ready, t0 // 32 + 2)
                    m = pe.matmul(hk[:], A("wk" if kind == "KP" else "wq"), x3[:, :, t0:t0 + 64], start=True, stop=True)
                elif kind in ("K", "Q"):
                    _, t, g, h = key
                    made = (kind + "P", t, h)
                    pe.wait_ge(dve_done, nth["dve", made])
                    for part in range(2):
                        m = pe.matmul(hk[:], spread[:, "KQ".index(kind), part, g * P:g * P + P],
                                      kq[:, kq_order[made] % 2, part, :], start=part == 0, stop=part == 1)
                elif kind == "V":
                    _, t, q = key
                    pe.wait_ge(x3_ready, 4 * (t + 1))
                    for i in range(4):
                        m = pe.matmul(hk[:, i * P:i * P + P], x3[:, 4 * q + i, t * QT:(t + 1) * QT], A("wv"),
                                      start=True, stop=True)
                elif kind == "A":
                    _, t, b, a = key
                    g = a // (t + 1)
                    pe.wait_ge(act_done, nth["act", ("K", t, g, 1)])
                    for i in range(2):
                        if ("act", ("QZ", t, g, 1, i)) in nth:
                            pe.wait_ge(act_done, nth["act", ("QZ", t, g, 1, i)])
                        else:
                            pe.wait_ge(dve_done, nth["dve", ("QZ", t, g, 1, i)])
                    if (t, b, a) == (0, 0, 0):
                        pe.wait_ge(masks, 4)
                    if t == 0:
                        pe.matmul(hk[:], ident[:], mb[:, b, 0:1, :].broadcast_to([P, J, QT]), start=True, stop=True)
                        for j in range(J):
                            m = pe.matmul(hk[:, j * QT:j * QT + QT], qz[:, a, b, j, :], kp[:, a, b, 0:QT],
                                          start=False, stop=True, skip_group_check=True)
                    else:
                        g, j0 = a // 2, 2 * (a % 2)
                        for i in range(2):
                            pe.matmul(hk[:, i * T:i * T + T], ident[:], mb[:, b, 1:3, :].rearrange("p a k -> p (a k)"),
                                      start=i == 0, stop=True, skip_group_check=True)
                        for i in range(2):
                            m = pe.matmul(hk[:, i * T:i * T + T], qz[:, g, b, j0 + i, :], kp[:, g, b, :],
                                          start=False, stop=True, skip_group_check=True)
                elif kind == "MX":
                    _, t, b = key
                    for g in range(G):
                        m = pe.matmul(hk[:, 0:H], fq[:, g, b, :], kbd[:, g, b, :], start=g == 0, stop=g == G - 1)
                elif kind == "IM":
                    _, t, q = key
                    for i in range(2):
                        b = 2 * q + i
                        pe.wait_ge(dve_done, nth["dve", ("MX", t, b)])
                        pe.matmul(hk[0:H, i * QT:i * QT + QT], mneg[:, b, :], ident[:], start=i == 0, stop=True,
                                  skip_group_check=True)
                        for g in range(G):
                            m = pe.matmul(hk[0:H, i * QT:i * QT + QT], kbd[:, g, b, :], fq[:, g, b, :], start=False,
                                          stop=True, skip_group_check=True)
                elif kind == "ID":
                    _, t, q = key
                    pe.wait_ge(act_done, nth["act", ("IM", t, q)])
                    m = pe.matmul(hk[:, 0:2 * QT], A("hexp"), eimg[:], start=True, stop=True)
                elif kind == "S":
                    _, t, b, g, kb = key
                    pe.wait_ge(dve_done, nth["dve", ("MX", t, b)])
                    pe.matmul(hk[:], kp[:, g, b, kb * QT:kb * QT + QT], qz[:, g, b, :, :].rearrange("p j q -> p (j q)"),
                              start=True, stop=True)
                    if kb == t:
                        pe.wait_ge(lm_ready, t * B + b + 1)
                    for j in range(J):
                        hh = J * g + j
                        w = lm[:, b % 2, hh, :] if kb == t else mneg[:, b, hh:hh + 1].broadcast_to([P, QT])
                        m = pe.matmul(hk[:, j * QT:j * QT + QT], w, ident[:], start=False, stop=True,
                                      skip_group_check=True)
                elif kind == "AV":
                    _, t, b, g, kb = key
                    pe.wait_ge(act_done, nth["act", ("S", t, b, g, kb)])
                    pe.wait_ge(dve_done, nth["dve", ("V", t, 1)])
                    if g == 0 and kb == 0 and (t or b):
                        pe.wait_ge(dve_done, nth["dve", ("X", t, b - 1 - t, 1) if b > t else ("X", t - 1, B - 1, 1)])
                        if t:
                            pe.wait_ge(h_full, T)
                    nbk, dbk = cbk if t and b % 2 else ybk
                    p = pt[:, s_order["S", t, b, g, kb] % NPT, :]
                    r = slice(HP * g, HP * g + HP)
                    pe.matmul(nbk[r, :], v[:, b, kb, r], p, start=kb == 0, stop=kb == t)
                    m = pe.matmul(dbk[r, :], ones[:], p, start=kb == 0, stop=kb == t)
                elif kind == "O":
                    _, t, q = key
                    pe.wait_ge(dve_done, nth["dve", ("X", t, 4 * q + 3, 3)])
                    m = pe.matmul(hk[:], A("wp"), on[:, 4 * q:4 * q + 4, :], start=True, stop=True)
                m.then_inc(pe_done, 1)

            def x_ready(kind, c, l):
                if l:
                    pe.wait_ge(dve_done, nth["dve", ("YL", c)])
                else:
                    pe.wait_ge(x_split, c + 1)
                if c == 0 and kind[0] in "SE":
                    pe.wait_ge(dve_done, nth["dve", ("W", l, 2 * l + (kind == "E"))])

            def times_x(into, c, l, name, i):
                a, n = UP[name, l][0] + i * P, CHUNKS[c] * B
                for j, (pw, px) in enumerate(((0, 0), (0, 1), (1, 0))):
                    m = pe.matmul(into, up[:, pw, a:a + P], x_part(c, l, px, slice(0, n)), start=j == 0, stop=j == 2)
                return m

            pe.wait_ge(in_small, 16)
            for l in range(2):
                m = pe.matmul(hid[0][:, l * E:l * E + E], S("cond"), S(f"wrt{l}"), start=True, stop=True)
            m.then_inc(cond_pe, 1)
            pe.wait_ge(consts, 1)
            pe.wait_ge(pool_set, 4)
            for s in range(n_slots):
                t = steps.get(s)
                if t is not None:
                    c = chunk_of(t)
                    o = (t - STARTS[c]) * B
                    pre = cbk[c % 2][:, o:o + B]
                    if t:
                        pe.wait_ge(h_hi, t)
                    for i in (2, 1, 0):
                        pe.matmul(pre, wh3[:, i, :], hhi[:, t % 2, :], start=False, stop=True, skip_group_check=True)
                    if t:
                        pe.wait_ge(h_lo, t)
                    pe.matmul(pre, wh3[:, 1, :], hlo[:, t % 2, :], start=False, stop=True, skip_group_check=True)
                    pe.matmul(pre, wh3[:, 0, :], hlo[:, t % 2, :], start=False, stop=True,
                              skip_group_check=True).then_inc(gate_pre, 1)
                for key in parts["pe"][s]:
                    unit(key)

        @block.vector
        def _(dve):
            chain = [0]

            def link(ins, wait=True):
                chain[0] += 1
                ins.then_inc(dve_link, 1)
                if wait:
                    dve.wait_ge(dve_link, chain[0])

            tts = nc.vector.tensor_tensor
            tsc = nc.vector.tensor_scalar
            stt = nc.vector.scalar_tensor_tensor

            dve.wait_ge(in_small, 16)
            nc.vector.tensor_copy(ident[:], S("ident"))
            nc.vector.tensor_copy(id16[:], S("ident"))
            for l in range(2):
                tsc(rb5[:, l], S(f"rb{l}"), 0.5, None, ALU.add)
            nc.vector.tensor_copy(sel[:], S("selc").rearrange("p (e o) -> p e o", o=1).broadcast_to([P, E, P]))
            tsc(leak[:], S("alpha"), -1.0, 1.0, ALU.mult, ALU.add)
            for l in range(2):
                link(nc.vector.tensor_copy(wrx[:, l, 0, :], S(f"wrx{l}")))
                tts(wrx[:, l, 1, :], S(f"wrx{l}"), wrx[:, l, 0, :], ALU.subtract)
            dve.wait_ge(cond_pe, 1)
            tc_copy = nc.vector.tensor_copy(tc[:].rearrange("p l e -> p (l e)"), hid[0][:, 0:2 * E])
            tc_copy.then_inc(consts, 1)
            dve.wait_ge(consts, 1)

            def unit(key, half):
                kind = key[0]
                last = half != 0
                if ("pe", key) in nth:
                    dve.wait_ge(pe_done, nth["pe", key])
                if key in bank_of:
                    hk = hid[bank_of[key]]
                if kind in ("X", "IK", "WH", "W") and half != 1 and nth["dve", key] > 1:
                    dve.wait_ge(dve_done, nth["dve", key] - 1)
                if kind in HALVED:
                    n = 512 if kind in ("O", "M", "KP", "QP") else CHUNKS[key[1]] * B
                    if kind in ("SA", "SB"):
                        n = min(512, SHARED[key[2]] * n)
                    w = slice(0, n) if half is None else slice(half * n // 2, (half + 1) * n // 2)
                if kind == "W":
                    _, l, i = key
                    a, b = PIECES[i][1:]
                    dve.wait_ge(act_done, nth["act", key])
                    i = stt(up[:, 1, a:b], raw[:, a:b], WS, up[:, 0, a:b], ALU.mult, ALU.subtract)
                elif kind == "WH":
                    if key[1] == 0:
                        dve.wait_ge(in_rec, 32)
                        link(nc.vector.tensor_copy(wh3[:, 0, :], wh))
                        link(tts(wr[:], wh, wh3[:, 0, :], ALU.subtract))
                        i = nc.vector.tensor_copy(wh3[:, 1, :], wr[:])
                    elif key[1] == 1:
                        link(tts(wr2[:], wr[:], wh3[:, 1, :], ALU.subtract))
                        i = nc.vector.tensor_copy(wh3[:, 2, :], wr2[:])
                    else:
                        nc.vector.tensor_copy(b2[:, 0:1], S("b2"))
                        link(nc.vector.tensor_copy(hhi[:, 0, :], hs[:, 0, :]))
                        tts(b2[:, 1:2], S("b2"), b2[:, 0:1], ALU.subtract)
                        i = tts(hlo[:, 0, :], hs[:, 0, :], hhi[:, 0, :], ALU.subtract)
                elif kind == "IK":
                    link(tts(fx[:], hk[:, 0:G * B].rearrange("p (g b) -> p g b", g=G),
                             A("ukb").rearrange("p (g o) -> p g o", o=1).broadcast_to([P, G, B]), ALU.add))
                    link(tsc(ft[:], fx[:], A("sk"), None, ALU.mult))
                    link(stt(fk[:], fx[:], A("mk"), ft[:], ALU.mult, ALU.add))
                    for g in range(G):
                        tts(kbd[:, g, :, :], fk[:, g, :].rearrange("p (b o) -> p b o", o=1).broadcast_to([P, B, H]),
                            A("hmk", g, H).rearrange("p (o h) -> p o h", o=1).broadcast_to([P, B, H]), ALU.mult)
                    dve.wait_ge(pool_set, 5)
                    for of, part, r in ((0, 0, 0), (0, 1, 1), (0, 0, 2), (1, 0, 0), (1, 0, 1), (1, 1, 2)):
                        nc.vector.tensor_copy(spread[:, of, part, :].rearrange("p (h r d) -> p h r d", r=4, d=HD)[:, :, r, :],
                                              id16[:].rearrange("p (h d) -> p h d", d=HD))
                    i = tsc(vimg[:], hk[:, G * B:G * B + B], A("uvb"), None, ALU.add)
                elif kind == "R":
                    _, c, l, r = key
                    k = CHUNKS[c] * B // P
                    a, b = 2 * r, min(2 * r + 2, k)
                    if c:
                        dve.wait_ge(act_done, nth["act", ("RT", c - 1, l)])
                    i = tts(lg[:, l, a:b, :], hk[:, a * E:b * E].rearrange("p (k e) -> p k e", e=E),
                            tc[:, l:l + 1, :].broadcast_to([P, b - a, E]), ALU.add)
                elif kind == "RS":
                    _, c, l = key
                    k = CHUNKS[c] * B // P
                    dve.wait_ge(act_done, nth["act", ("RT", c, l)])
                    if half != 1:
                        if c:
                            dve.wait_ge(gates_made, nth["pool", ("RG", c - 1, l)])
                        tsc(sg[:, l, 0:k, :], th[:, l, 0:k, :], 0.5, 0.5, ALU.mult, ALU.add)
                        link(stt(sl[:, l, 0:k, :], th[:, l, 0:k, :], 0.5,
                                 rb5[:, l:l + 1, :].broadcast_to([P, k, E]), ALU.mult, ALU.add))
                        for i in range(k):
                            m = nc.vector.max(mx8[:, l, i, :], sl[:, l, i, :])
                        link(m, wait=False)
                    if half != 0:
                        dve.wait_ge(dve_link, chain[0])
                        for i in range(k):
                            m = nc.vector.max_index(ix8[:, l, i, :], mx8[:, l, i, :], sl[:, l, i, :])
                        i = m
                elif kind == "RD":
                    _, c, l = key
                    k = CHUNKS[c] * B // P
                    io = S("iota").rearrange("p (o e) -> p o e", o=1).broadcast_to([P, k, E])
                    one, two = pick[:, l, 0:k, :], pick2[:, l, 0:k, :]
                    if half != 1:
                        dve.wait_ge(dve_done, nth["dve", ("RS", c, l)])
                        tts(one, io, ix8[:, l, 0:k, 0:1].broadcast_to([P, k, E]), ALU.is_equal)
                        link(tts(two, io, ix8[:, l, 0:k, 1:2].broadcast_to([P, k, E]), ALU.is_equal))
                        link(tts(one, one, two, ALU.add), wait=False)
                    if half != 0:
                        dve.wait_ge(dve_link, chain[0])
                        link(tts(two, one, sg[:, l, 0:k, :], ALU.mult))
                        i = nc.vector.tensor_reduce(den2[:, l, 0:k], two, AX.X, ALU.add)
                elif kind == "RC":
                    _, c, l = key
                    k = CHUNKS[c] * B // P
                    total, factor = den2[:, l, 0:k], rcp2[:, l, 0:k]
                    if half != 1:
                        dve.wait_ge(dve_done, nth["dve", ("RD", c, l)])
                        tsc(zer2[:, l, 0:k], total, EPS, 0.5 * GATE_SCALE[l] * GS, ALU.is_le, ALU.mult)
                        link(tsc(factor, total, EPS, 1 / (GATE_SCALE[l] * GS), ALU.add, ALU.mult))
                        link(nc.vector.reciprocal(factor, factor), wait=False)
                    if half != 0:
                        dve.wait_ge(dve_link, chain[0])
                        i = stt(factor, total, EPS, factor, ALU.is_gt, ALU.mult)
                elif kind == "GT":
                    _, c, l = key
                    if c and half != 1:
                        dve.wait_ge(pe_done, nth["pe", ("M", c - 1, l, E * CHUNKS[c - 1] * B // 512 - 1)])
                    i = nc.vector.tensor_copy(gt[0:2 * E, l, w], hk[0:2 * E, w])
                elif kind == "SA":
                    dve.wait_ge(act_done, nth["act", key])
                    j = sa_key.index(key)
                    if j:
                        dve.wait_ge(dve_done, nth["dve", ("SB",) + sa_key[j - 1][1:]])
                    i = stt(sgl[:, w], sth[:, w], 1.0, hk[:, w], ALU.add, ALU.mult)
                elif kind == "SB":
                    _, c, l, j = key
                    dve.wait_ge(dve_done, nth["dve", ("SA", c, l, j)])
                    hg_free(key)
                    i = stt(hg[:, hg_of[key] % NHG, w], hk[:, w], SHARED_SCALE[l] * GS / WS ** 2, sgl[:, w], ALU.mult, ALU.mult)
                elif kind == "M":
                    _, c, l, e = key
                    dve.wait_ge(act_done, nth["act", ("E", c, l, e)])
                    hg_free(key)
                    i = tts(hg[:, hg_of[key] % NHG, w], hb[:, hb_of["E", c, l, e] % NHB, w], hk[:, w], ALU.mult)
                elif kind == "YE":
                    _, c, l = key
                    a = STARTS[c] * B
                    dve.wait_ge(pe_done, nth["pe", last_y[c, l]])
                    ww = slice(a + w.start, a + w.stop)
                    if l == 0:
                        if c and half != 1:
                            dve.wait_ge(pe_done, max(nth["pe", u] for u in x_users(c - 1, 1)))
                        stt(xsp1[:, 0, w], ybk[l][:, w], 1 / GS, x[:, ww], ALU.mult, ALU.add)
                    i = stt(x[:, ww], ybk[l][:, w], 1 / GS, x[:, ww], ALU.mult, ALU.add)
                elif kind == "YL":
                    _, c = key
                    dve.wait_ge(dve_done, nth["dve", ("YE", c, 0)])
                    ww = slice(STARTS[c] * B + w.start, STARTS[c] * B + w.stop)
                    i = tts(xsp1[:, 1, w], x[:, ww], xsp1[:, 0, w], ALU.subtract)
                elif kind in ("KP", "QP"):
                    dve.wait_ge(act_done, nth["act", key])
                    i = kq_order[key] % 2
                    i = stt(kq[:, i, 1, w], hk[:, w], A("kb" if kind == "KP" else "qb"), kq[:, i, 0, w], ALU.add, ALU.subtract)
                elif kind == "QZ":
                    _, t, g, h, i2 = key
                    q0 = 64 * h
                    dve.wait_ge(act_done, nth["act", ("Q", t, g, h)])
                    for j in (2 * i2, 2 * i2 + 1):
                        i = tsc(qz[:, g, :, j, q0:q0 + 64], fq[:, g, :, q0:q0 + 64], hm[:, j:j + 1], None, ALU.mult)
                elif kind == "V":
                    _, t, q = key
                    r = slice(0, 4) if half is None else slice(2 * half, 2 * half + 2)
                    i = tts(v[:, 4 * q + r.start:4 * q + r.stop, t, :], hk[:].rearrange("p (b d) -> p b d", b=4)[:, r],
                            A("vb").rearrange("p (o d) -> p o d", o=1).broadcast_to([P, r.stop - r.start, P]), ALU.add)
                elif kind == "A":
                    _, t, b, a = key
                    nh = J if t == 0 else 2
                    r = slice(0, nh) if half is None else slice(half * nh // 2, (half + 1) * nh // 2)
                    i = nc.vector.tensor_reduce(wm[:, b, a * nh + r.start:a * nh + r.stop],
                                                hk[:].rearrange("p (h k) -> p h k", h=nh)[:, r], AX.X, ALU.max)
                elif kind == "MX":
                    _, t, b = key
                    dve.wait_ge(dve_done, nth["dve", ("A", t, b, (4 if t == 0 else 8) - 1)])
                    if t:
                        dve.wait_ge(pe_done, nth["pe", ("S", t - 1, b, G - 1, t - 1)])
                        dve.wait_ge(lm_ready, (t - 1) * B + b + 1)
                    link(tts(mm[:, b, :], hk[:, 0:H], wm[:, b, :], ALU.max))
                    i = tsc(mneg[:, b, :], mm[:, b, :], -1.0, None, ALU.mult)
                elif kind == "ID":
                    _, t, q = key
                    d = hk[:, 0:2 * QT].rearrange("p (b q) -> p b q", b=2)
                    r = slice(2 * q, 2 * q + 2)
                    if t:
                        dve.wait_ge(dve_done, nth["dve", ("X", t - 1, B - 1, 1)])
                    if half != 1:
                        nc.vector.tensor_copy(dimg[:, r, :], d)
                    if half != 0:
                        i = tts(nimg[:, r, :], d,
                                vimg[:, r].rearrange("p (b o) -> p b o", o=1).broadcast_to([P, 2, QT]), ALU.mult)
                elif kind == "X":
                    _, t, b, part = key
                    dve.wait_ge(pe_done, nth["pe", ("AV", t, b, G - 1, t)])
                    dve.wait_ge(dve_done, nth["dve", ("ID", t, b // 2)])
                    nbk, dbk = cbk if t and b % 2 else ybk
                    if part < 2:
                        for j in (2 * part, 2 * part + 1) if half is None else (2 * part + half,):
                            w = slice(j * QT, j * QT + QT)
                            for bank, sums, image in ((dbk, den, dimg), (nbk, num, nimg)):
                                if j % 2:
                                    dve.wait_ge(dve_link, chain[0] - 1 if sums is den else chain[0])
                                i = stt(sums[:, j % 2, :], bank[:, w], hx[:, j:j + 1],
                                        sums[:, (j - 1) % 2, :] if j else image[:, b, :], ALU.mult, ALU.add)
                                if j % 2 == 0:
                                    chain[0] += 1
                                    i.then_inc(dve_link, 1)
                    elif part == 2:
                        w = slice(0, QT) if half is None else slice(half * QT // 2, (half + 1) * QT // 2)
                        i = nc.vector.reciprocal(den[:, 0, w], den[:, 1, w])
                    else:
                        if t and b % 4 == 0:
                            dve.wait_ge(pe_done, nth["pe", ("O", t - 1, b // 4)])
                        w = slice(0, QT) if half is None else slice(half * QT // 2, (half + 1) * QT // 2)
                        i = tts(on[:, b, w], num[:, 1, w], den[:, 0, w], ALU.mult)
                elif kind == "O":
                    _, t, q = key
                    h0, h1 = (0, 4) if half is None else (2 * half, 2 * half + 2)
                    bb = slice(4 * q + h0, 4 * q + h1)
                    if t:
                        dve.wait_ge(stored[q], 16 * t)
                    i = stt(ob[:, q, h0:h1, :], hk[:, w].rearrange("p (b q) -> p b q", q=QT), A("pb"),
                            x3[:, bb, t * QT:(t + 1) * QT], ALU.add, ALU.add)
                if last:
                    i.then_inc(dve_done, 1)

            def hg_free(key):
                i = hg_of[key]
                if i >= NHG:
                    k = hg_key[i - NHG]
                    y = ("Y", k[1], k[2], "e" if k[0] == "M" else "s", k[3])
                    dve.wait_ge(pe_done, nth["pe", y])

            for s in range(n_slots):
                t = steps.get(s)
                units = parts["dve"][s]
                if t is None:
                    for key in units:
                        unit(key, None)
                    continue
                if t:
                    dve.wait_ge(h_full, t)
                    tts(hlo[:, t % 2, :], hs[:, t, :], hhi[:, t % 2, :], ALU.subtract).then_inc(h_lo, 1)
                dve.wait_ge(z_ready, chunk_of(t) + 1)
                stt(d1[:, t % 2, :, 1], hs[:, t, :], leak[:], d0[:, t % ZR, :, 1], ALU.mult, ALU.add).then_inc(decay, 1)
                first = [k for i, k in enumerate(units) if i < len(units) // 2]
                rest = units[len(units) // 2:]
                cut = len(units) % 2 == 1 and rest[0][0] in HALVED
                for key in first:
                    unit(key, None)
                if cut:
                    unit(rest[0], 0)
                dve.wait_ge(gate_th, t + 1)
                dve.wait_ge(decay, t + 1)
                nc.vector.tensor_tensor_scan(vps, d0[:, t % ZR].rearrange("p b o -> p (b o)"),
                                             d1[:, t % 2].rearrange("p b o -> p (b o)"), 0.0, ALU.mult,
                                             ALU.add).then_inc(blend, 1)
                if cut:
                    unit(rest[0], 1)
                    rest = rest[1:]
                for key in rest:
                    unit(key, None)


HALVED = ("GT", "YL", "SA", "SB", "M", "YE", "O", "RS", "RD", "RC", "KP", "QP", "A", "V", "ID", "X")



def padded(a):
    lead = a.shape[:-2]
    out = np.zeros(lead + (G, J, HP), a.dtype)
    for r in range(3):
        out[..., r * HD:(r + 1) * HD] = a.reshape(lead + (G, J, HD))
    return out.reshape(lead + (G * J * HP,))


def constants():
    p = np.arange(P)
    one = lambda cond: cond.astype(np.float32)
    selc = one(np.arange(E) == np.where(p < 2 * E, p % E, -1)[:, None])
    lo_k = one((p % HP) // HD == 1)
    h = np.arange(H)
    hmk = np.stack([one(h[None, :] == (J * g + p // HP)[:, None]) for g in range(G)], 1)
    return {
        "ident": np.eye(P, dtype=np.float32), "iota": np.tile(np.arange(E, dtype=np.float32), (P, 1)),
        "selc": selc,
        "causal": one(p[None, :] > p[:, None]) * np.float32(NEG),
        "hm": one(p[:, None] // HP == np.arange(J)), "hx": one((p[:, None] % HP) // HD == np.arange(J)),
        "sk": (1 - 2 * lo_k)[:, None], "mk": lo_k[:, None],
        "hmk": hmk.reshape(P, G * H), "hexp": one(p[:, None] == p[None, :] // HD),
    }


def kernel(**inputs):
    import concourse.bacc as bacc
    from concourse.bass_utils import run_bass_kernel_spmd

    a = {k: np.asarray(v) for k, v in inputs.items()}
    con = constants()
    rows = lambda w: np.ascontiguousarray(np.broadcast_to(w, (P,) + w.shape)).reshape(P, -1)
    wide = lambda w: np.ascontiguousarray(w).reshape(P, -1)
    tiles = lambda w: wide(w.transpose(1, 0, 2))

    def pack(layout, total, blocks):
        out = np.zeros((P, total), np.float32)
        for name, (at, width) in layout.items():
            out[:, at:at + width] = (blocks if name in blocks else con)[name]
        return out

    L0, L1, L2, L3 = (lambda n, l=l: a[f"L{l}_cond_{n}"] for l in range(4))
    small = pack(SMALL, N_SMALL, {
        "cond": np.tile(a["cond_1024"].T, (1, P // B)), "wrx0": L0("router_W")[:D], "wrt0": L0("router_W")[D:],
        "wrx1": L1("W_router")[:, :D].T, "wrt1": L1("W_router")[:, D:].T,
        "rb0": rows(L0("router_bias")), "rb1": rows(L1("router_bias")),
        "alpha": L2("alpha")[:, None], "b2": L2("b")[:, None]})
    up = pack(UP, N_UP, {
        ("w1", 0): L0("w1"), ("w3", 0): L0("w3"), ("e1", 0): tiles(L0("W1e")),
        ("w1", 1): wide(L1("s_w1").transpose(2, 0, 1)), ("w3", 1): wide(L1("s_w3").transpose(2, 0, 1)),
        ("e1", 1): tiles(L1("r_w1").transpose(0, 2, 1))})
    down = pack(DOWN, N_DOWN, {
        ("w2", 0): tiles(L0("w2").reshape(2, P, D)), ("e2", 0): tiles(L0("W2e")),
        ("w2", 1): tiles(L1("s_w2").transpose(0, 2, 1).reshape(4, P, D)), ("e2", 1): tiles(L1("r_w2").transpose(0, 2, 1))})
    rec = pack({"wh": (0, P), "wz": (P, P)}, N_REC, {"wh": L2("W")[:, :D].T, "wz": L2("W")[:, D:].T})
    w, wb = L3("c_attn_w"), L3("c_attn_b")
    col = lambda v: padded(v.reshape(H, HD)).reshape(G, P).T
    att = pack(ATT, N_ATT, {
        "wq": w[:, :D], "wk": w[:, D:2 * D], "wv": w[:, 2 * D:],
        "wp": L3("c_proj_w"), "uk": padded(L3("uk_w").T.reshape(D, H, HD)), "uv": L3("uv_w").T,
        "qb": wb[:D, None], "kb": wb[D:2 * D, None], "ukb": col(L3("uk_b")), "pb": L3("c_proj_b")[:, None],
        "uvb": L3("uv_b")[:, None], "vb": rows(wb[2 * D:]),
        "maskt": wide(a["mask_Bx1x1xS_ff0"].reshape(B, 2, P).transpose(2, 0, 1))})
    arrays = {"x_in": wide(a["x"].transpose(2, 1, 0)), "small_in": small, "up_in": up, "down_in": down, "rec_in": rec,
              "att_in": att, "maskr_in": rows(a["mask_Bx1x1xS_ff0"].reshape(B * T))}

    nc = bacc.Bacc("TRN2", target_bir_lowering=False, num_devices=1)
    args = [nc.dram_tensor(n, v.shape, mybir.dt.from_np(v.dtype), kind="ExternalInput").ap() for n, v in arrays.items()]
    out = nc.dram_tensor("out_dram", (P, B, T), F32, kind="ExternalOutput").ap()
    build(nc, *args, out)
    r = run_bass_kernel_spmd(nc, [arrays], core_ids=[0])
    return np.ascontiguousarray(r.results[0]["out_dram"].transpose(1, 2, 0))
```
